# Optimizing a Trainium2 kernel written in Bass

```python
import numpy as np
import jax
import jax.numpy as jnp

def _softmax(x, axis=-1):
    return jax.nn.softmax(x, axis=axis)

def _gelu(x):
    return jax.nn.gelu(x, approximate=True)

def _silu(x):
    return jax.nn.silu(x)

def _sigmoid(x):
    return jax.nn.sigmoid(x)

def _layernorm(x, axis=-1, eps=1e-05):
    m = jnp.mean(x, axis=axis, keepdims=True)
    v = jnp.var(x, axis=axis, keepdims=True)
    return (x - m) / jnp.sqrt(v + eps)

def _scatter_add(tgt, idx, src, axis=0):
    return tgt.at[idx].add(src)

def _segment_sum(src, seg, n):
    return jax.ops.segment_sum(src, seg, n)
kernel_name = 'mk_hybrid_d1_jaxref_r4_721f76'

def setup_inputs(seed: int=0):
    np.random.seed(seed)
    _w = jnp.asarray

    def _L0_attn_a_setup():
        import jax, jax.numpy as jnp
        import numpy as np
        import math
        B, S, D, H = (4, 512, 512, 16)
        HD = D // H

        def _alibi_slopes(n_heads):
            return jnp.asarray([2.0 ** (-8.0 / n_heads * (h + 1)) for h in range(n_heads)], dtype=jnp.float32)
        key = jax.random.key(seed)
        ks = jax.random.split(key, 10)
        w = lambda k: jax.random.normal(k, (D, D), dtype=jnp.float32) * 0.02
        b = lambda k: jax.random.normal(k, (D,), dtype=jnp.float32) * 0.01
        return {'hidden_states': jax.random.normal(ks[0], (B, S, D), dtype=jnp.float32), 'Wq': w(ks[1]), 'bq': b(ks[2]), 'Wk': w(ks[3]), 'bk': b(ks[4]), 'Wv': w(ks[5]), 'bv': b(ks[6]), 'Wo': w(ks[7]), 'bo': b(ks[8]), 'alibi_slopes': _alibi_slopes(H)}
    _L0_attn_a_in = _L0_attn_a_setup()

    def _L0_attn_b_setup():
        import jax, jax.numpy as jnp
        import numpy as np
        L, N, E, H = (512, 2, 512, 16)
        DH = E // H
        SCALE = DH ** (-0.5)
        key = jax.random.key(seed)
        k1, k2, k3 = jax.random.split(key, 3)
        x = jax.random.normal(k1, (L, N, E), dtype=jnp.float32)
        weight_qkv = jax.random.normal(k2, (3 * E, E), dtype=jnp.float32) * 0.02
        weight_out = jax.random.normal(k3, (E, E), dtype=jnp.float32) * 0.02
        return {'x': x, 'weight_qkv': weight_qkv, 'weight_out': weight_out}
    _L0_attn_b_in = _L0_attn_b_setup()

    def _L0_ffn_setup():
        import jax, jax.numpy as jnp
        import numpy as np
        import math
        NUM_EXPERTS = 12
        TOP_K = 2
        CAP_FACTOR = 1.25
        key = jax.random.key(seed)
        k0, k1, k2, k3, k4 = jax.random.split(key, 5)
        B, S, H, F = (4, 1024, 512, 64)
        hidden_states = jax.random.normal(k0, (B, S, H), jnp.float32)
        gate_w = jax.random.normal(k1, (NUM_EXPERTS, H), jnp.float32) * 0.02
        w1 = jax.random.normal(k2, (NUM_EXPERTS, F, H), jnp.float32) * 0.02
        w2 = jax.random.normal(k3, (NUM_EXPERTS, H, F), jnp.float32) * 0.02
        w3 = jax.random.normal(k4, (NUM_EXPERTS, F, H), jnp.float32) * 0.02
        return dict(hidden_states=hidden_states, gate_w=gate_w, w1=w1, w2=w2, w3=w3)
    _L0_ffn_in = _L0_ffn_setup()
    _d = {'L0_attn_a_hidden_states': _L0_attn_a_in['hidden_states'], 'L0_attn_a_Wq': _L0_attn_a_in['Wq'], 'L0_attn_a_bq': _L0_attn_a_in['bq'], 'L0_attn_a_Wk': _L0_attn_a_in['Wk'], 'L0_attn_a_bk': _L0_attn_a_in['bk'], 'L0_attn_a_Wv': _L0_attn_a_in['Wv'], 'L0_attn_a_bv': _L0_attn_a_in['bv'], 'L0_attn_a_Wo': _L0_attn_a_in['Wo'], 'L0_attn_a_bo': _L0_attn_a_in['bo'], 'L0_attn_a_alibi_slopes': _L0_attn_a_in['alibi_slopes'], 'L0_attn_b_weight_qkv': _L0_attn_b_in['weight_qkv'], 'L0_attn_b_weight_out': _L0_attn_b_in['weight_out'], 'L0_ffn_gate_w': _L0_ffn_in['gate_w'], 'L0_ffn_w1': _L0_ffn_in['w1'], 'L0_ffn_w2': _L0_ffn_in['w2'], 'L0_ffn_w3': _L0_ffn_in['w3']}
    _x0 = _d['L0_attn_a_hidden_states']
    _d['L0_attn_a_hidden_states'] = jax.random.normal(jax.random.fold_in(jax.random.key(seed), 1), (2, 2048, 512), dtype=_x0.dtype)
    del _x0
    return _d

def reference(L0_attn_a_hidden_states, L0_attn_a_Wq, L0_attn_a_bq, L0_attn_a_Wk, L0_attn_a_bk, L0_attn_a_Wv, L0_attn_a_bv, L0_attn_a_Wo, L0_attn_a_bo, L0_attn_a_alibi_slopes, L0_attn_b_weight_qkv, L0_attn_b_weight_out, L0_ffn_gate_w, L0_ffn_w1, L0_ffn_w2, L0_ffn_w3):

    def _L0_attn_a_ref(hidden_states, Wq, bq, Wk, bk, Wv, bv, Wo, bo, alibi_slopes):
        import jax, jax.numpy as jnp
        import numpy as np
        import math
        B, S, D, H = (4, 512, 512, 16)
        HD = D // H

        def _alibi_slopes(n_heads):
            return jnp.asarray([2.0 ** (-8.0 / n_heads * (h + 1)) for h in range(n_heads)], dtype=jnp.float32)
        Bn, t, _ = hidden_states.shape
        split = lambda x: x.reshape(Bn, t, H, HD).transpose(0, 2, 1, 3)
        q = split(hidden_states @ Wq.T + bq)
        k = split(hidden_states @ Wk.T + bk)
        v = split(hidden_states @ Wv.T + bv)
        scores = jnp.einsum('bhsd,bhtd->bhst', q, k)
        pos = jnp.arange(t)
        rel = (pos[None, :] - pos[:, None]).astype(scores.dtype)
        bias = alibi_slopes[:, None, None] * rel
        scores = (scores + bias[None]) / math.sqrt(HD)
        scores = 30.0 * jnp.tanh(scores / 30.0)
        causal = pos[:, None] >= pos[None, :]
        scores = jnp.where(causal[None, None], scores, -jnp.inf)
        probs = jax.nn.softmax(scores, axis=-1)
        ctx = jnp.einsum('bhst,bhtd->bhsd', probs, v)
        ctx = ctx.transpose(0, 2, 1, 3).reshape(Bn, t, D)
        return ctx @ Wo.T + bo

    def _L0_attn_b_ref(x, weight_qkv, weight_out):
        import jax, jax.numpy as jnp
        import numpy as np
        L, N, E, H = (512, 2, 512, 16)
        DH = E // H
        SCALE = DH ** (-0.5)
        l, n, e = x.shape
        h, dh = (H, DH)
        qkv = jnp.einsum('lne,fe->lnf', x, weight_qkv)
        q, k, v = jnp.split(qkv, 3, axis=-1)
        q = q.reshape(l, n, h, dh) * jnp.asarray(SCALE, x.dtype)
        k = k.reshape(l, n, h, dh)
        v = v.reshape(l, n, h, dh)
        attn = jnp.einsum('lnhd,mnhd->nhlm', q, k)
        causal = jnp.tril(jnp.ones((l, l), dtype=bool))
        attn = jnp.where(causal, attn, jnp.asarray(-jnp.inf, attn.dtype))
        attn = jax.nn.softmax(attn, axis=-1)
        out = jnp.einsum('nhlm,mnhd->lnhd', attn, v).reshape(l, n, e)
        return jnp.einsum('lne,fe->lnf', out, weight_out)

    def _L0_ffn_ref(hidden_states, gate_w, w1, w2, w3):
        import jax, jax.numpy as jnp
        import numpy as np
        import math
        NUM_EXPERTS = 12
        TOP_K = 2
        CAP_FACTOR = 1.25
        B, S, H = hidden_states.shape
        T = B * S
        E = gate_w.shape[0]
        cap = math.ceil(T / E * CAP_FACTOR)
        x = hidden_states.reshape(T, H)
        logits = x @ gate_w.T
        probs = jax.nn.softmax(logits, axis=-1)
        rw, sel = jax.lax.top_k(probs, TOP_K)
        rw = rw / rw.sum(axis=-1, keepdims=True)
        ar_cap = jnp.arange(cap)
        ar_flat = jnp.arange(TOP_K * T, dtype=jnp.int32)

        def per_expert(e, we1, we2, we3):
            mask = sel.T == e
            fm = mask.ravel()
            pos = jnp.cumsum(fm) - 1
            slot_idx = jnp.where(fm & (pos < cap), pos, cap)
            buf = jnp.zeros(cap + 1, jnp.int32).at[slot_idx].set(ar_flat)
            flat = buf[:cap]
            valid = ar_cap < fm.sum()
            tok = flat % T
            slot = flat // T
            xs = x[tok]
            h = jax.nn.silu(xs @ we1.T * (xs @ we3.T)) @ we2.T
            w = jnp.where(valid, rw[tok, slot], 0.0)
            return (tok, h * w[:, None])
        toks, contribs = jax.vmap(per_expert)(jnp.arange(E), w1, w2, w3)
        out = jnp.zeros((T, H), x.dtype).at[toks.ravel()].add(contribs.reshape(-1, H))
        return out.reshape(B, S, H)
    x = L0_attn_a_hidden_states
    x = x + _L0_attn_a_ref(_layernorm(x, axis=-1), L0_attn_a_Wq, L0_attn_a_bq, L0_attn_a_Wk, L0_attn_a_bk, L0_attn_a_Wv, L0_attn_a_bv, L0_attn_a_Wo, L0_attn_a_bo, L0_attn_a_alibi_slopes)
    x = x + _L0_ffn_ref(_layernorm(x, axis=-1), L0_ffn_gate_w, L0_ffn_w1, L0_ffn_w2, L0_ffn_w3)
    x = x + _L0_attn_b_ref(_layernorm(x, axis=-1), L0_attn_b_weight_qkv, L0_attn_b_weight_out)
    x = x + _L0_ffn_ref(_layernorm(x, axis=-1), L0_ffn_gate_w, L0_ffn_w1, L0_ffn_w2, L0_ffn_w3)
    return x

_drawn_inputs = setup_inputs


def setup_inputs(seed=0):
    import zlib

    import numpy as np

    out = dict(_drawn_inputs(seed))
    spreads = {}
    factors = {'L0_attn_a_Wq': 8.0,
     'L0_attn_a_bq': 8.0,
     'L0_attn_a_Wk': 8.0,
     'L0_attn_a_bk': 26.659,
     'L0_attn_a_bv': 8.0,
     'L0_attn_a_bo': 5.836,
     'L0_attn_a_alibi_slopes': 2.836,
     'L0_ffn_gate_w': 3.143,
     'L0_ffn_w1': 2.979,
     'L0_ffn_w2': 2.937,
     'L0_ffn_w3': 2.976}
    for name, (base, spread) in spreads.items():
        noise = np.random.default_rng([zlib.crc32(name.encode()), seed]).standard_normal(out[name].shape)
        drawn = base * np.exp(spread * noise) if base else spread * noise
        out[name] = jnp.asarray(drawn.astype(out[name].dtype))
    for name, factor in factors.items():
        out[name] = (out[name] * factor).astype(out[name].dtype)
    return out
```

```python
from contextlib import ExitStack

import numpy as np

import concourse.bass as bass
from concourse import mybir

P = 128
B, S, D = 2, 2048, 512
H, HD = 16, 32
T = B * S
TILES = T // P
C = D // P
HG = P // HD
GROUPS = H // HG
QW = 512
QB, KB = S // QW, S // P
E_N, F = 12, 64
CAP = -(-T * 5 // (E_N * 4))
SLOTS = 512
EPS = 1e-5
CAPPED = 30.0
SQRT_HD = float(np.sqrt(np.float32(HD)))

F32 = mybir.dt.float32
BF16 = mybir.dt.bfloat16
U32 = mybir.dt.uint32
ALU = mybir.AluOpType
ACT = mybir.ActivationFunctionType
AX = mybir.AxisListType
ds = bass.DynSlice


class Memory:

    def __init__(self, nc, ctx, tag):
        self.nc, self.ctx, self.tag = nc, ctx, tag
        self.sems = []
        ctx.callback(self.free_semaphores)

    def sb(self, name, shape, dt=F32):
        return self.ctx.enter_context(self.nc.sbuf_tensor(f"{self.tag}_{name}", shape, dt))

    def ps(self, name, shape, dt=F32):
        return self.ctx.enter_context(self.nc.psum_tensor(f"{self.tag}_ps_{name}", shape, dt))

    def sem(self, name):
        self.sems.append(self.nc.alloc_semaphore(f"{self.tag}_{name}"))
        return self.sems[-1]

    def free_semaphores(self):
        if self.sems:
            self.nc.clear_and_free_semaphores(self.sems)
            self.nc.all_engine_barrier()


def wait_alone(eng, sem, value, passed):
    eng.wait_ge(sem, value)
    eng.sem_inc(passed, 1)

def attention_a(nc, x, x_out, w):
    units = []
    for qb in range(QB):
        for kb in range((qb + 1) * QW // P):
            units.append((qb, kb, max(0, kb * P - qb * QW)))
    NU = len(units)
    NDIAG = QB * QW // P
    NPROJ = 3 * QB
    first_of = {qb: next(i for i, u in enumerate(units) if u[0] == qb) for qb in range(QB)}
    diag_of = {u: n for n, u in enumerate(i for i, t in enumerate(units) if t[1] * P >= t[0] * QW)}
    proj_after = {2 + 3 * k: k for k in range(NPROJ)}
    RP, RS = 4, 3
    LN_IT = 4
    AUX_G = NPROJ + QB
    AUX_B = NPROJ + (GROUPS - 1) * AUX_G + QB

    def aux_plan(project):
        n, sums, projs = 0, {}, {}
        for u, (qb, _, _) in enumerate(units):
            if u and first_of[qb] == u:
                sums[qb - 1] = n
                n += 1
            if project and u in proj_after:
                projs[proj_after[u]] = n
                n += 1
        sums[QB - 1] = n
        return sums, projs

    with ExitStack() as ctx:
        m = Memory(nc, ctx, "aa")
        ident = m.sb("ident", [P, P])
        distance = m.sb("distance", [P, S], BF16)
        mult = m.sb("mult", [P, P])
        part_of = m.sb("part_of", [P, 3])
        slopes = m.sb("slopes", [P, GROUPS])
        slope_j = m.sb("slope_j", [P, P])
        part = [m.sb(f"part{i}", [P, P], BF16) for i in range(3)]
        rest = m.sb("rest", [P, P])
        alibi_sum = m.sb("alibi_sum", [P, P])
        alibi_all = m.sb("alibi_all", [P, GROUPS, P], BF16)
        alibi = m.sb("alibi", [P, P], BF16)
        ones = m.sb("ones", [P, HD])
        half = m.sb("half", [P, LN_IT])
        bias_all = m.sb("bias_all", [P, 2, GROUPS])
        bias = m.sb("bias", [P, 2])
        bv = m.sb("bv_g", [P, QW // P, P])
        bv_all = m.sb("bv_all", [P, D])
        bo_all = m.sb("bo_all", [P, D])
        wo = m.sb("wo", [P, C, D])
        wg = m.sb("wg", [P, 3, C, P])
        stats = m.sb("stats", [P, LN_IT, 6])
        mv = m.sb("mv", [P, LN_IT, 2])
        veps = m.sb("veps", [P, LN_IT])
        rstd = m.sb("rstd", [P, LN_IT])
        xnT = m.sb("xnT", [P, C, S])
        qkv_next = m.sb("qkv_next", [P, 3, S])
        qkv = m.sb("qkv", [P, 3, S])
        probs = m.sb("probs", [P, RP, HG, QW])
        acc = m.sb("acc", [P, HG, QW])
        distance_f = acc[:, :, :].rearrange("p h n -> p (h n)")
        recip = m.sb("recip", [P, QW])
        ctxT = m.sb("ctxT", [P, GROUPS, S])
        assert LN_IT * D == HG * QW
        xn, x_in = probs[:, 0:2], probs[:, 2:4]
        x_new, x_old = probs[:, 0, 0:2, :], probs[:, 0, 2:4, :]

        ps_s = m.ps("scores", [P, RS, 2, QW])
        ps_v = m.ps("values", [P, QW])
        ps_x = m.ps("shared", [P, QW])

        dve_passed, pool_passed, sp_passed = m.sem("dve_passed"), m.sem("pool_passed"), m.sem("sp_passed")
        consts_in = m.sem("consts_in")
        alibi_chain = m.sem("alibi_chain")
        ones_set = m.sem("ones_set")
        x_loaded = [m.sem(f"x_loaded{i}") for i in range(2)]
        ln_chain = m.sem("ln_chain")
        rstd_done = m.sem("rstd_done")
        var_done = m.sem("var_done")
        xn_done = m.sem("xn_done")
        turned = m.sem("turned")
        xnT_done = m.sem("xnT_done")
        w_loaded = m.sem("w_loaded")
        bias_done = m.sem("bias_done")
        shared_full = m.sem("shared_full")
        shared_free = m.sem("shared_free")
        group_set = m.sem("group_set")
        scores_done = m.sem("scores_done")
        tanh_done = m.sem("tanh_done")
        exp_done = m.sem("exp_done")
        masked = m.sem("masked")
        pv_done = m.sem("pv_done")
        acc_done = m.sem("acc_done")
        recip_done = m.sem("recip_done")
        ctx_done = m.sem("ctx_done")
        out_full = m.sem("out_full")
        out_chain = m.sem("out_chain")
        out_done = m.sem("out_done")
        res_loaded = [m.sem(f"res_loaded{i}") for i in range(2)]
        stored = [m.sem(f"stored{i}") for i in range(2)]

        x_tiles = x.rearrange("(b i j p) d -> b i p j d", b=B, j=LN_IT, p=P)
        x_rows = x.rearrange("(b t p) d -> b t p d", b=B, p=P)
        o_rows = x_out.rearrange("(b t p) d -> b t p d", b=B, p=P)
        LN_STEPS = S // P // LN_IT
        NT = S // P

        block = ctx.enter_context(nc.Block())

        @block.sync
        def _(sp):
            for sem in stored:
                sp.sem_inc(sem, 16)
            for dst, src in ((ident, w["ident"]), (mult, w["mult"]),
                             (part_of, w["part_of"]), (slopes, w["slopes"]), (bias_all, w["qk_bias"]),
                             (bv_all, w["bv"]), (bo_all, w["bo"]),
                             (wo, w["woT"].rearrange("(c p) n -> p c n", p=P))):
                sp.dma_start(dst[:], src).then_inc(consts_in, 16)
            sp.dma_start(distance_f, w["distance"]).then_inc(consts_in, 16)

            def load_weights(hg, b):
                if hg == 0:
                    wait_alone(sp, shared_full, 1 + b * AUX_B, sp_passed)
                elif hg == 1:
                    wait_alone(sp, shared_full, 1 + b * AUX_B + NPROJ, sp_passed)
                else:
                    wait_alone(sp, shared_full, 1 + b * AUX_B + NPROJ + (hg - 2) * AUX_G + aux_plan(True)[1][NPROJ - 1] + 1, sp_passed)
                for n in range(3):
                    src = w["wqkvT"][n].rearrange("(c p) n -> p c n", p=P)
                    sp.dma_start(wg[:, n, :, :], src[:, :, ds(hg * P, P)]).then_inc(w_loaded, 16)

            with sp.Fori(0, B) as b:
                for i in range(LN_STEPS):
                    if i >= 2:
                        wait_alone(sp, xn_done, b * LN_STEPS + i - 1, sp_passed)
                    else:
                        wait_alone(sp, stored[i], 16 + b * (NT // 2) * 16, sp_passed)
                        wait_alone(sp, out_done, 1 + b * NT, sp_passed)
                    sp.dma_start(x_in[:, i % 2, :, :], x_tiles[ds(b, 1), i].rearrange("a p j d -> (a p) j d")
                                 ).then_inc(x_loaded[i % 2], 16)
                for hg in range(GROUPS):
                    load_weights(hg, b)
                for t in range(NT):
                    if t >= 2:
                        wait_alone(sp, out_done, 1 + b * NT + t - 1, sp_passed)
                    else:
                        wait_alone(sp, ctx_done, 1 + (b + 1) * GROUPS * QB, sp_passed)
                    sp.dma_start(x_old[:, t % 2, :], x_rows[ds(b, 1), t].rearrange("a p d -> (a p) d")
                                 ).then_inc(res_loaded[t % 2], 16)
                    wait_alone(sp, out_done, 1 + b * NT + t + 1, sp_passed)
                    sp.dma_start(o_rows[ds(b, 1), t].rearrange("a p d -> (a p) d"), x_new[:, t % 2, :]
                                 ).then_inc(stored[t % 2], 16)
            for i in range(2):
                sp.wait_ge(stored[i], 16 + B * NT // 2 * 16)

        @block.gpsimd
        def _(pool):
            nc.gpsimd.memset(ones[:], 1.0).then_inc(ones_set, 1)
            nc.gpsimd.memset(half[:], -0.5).then_inc(ones_set, 1)
            pool.wait_ge(ones_set, 2)
            with pool.Fori(0, B) as b:
                for i in range(LN_STEPS):
                    pool.wait_ge(var_done, b * LN_STEPS + i + 1)
                    nc.gpsimd.tensor_tensor(rstd[:], veps[:], half[:], ALU.pow).then_inc(rstd_done, 1)

                def masks(g):
                    for u, n in diag_of.items():
                        off = units[u][2]
                        tri = probs[:, u % RP, :, off:off + P]
                        wait_alone(pool, exp_done, g * NU + u + 1, pool_passed)
                        nc.gpsimd.affine_select(out=tri, in_=tri, compare_op=ALU.is_ge, fill=0.0, base=0,
                                                pattern=[[0, HG], [1, P]], channel_multiplier=-1
                                                ).then_inc(masked, 1)

                with pool.Fori(0, GROUPS) as hg:
                    masks(b * GROUPS + hg)

        @block.scalar
        def _(act):
            act.sem_inc(tanh_done, 1)
            with act.Fori(0, B) as b:
                for i in range(LN_STEPS * LN_IT):
                    act.wait_ge(turned, b * NT + i + 1)
                    nc.scalar.copy(xnT[:, :, i * P:(i + 1) * P],
                                   ps_s[:, i % 4 // 2, i % 2, :].rearrange("p (c t) -> p c t", c=C)
                                   ).then_inc(xnT_done, 1)

                def group(g):
                    for u, (qb, kb, off) in enumerate(units):
                        r = u % RP
                        act.wait_ge(pv_done, g * NU + u + 1)
                        act.wait_ge(acc_done, g * NU + u + 1)
                        for p in range(2):
                            hu = 2 * u + p
                            act.wait_ge(scores_done, g * 2 * NU + hu + 1)
                            nc.scalar.activation(probs[:, r, 2 * p:2 * p + 2, off:], ps_s[:, hu % RS, :, off:],
                                                 ACT.Tanh, scale=1.0 / (SQRT_HD * CAPPED)).then_inc(tanh_done, 1)
                        act.wait_ge(tanh_done, 1 + g * 2 * NU + 2 * u + 2)
                        nc.scalar.activation(probs[:, r, :, off:], probs[:, r, :, off:], ACT.Exp,
                                             scale=CAPPED).then_inc(exp_done, 1)

                with act.Fori(0, GROUPS) as hg:
                    group(b * GROUPS + hg)

        @block.vector
        def _(dve):
            for sem in (shared_free, out_done, ctx_done):
                dve.sem_inc(sem, 1)
            dve.wait_ge(consts_in, 9 * 16)
            chain = 0

            def link(ins):
                nonlocal chain
                ins.then_inc(alibi_chain, 1)
                chain += 1
                dve.wait_ge(alibi_chain, chain)

            link(nc.vector.tensor_copy(distance[:], distance_f))
            for g in range(GROUPS):
                link(nc.vector.tensor_scalar(slope_j[:], mult[:], slopes[:, g:g + 1], None, ALU.mult))
                link(nc.vector.tensor_copy(part[0][:], slope_j[:]))
                link(nc.vector.tensor_tensor(rest[:], slope_j[:], part[0][:], ALU.subtract))
                link(nc.vector.tensor_copy(part[1][:], rest[:]))
                link(nc.vector.tensor_tensor(slope_j[:], rest[:], part[1][:], ALU.subtract))
                link(nc.vector.tensor_copy(part[2][:], slope_j[:]))
                link(nc.vector.tensor_scalar(alibi_sum[:], part[0][:], part_of[:, 0:1], None, ALU.mult))
                link(nc.vector.scalar_tensor_tensor(rest[:], part[1][:], part_of[:, 1:2], alibi_sum[:],
                                                    ALU.mult, ALU.add))
                link(nc.vector.scalar_tensor_tensor(alibi_all[:, g, :], part[2][:], part_of[:, 2:3], rest[:],
                                                    ALU.mult, ALU.add))
            dve.sem_inc(acc_done, RP)

            with dve.Fori(0, B) as b:
                for i in range(LN_STEPS):
                    dve.wait_ge(x_loaded[i % 2], (b * (LN_STEPS // 2) + i // 2 + 1) * 16)
                    for j in range(LN_IT):
                        nc.vector.bn_stats(stats[:, j, :], x_in[:, i % 2, j, :]).then_inc(ln_chain, 1)
                    wait_alone(dve, ln_chain, (b * LN_STEPS + i) * (2 * LN_IT) + LN_IT, dve_passed)
                    for j in range(LN_IT):
                        nc.vector.bn_aggr(mv[:, j, :], stats[:, j, :]).then_inc(ln_chain, 1)
                    dve.wait_ge(ln_chain, (b * LN_STEPS + i + 1) * (2 * LN_IT))
                    nc.vector.tensor_scalar(veps[:], mv[:, :, 1], EPS, None, ALU.add).then_inc(var_done, 1)
                    dve.wait_ge(rstd_done, b * LN_STEPS + i + 1)
                    if i >= 2:
                        dve.wait_ge(turned, b * NT + (i - 1) * LN_IT)
                    for j in range(LN_IT):
                        last = nc.vector.tensor_scalar(xn[:, i % 2, j, :], x_in[:, i % 2, j, :], mv[:, j, 0:1],
                                                       rstd[:, j:j + 1], ALU.subtract, ALU.mult)
                    last.then_inc(xn_done, 1)

                def take(k, n):
                    kind, blk = divmod(k, QB)
                    dve.wait_ge(shared_full, 1 + n + 1)
                    dst = qkv_next[:, kind, blk * QW:(blk + 1) * QW]
                    if kind < 2:
                        ins = nc.vector.tensor_scalar(dst, ps_x[:], bias[:, kind:kind + 1], None, ALU.add)
                    else:
                        tiles = QW // P
                        ins = nc.vector.tensor_tensor(
                            dst.rearrange("p (t n) -> p t n", t=tiles),
                            ps_x[:].rearrange("p (t n) -> p t n", t=tiles), bv[:], ALU.add)
                    ins.then_inc(shared_free, 1)

                def context(g, hg, qb, n):
                    dve.wait_ge(shared_full, 1 + n + 1)
                    dve.wait_ge(ctx_done, 1 + g * QB + qb)
                    nc.vector.reciprocal(recip[:], ps_x[:]).then_inc(shared_free, 1)
                    dve.wait_ge(shared_free, 1 + n + 1)
                    dve.wait_ge(pv_done, RP + g * NU + (first_of[qb + 1] if qb + 1 < QB else NU))
                    nc.vector.tensor_tensor(ctxT[:, ds(hg, 1), qb * QW:(qb + 1) * QW].rearrange("p a n -> p (a n)"),
                                            ps_v[:], recip[:], ALU.mult).then_inc(ctx_done, 1)

                def set_bias(hg, g):
                    nc.vector.tensor_copy(bias[:], bias_all[:, :, ds(hg, 1)].rearrange("p a b -> p (a b)")
                                          ).then_inc(bias_done, 1)
                    nc.vector.tensor_copy(bv[:, 0, :], bv_all[:, ds(hg * P, P)]).then_inc(bias_done, 1)
                    for t in range(1, QW // P):
                        nc.vector.tensor_copy(bv[:, t, :], bv_all[:, ds(hg * P, P)]).then_inc(bias_done, 1)
                    dve.wait_ge(bias_done, (g + 1) * 5)

                def group(hg, project):
                    g = b * GROUPS + hg
                    aux = b * AUX_B + NPROJ + hg * AUX_G
                    sums, projs = aux_plan(project)
                    dve.wait_ge(shared_free, 1 + aux)
                    dve.wait_ge(pv_done, RP + g * NU)
                    for n in range(3):
                        nc.vector.tensor_copy(qkv[:, n, :], qkv_next[:, n, :]).then_inc(group_set, 1)
                    nc.vector.tensor_copy(alibi[:], alibi_all[:, ds(hg, 1), :].rearrange("p a n -> p (a n)")
                                          ).then_inc(group_set, 1)
                    dve.wait_ge(group_set, (g + 1) * 4)
                    if project:
                        set_bias(hg + 1, g + 1)
                    for u, (qb, kb, off) in enumerate(units):
                        if u and first_of[qb] == u:
                            context(g, hg, qb - 1, aux + sums[qb - 1])
                        p = probs[:, u % RP, :, off:]
                        if u in diag_of:
                            dve.wait_ge(masked, g * NDIAG + diag_of[u] + 1)
                        else:
                            dve.wait_ge(exp_done, g * NU + u + 1)
                        dve.wait_ge(acc_done, RP + g * NU + u)
                        if kb == 0:
                            ins = nc.vector.tensor_copy(acc[:], p)
                        else:
                            ins = nc.vector.tensor_tensor(acc[:, :, off:], acc[:, :, off:], p, ALU.add)
                        ins.then_inc(acc_done, 1)
                        if project and u in proj_after:
                            take(proj_after[u], aux + projs[proj_after[u]])
                    context(g, hg, QB - 1, aux + sums[QB - 1])

                set_bias(0, b * GROUPS)
                for k in range(NPROJ):
                    take(k, b * AUX_B + k)
                with dve.Fori(0, GROUPS - 1) as hg:
                    group(hg, True)
                group(GROUPS - 1, False)

                for t in range(NT):
                    dve.wait_ge(out_full, b * NT + t + 1)
                    if t >= 2:
                        dve.wait_ge(stored[t % 2], 16 + (b * (NT // 2) + t // 2) * 16)
                    nc.vector.tensor_tensor(x_new[:, t % 2, :], ps_s[:, 0, t % 2, :], bo_all[:], ALU.add
                                            ).then_inc(out_chain, 1)
                    dve.wait_ge(out_chain, b * NT + t + 1)
                    dve.wait_ge(res_loaded[t % 2], (b * (NT // 2) + t // 2 + 1) * 16)
                    nc.vector.tensor_tensor(x_new[:, t % 2, :], x_new[:, t % 2, :], x_old[:, t % 2, :], ALU.add
                                            ).then_inc(out_done, 1)

        @block.tensor
        def _(pe):
            pe.wait_ge(consts_in, 9 * 16)
            pe.wait_ge(ones_set, 2)
            pe.sem_inc(pv_done, RP)
            pe.sem_inc(shared_full, 1)

            with pe.Fori(0, B) as b:
                for i in range(NT):
                    if i >= 4:
                        pe.wait_ge(xnT_done, b * NT + i - 3)
                    else:
                        pe.wait_ge(out_done, 1 + b * NT)
                    pe.wait_ge(xn_done, b * LN_STEPS + i // LN_IT + 1)
                    for c in range(C):
                        last = nc.tensor.transpose(ps_s[:, i % 4 // 2, i % 2, c * P:(c + 1) * P],
                                                   xn[:, i // LN_IT % 2, i % LN_IT, c * P:(c + 1) * P], ident[:])
                    last.then_inc(turned, 1)
                pe.wait_ge(xnT_done, (b + 1) * NT)

                def project(k, n, g):
                    kind, blk = divmod(k, QB)
                    if k == 0:
                        pe.wait_ge(w_loaded, (g + 1) * 48)
                    pe.wait_ge(shared_free, 1 + n)
                    if kind < 2:
                        for c in range(C):
                            last = nc.tensor.matmul(ps_x[:], wg[:, kind, c, :], xnT[:, c, blk * QW:(blk + 1) * QW],
                                                    start=(c == 0), stop=(c == C - 1))
                    else:
                        for t in range(QW // P):
                            at = blk * QW + t * P
                            for c in range(C):
                                last = nc.tensor.matmul(ps_x[:, t * P:(t + 1) * P], xnT[:, c, at:at + P],
                                                        wg[:, 2, c, :], start=(c == 0), stop=(c == C - 1))
                    last.then_inc(shared_full, 1)

                def sums_of(g, qb, n):
                    pe.wait_ge(shared_free, 1 + n)
                    pe.wait_ge(acc_done, RP + g * NU + (first_of[qb + 1] if qb + 1 < QB else NU))
                    for h in range(HG):
                        last = nc.tensor.matmul(ps_x[HD * h:HD * h + HD, :], ones[:], acc[:, h, :],
                                                start=True, stop=True)
                    last.then_inc(shared_full, 1)

                def scores(g, u):
                    qb, kb, off = units[u]
                    for p in range(2):
                        hu = 2 * u + p
                        if hu >= RS:
                            pe.wait_ge(tanh_done, 1 + g * 2 * NU + hu - RS + 1)
                        dst = ps_s[:, hu % RS, :, :]
                        first = kb * P - qb * QW
                        for j in range(2):
                            rows = slice(HD * (2 * p + j), HD * (2 * p + j + 1))
                            nc.tensor.matmul(dst[:, j, off:], alibi[rows, :],
                                             distance[rows, off - first:QW - first], start=True, stop=False)
                        for j in range(2):
                            rows = slice(HD * (2 * p + j), HD * (2 * p + j + 1))
                            last = nc.tensor.matmul(dst[:, j, off:], qkv[rows, 1, kb * P:(kb + 1) * P],
                                                    qkv[rows, 0, qb * QW + off:(qb + 1) * QW], start=False, stop=True)
                        last.then_inc(scores_done, 1)

                def values(g, u):
                    qb, kb, off = units[u]
                    if kb == 0:
                        pe.wait_ge(ctx_done, 1 + g * QB + qb)
                    if u in diag_of:
                        pe.wait_ge(masked, g * NDIAG + diag_of[u] + 1)
                    else:
                        pe.wait_ge(exp_done, g * NU + u + 1)
                    last_kb = (qb + 1) * QW // P - 1
                    for h in range(HG):
                        last = nc.tensor.matmul(ps_v[HD * h:HD * h + HD, off:],
                                                qkv[:, 2, kb * P + HD * h:kb * P + HD * h + HD],
                                                probs[:, u % RP, h, off:], start=(kb == 0), stop=(kb == last_kb))
                    last.then_inc(pv_done, 1)

                def group(hg, project_next):
                    g = b * GROUPS + hg
                    aux = b * AUX_B + NPROJ + hg * AUX_G
                    sums, projs = aux_plan(project_next)
                    pe.wait_ge(group_set, (g + 1) * 4)
                    pe.wait_ge(tanh_done, 1 + g * 2 * NU)
                    scores(g, 0)
                    for u, (qb, kb, off) in enumerate(units):
                        if u + 1 < NU:
                            scores(g, u + 1)
                        if u and first_of[qb] == u:
                            sums_of(g, qb - 1, aux + sums[qb - 1])
                        values(g, u)
                        if project_next and u in proj_after:
                            project(proj_after[u], aux + projs[proj_after[u]], g + 1)
                    sums_of(g, QB - 1, aux + sums[QB - 1])

                for k in range(NPROJ):
                    project(k, b * AUX_B + k, b * GROUPS)
                with pe.Fori(0, GROUPS - 1) as hg:
                    group(hg, True)
                group(GROUPS - 1, False)

                for t in range(NT):
                    pe.wait_ge(ctx_done, 1 + (b + 1) * GROUPS * QB)
                    if t >= 2:
                        pe.wait_ge(out_chain, b * NT + t - 1)
                    for c in range(C):
                        last = nc.tensor.matmul(ps_s[:, 0, t % 2, :], ctxT[:, c, t * P:(t + 1) * P], wo[:, c, :],
                                                start=(c == 0), stop=(c == C - 1))
                    last.then_inc(out_full, 1)

def moe(nc, tag, x, x_out, w, scratch, clear_scratch):
    xn_d, rows_in, rows_out = scratch
    NROWS = E_N * SLOTS
    J = 4
    STEPS = TILES // J
    ST = SLOTS // P
    NE = 2 * TILES
    tiles_of = lambda d: d.rearrange("(i j p) d -> i p j d", j=J, p=P)

    with ExitStack() as keep:
        k = Memory(nc, keep, tag)
        row_of = k.sb("row_of", [P, NE], U32)
        weight = k.sb("weight", [P, NE])

        with ExitStack() as ctx:
            m = Memory(nc, ctx, tag + "r")
            ident = m.sb("ident", [P, P])
            gate = m.sb("gate", [P, C, E_N])
            before = m.sb("before", [P, P], BF16)
            before_f = m.sb("before_f", [P, P])
            ones_b = m.sb("ones_b", [P, P], BF16)
            ones_f = m.sb("ones_f", [P, E_N * NE])
            expert_no = m.sb("expert_no", [P, E_N])
            spare_row = m.sb("spare_row", [P, 1])
            half = m.sb("half", [P, J])
            zero = m.sb("zero", [P, SLOTS * D // P])
            x_in = m.sb("x_in", [P, 2, J, D])
            xn = m.sb("xn", [P, 2, J, D])
            xnT = m.sb("xnT", [P, 2, J, D])
            stats = m.sb("stats", [P, J, 6])
            mv = m.sb("mv", [P, J, 2])
            veps = m.sb("veps", [P, J])
            rstd = m.sb("rstd", [P, J])
            logits = m.sb("logits", [P, J, E_N])
            best = m.sb("best", [P, J, 8])
            best_no = m.sb("best_no", [P, J, 8], U32)
            chosen_f = m.sb("chosen_f", [P, J, 2])
            chosen = m.sb("chosen", [P, NE])
            gap = m.sb("gap", [P, TILES])
            hot = m.sb("hot", [P, E_N, 2, TILES], BF16)
            e_gap = m.sb("e_gap", [P, TILES])
            den = m.sb("den", [P, TILES])
            share = m.sb("share", [P, 2, TILES])
            totals = m.sb("totals", [P, E_N * NE])
            running = m.sb("running", [P, E_N * NE])
            earlier = m.sb("earlier", [P, E_N * NE])
            place = m.sb("place", [P, E_N * NE])
            placed = m.sb("placed", [P, E_N * NE])
            pos = m.sb("pos", [P, NE])
            fits = m.sb("fits", [P, NE])
            row_f = m.sb("row_f", [P, NE])
            row_g = m.sb("row_g", [P, NE])
            ps_t = m.ps("turned", [P, J, D])
            ps_l = m.ps("logits", [P, 2, D])
            ps_c = m.ps("counts", [P, 2, D])

            consts_in = m.sem("consts_in")
            sets = m.sem("sets")
            cleared = m.sem("cleared")
            x_loaded = [m.sem(f"x_loaded{i}") for i in range(2)]
            xn_stored = [m.sem(f"xn_stored{i}") for i in range(2)]
            stats_done = m.sem("stats_done")
            mean_done = m.sem("mean_done")
            var_done = m.sem("var_done")
            rstd_done = m.sem("rstd_done")
            xn_done = m.sem("xn_done")
            turned = m.sem("turned")
            xnT_done = m.sem("xnT_done")
            logits_full = m.sem("logits_full")
            logits_done = m.sem("logits_done")
            best_done = m.sem("best_done")
            chain = m.sem("chain")
            gaps_done = m.sem("gaps_done")
            e_done = m.sem("e_done")
            prefix_full = m.sem("prefix_full")
            totals_full = m.sem("totals_full")
            chosen_done = m.sem("chosen_done")
            hot_done = m.sem("hot_done")
            place_done = m.sem("place_done")
            dve_passed, sp_passed = m.sem("dve_passed"), m.sem("sp_passed")

            block = ctx.enter_context(nc.Block())

            @block.sync
            def _(sp):
                for dst, src in ((ident, w["ident"]), (gate, w["gateT"].rearrange("(c p) e -> p c e", p=P)),
                                 (before_f, w["before"]), (expert_no, w["expert_no"]), (spare_row, w["spare_row"])):
                    sp.dma_start(dst[:], src).then_inc(consts_in, 16)
                for s in range(2):
                    sp.sem_inc(xn_stored[s], 16)
                    sp.dma_start(x_in[:, s], tiles_of(x)[s]).then_inc(x_loaded[s], 16)
                with sp.Fori(0, STEPS // 2) as ii:
                    for s in range(2):
                        wait_alone(sp, xn_done, (2 * ii + s + 1) * J, sp_passed)
                        sp.dma_start(tiles_of(xn_d)[ds(2 * ii + s, 1)].rearrange("a p j d -> (a p) j d"), xn[:, s]
                                     ).then_inc(xn_stored[s], 16)
                        nxt = tiles_of(x)[ds((2 * ii + 2 + s) % STEPS, 1)]
                        sp.dma_start(x_in[:, s], nxt.rearrange("a p j d -> (a p) j d")).then_inc(x_loaded[s], 16)
                for s in range(2):
                    sp.wait_ge(xn_stored[s], 16 + STEPS // 2 * 16)
                    sp.wait_ge(x_loaded[s], (STEPS // 2 + 1) * 16)
                if clear_scratch:
                    sp.wait_ge(sets, 4)
                    for e in range(E_N):
                        sp.dma_start(rows_in[e * SLOTS:(e + 1) * SLOTS, :].rearrange("(p r) d -> p (r d)", p=P),
                                     zero[:]).then_inc(cleared, 16)
                    for d in (rows_in, rows_out):
                        sp.dma_start(d[NROWS:NROWS + P, :], zero[:, 0:D]).then_inc(cleared, 16)
                    sp.wait_ge(cleared, (E_N + 2) * 16)

            @block.gpsimd
            def _(pool):
                nc.gpsimd.memset(ones_b[:], 1.0).then_inc(sets, 1)
                nc.gpsimd.memset(ones_f[:], 1.0).then_inc(sets, 1)
                nc.gpsimd.memset(half[:], -0.5).then_inc(sets, 1)
                nc.gpsimd.memset(zero[:], 0.0).then_inc(sets, 1)
                pool.wait_ge(consts_in, 5 * 16)
                nc.gpsimd.tensor_copy(before[:], before_f[:]).then_inc(sets, 1)
                pool.wait_ge(sets, 5)
                with pool.Fori(0, STEPS) as i:
                    pool.wait_ge(var_done, i + 1)
                    nc.gpsimd.tensor_tensor(rstd[:], veps[:], half[:], ALU.pow).then_inc(rstd_done, 1)

            @block.scalar
            def _(act):
                act.sem_inc(xnT_done, 1)
                with act.Fori(0, STEPS // 2) as ii:
                    for s in range(2):
                        i = 2 * ii + s
                        for j in range(J):
                            act.wait_ge(turned, i * J + j + 1)
                            if j == 0:
                                act.wait_ge(logits_full, i + 1)
                            nc.scalar.copy(xnT[:, s, j, :], ps_t[:, j, :]).then_inc(xnT_done, 1)
                act.wait_ge(gaps_done, STEPS)
                nc.scalar.activation(e_gap[:], gap[:], ACT.Exp).then_inc(e_done, 1)

            @block.tensor
            def _(pe):
                pe.wait_ge(consts_in, 5 * 16)
                pe.wait_ge(sets, 5)
                pe.sem_inc(logits_full, 2)
                with pe.Fori(0, STEPS // 2) as ii:
                    for s in range(2):
                        i = 2 * ii + s
                        pe.wait_ge(xn_done, (i + 1) * J)
                        pe.wait_ge(xnT_done, 1 + i * J)
                        for j in range(J):
                            for c in range(C):
                                last = nc.tensor.transpose(ps_t[:, j, c * P:(c + 1) * P],
                                                           xn[:, s, j, c * P:(c + 1) * P], ident[:])
                            last.then_inc(turned, 1)
                        pe.wait_ge(logits_done, i + 1)
                        for j in range(J):
                            pe.wait_ge(xnT_done, 1 + i * J + j + 1)
                            for c in range(C):
                                last = nc.tensor.matmul(ps_l[:, s, j * E_N:(j + 1) * E_N],
                                                        xnT[:, s, j, c * P:(c + 1) * P], gate[:, c, :],
                                                        start=(c == 0), stop=(c == C - 1))
                        last.then_inc(logits_full, 1)
                pe.wait_ge(hot_done, STEPS * (2 * J + 1))
                flat = hot[:, :, :, :].rearrange("p e s t -> p (e s t)")
                n = E_N * NE // 2
                for i in range(2):
                    last = nc.tensor.matmul(ps_c[:, i, 0:n], before[:], flat[:, i * n:(i + 1) * n], start=True, stop=True)
                last.then_inc(prefix_full, 1)
                pe.wait_ge(logits_done, 2 + STEPS)
                for i in range(2):
                    last = nc.tensor.matmul(ps_l[:, i, 0:n], ones_b[:], flat[:, i * n:(i + 1) * n], start=True, stop=True)
                last.then_inc(totals_full, 1)

            @block.vector
            def _(dve):
                dve.wait_ge(consts_in, 5 * 16)
                dve.wait_ge(sets, 4)
                dve.sem_inc(logits_done, 2)
                with dve.Fori(0, STEPS // 2) as ii:
                    for s in range(2):
                        i = 2 * ii + s
                        dve.wait_ge(x_loaded[s], (ii + 1) * 16)
                        for j in range(J):
                            nc.vector.bn_stats(stats[:, j, :], x_in[:, s, j, :]).then_inc(stats_done, 1)
                        wait_alone(dve, stats_done, (i + 1) * J, dve_passed)
                        for j in range(J):
                            nc.vector.bn_aggr(mv[:, j, :], stats[:, j, :]).then_inc(mean_done, 1)
                        dve.wait_ge(mean_done, (i + 1) * J)
                        nc.vector.tensor_scalar(veps[:], mv[:, :, 1], EPS, None, ALU.add).then_inc(var_done, 1)
                        dve.wait_ge(xn_stored[s], 16 + ii * 16)
                        dve.wait_ge(logits_done, i + 1)
                        dve.wait_ge(rstd_done, i + 1)
                        for j in range(J):
                            nc.vector.tensor_scalar(xn[:, s, j, :], x_in[:, s, j, :], mv[:, j, 0:1],
                                                    rstd[:, j:j + 1], ALU.subtract, ALU.mult).then_inc(xn_done, 1)
                        dve.wait_ge(logits_full, i + 3)
                        nc.vector.tensor_copy(logits[:].rearrange("p j e -> p (j e)"), ps_l[:, s, 0:J * E_N]
                                              ).then_inc(logits_done, 1)
                        wait_alone(dve, logits_done, i + 3, dve_passed)
                        for j in range(J):
                            nc.vector.max(best[:, j, :], logits[:, j, :]).then_inc(best_done, 1)
                        wait_alone(dve, best_done, (2 * i + 1) * J, dve_passed)
                        for j in range(J):
                            nc.vector.max_index(best_no[:, j, :], best[:, j, :], logits[:, j, :]).then_inc(best_done, 1)
                        nc.vector.tensor_tensor(gap[:, ds(i * J, J)], best[:, :, 1], best[:, :, 0], ALU.subtract
                                                ).then_inc(gaps_done, 1)
                        dve.wait_ge(best_done, (2 * i + 2) * J)
                        nc.vector.tensor_copy(chosen_f[:], best_no[:, :, 0:2]).then_inc(chosen_done, 1)
                        dve.wait_ge(chosen_done, i + 1)
                        nc.vector.tensor_copy(chosen[:, ds(2 * i * J, 2 * J)],
                                              chosen_f[:].rearrange("p j s -> p (j s)")).then_inc(hot_done, 1)
                        for j in range(J):
                            for c in range(2):
                                nc.vector.tensor_scalar(
                                    hot[:, :, c, ds(i * J + j, 1)].rearrange("p e a -> p (e a)"), expert_no[:],
                                    chosen_f[:, j, c:c + 1], None, ALU.is_equal).then_inc(hot_done, 1)
                dve.wait_ge(hot_done, STEPS * (2 * J + 1))
                n_chain = 0

                def link(ins):
                    nonlocal n_chain
                    ins.then_inc(chain, 1)
                    n_chain += 1
                    dve.wait_ge(chain, n_chain)

                dve.wait_ge(e_done, 1)
                link(nc.vector.tensor_scalar(den[:], e_gap[:], 1.0, None, ALU.add))
                link(nc.vector.reciprocal(share[:, 0, :], den[:]))
                link(nc.vector.tensor_tensor(share[:, 1, :], e_gap[:], share[:, 0, :], ALU.mult))
                dve.wait_ge(totals_full, 1)
                n = E_N * NE // 2
                for q in range(2):
                    link(nc.vector.tensor_copy(totals[:, q * n:(q + 1) * n], ps_l[:, q, 0:n]))
                link(nc.vector.tensor_tensor_scan(running[:], ones_f[:], totals[:], 0.0, ALU.mult, ALU.add))
                link(nc.vector.tensor_tensor(earlier[:], running[:], totals[:], ALU.subtract))
                dve.wait_ge(prefix_full, 1)
                for e in range(E_N):
                    q = e * NE // n
                    own = slice(e * NE, (e + 1) * NE)
                    nc.vector.scalar_tensor_tensor(place[:, own], earlier[:, own], earlier[:, e * NE:e * NE + 1],
                                                   ps_c[:, q, e * NE - q * n:(e + 1) * NE - q * n],
                                                   ALU.subtract, ALU.add).then_inc(place_done, 1)
                dve.wait_ge(place_done, E_N)
                link(nc.vector.tensor_tensor(placed[:], place[:], hot[:].rearrange("p e c t -> p (e c t)"), ALU.mult))
                link(nc.vector.tensor_reduce(pos[:], placed[:].rearrange("p (e n) -> p n e", e=E_N), AX.X, ALU.add))
                link(nc.vector.tensor_scalar(fits[:], pos[:], float(CAP), None, ALU.is_lt))
                turn = lambda a: a.rearrange("p (c t) -> p t c", c=2)
                pair = lambda a: a.rearrange("p (t c) -> p t c", c=2)
                link(nc.vector.scalar_tensor_tensor(pair(row_f[:]), pair(chosen[:]), float(SLOTS), turn(pos[:]),
                                                    ALU.mult, ALU.add))
                link(nc.vector.tensor_scalar(row_g[:], row_f[:], spare_row[:, 0:1], None, ALU.subtract))
                link(nc.vector.tensor_tensor(pair(row_f[:]), pair(row_g[:]), turn(fits[:]), ALU.mult))
                link(nc.vector.tensor_scalar(row_g[:], row_f[:], spare_row[:, 0:1], None, ALU.add))
                link(nc.vector.tensor_copy(row_of[:], row_g[:]))
                link(nc.vector.tensor_tensor(pair(weight[:]), share[:].rearrange("p c t -> p t c"), turn(fits[:]),
                                             ALU.mult))

        with ExitStack() as ctx:
            m = Memory(nc, ctx, tag + "s")
            xn4 = m.sb("xn4", [P, 2, J, D])
            row4 = m.sb("row4", [P, 2, 2 * J], U32)
            loaded = [m.sem(f"loaded{i}") for i in range(2)]
            scattered = m.sem("scattered")
            rows_set = m.sem("rows_set")
            sp_passed, pool_passed = m.sem("sp_passed"), m.sem("pool_passed")
            block = ctx.enter_context(nc.Block())

            @block.sync
            def _(sp):
                for s in range(2):
                    sp.dma_start(xn4[:, s], tiles_of(xn_d)[s]).then_inc(loaded[s], 16)
                with sp.Fori(1, STEPS // 2) as ii:
                    for s in range(2):
                        wait_alone(sp, scattered, (2 * ii + s - 1) * (2 * J * 16), sp_passed)
                        src = tiles_of(xn_d)[ds(2 * ii + s, 1)]
                        sp.dma_start(xn4[:, s], src.rearrange("a p j d -> (a p) j d")).then_inc(loaded[s], 16)

            @block.gpsimd
            def _(pool):
                def step(ii, first):
                    for s in range(2):
                        i = 2 * ii + s
                        nc.gpsimd.tensor_copy(row4[:, s, :], row_of[:, ds(2 * i * J, 2 * J)]).then_inc(rows_set, 1)
                        wait_alone(pool, loaded[s], (ii + 1) * 16, pool_passed)
                        wait_alone(pool, rows_set, i + 1, pool_passed)
                        for j in range(J):
                            for c in range(2):
                                if not (first and s == j == c == 0):
                                    wait_alone(pool, scattered, (i * 2 * J + 2 * j + c) * 16, pool_passed)
                                nc.gpsimd.indirect_dma_start(
                                    rows_in, bass.IndirectOffsetOnAxis(row4[:, s, 2 * j + c:2 * j + c + 1], 0),
                                    xn4[:, s, j, :], None).then_inc(scattered, 16)

                step(0, True)
                with pool.Fori(1, STEPS // 2) as ii:
                    step(ii, False)
                pool.wait_ge(scattered, STEPS * 2 * J * 16)

        with ExitStack() as ctx:
            m = Memory(nc, ctx, tag + "e")
            ident = m.sb("ident", [P, P])
            w13 = m.sb("w13", [P, E_N, C, 2 * F])
            w2 = m.sb("w2", [F, E_N, D])
            rows = m.sb("rows", [P, 2, ST, D])
            rowsT = m.sb("rowsT", [P, 2, D])
            up = m.sb("up", [P, 2, F])
            z = m.sb("z", [P, 2, F])
            th = m.sb("th", [P, 2, F])
            hid = m.sb("hid", [P, 2, F])
            hidT = m.sb("hidT", [F, 2, P])
            res = m.sb("res", [P, 2, ST, D])
            ps_t = m.ps("turned", [P, 2, D])
            ps_h = m.ps("hidden", [P, 2, D])
            ps_ht = m.ps("hidden_turned", [P, 2, D])
            ps_y = m.ps("result", [P, 2, D])
            consts_in = m.sem("consts_in")
            loaded = [m.sem(f"loaded{i}") for i in range(2)]
            stored = [m.sem(f"stored{i}") for i in range(2)]
            turned = m.sem("turned")
            rowsT_done = m.sem("rowsT_done")
            hidden_full = m.sem("hidden_full")
            up_done = m.sem("up_done")
            z_done = m.sem("z_done")
            th_done = m.sem("th_done")
            hid_done = m.sem("hid_done")
            hid_turned = m.sem("hid_turned")
            hidT_done = m.sem("hidT_done")
            result_full = m.sem("result_full")
            res_done = m.sem("res_done")
            sp_passed, pe_passed = m.sem("sp_passed"), m.sem("pe_passed")
            block = ctx.enter_context(nc.Block())
            rows_of = lambda d: d[0:NROWS, :].rearrange("(e j p) d -> e p j d", j=ST, p=P)

            @block.sync
            def _(sp):
                for s in range(2):
                    sp.sem_inc(stored[s], 16)
                    sp.dma_start(rows[:, s], rows_of(rows_in)[s]).then_inc(loaded[s], 16)
                sp.dma_start(ident[:], w["ident"]).then_inc(consts_in, 16)
                sp.dma_start(w13[:], w["w13T"].rearrange("e (c p) f -> p e c f", p=P)).then_inc(consts_in, 16)
                sp.dma_start(w2[:], w["w2T"].rearrange("e f d -> f e d")).then_inc(consts_in, 16)
                with sp.Fori(0, E_N // 2) as ee:
                    for s in range(2):
                        e = 2 * ee + s
                        wait_alone(sp, turned, (e + 1) * ST, sp_passed)
                        nxt = rows_of(rows_in)[ds((e + 2) % E_N, 1)]
                        sp.dma_start(rows[:, s], nxt.rearrange("a p j d -> (a p) j d")).then_inc(loaded[s], 16)
                        wait_alone(sp, res_done, 2 + (e + 1) * ST, sp_passed)
                        dst = rows_of(rows_out)[ds(e, 1)]
                        sp.dma_start(dst.rearrange("a p j d -> (a p) j d"), res[:, s]).then_inc(stored[s], 16)
                for s in range(2):
                    sp.wait_ge(stored[s], 16 + E_N // 2 * 16)
                    sp.wait_ge(loaded[s], (E_N // 2 + 1) * 16)

            @block.scalar
            def _(act):
                act.sem_inc(rowsT_done, 2)
                with act.Fori(0, E_N // 2) as ee:
                    for s in range(2):
                        n0 = (2 * ee + s) * ST
                        for q in range(ST + 1):
                            if q < ST:
                                n = n0 + q
                                act.wait_ge(turned, n + 1)
                                act.wait_ge(hidden_full, n + 1)
                                nc.scalar.copy(rowsT[:, q % 2, :], ps_t[:, q % 2, :]).then_inc(rowsT_done, 1)
                            if q >= 1:
                                n, r = n0 + q - 1, (q - 1) % 2
                                act.wait_ge(hidden_full, n + 3)
                                nc.scalar.copy(up[:, r, :], ps_h[:, r, F:2 * F]).then_inc(up_done, 1)
                                act.wait_ge(z_done, n + 3)
                                nc.scalar.activation(th[:, r, :], z[:, r, :], ACT.Tanh).then_inc(th_done, 1)

            @block.vector
            def _(dve):
                dve.sem_inc(z_done, 2)
                dve.sem_inc(hidT_done, 2)
                dve.sem_inc(res_done, 2)
                with dve.Fori(0, E_N // 2) as ee:
                    for s in range(2):
                        n0 = (2 * ee + s) * ST
                        for q in range(ST + 2):
                            if q < ST:
                                n, r = n0 + q, q % 2
                                dve.wait_ge(up_done, n + 1)
                                nc.vector.scalar_tensor_tensor(z[:, r, :], ps_h[:, r, 0:F], 0.5, up[:, r, :],
                                                               ALU.mult, ALU.mult).then_inc(z_done, 1)
                                dve.wait_ge(th_done, n + 1)
                                dve.wait_ge(z_done, n + 3)
                                dve.wait_ge(hid_turned, n + 1)
                                nc.vector.scalar_tensor_tensor(hid[:, r, :], th[:, r, :], 1.0, z[:, r, :],
                                                               ALU.add, ALU.mult).then_inc(hid_done, 1)
                            if 0 <= q - 1 < ST:
                                n, r = n0 + q - 1, (q - 1) % 2
                                dve.wait_ge(hid_turned, n + 3)
                                dve.wait_ge(result_full, n + 1)
                                nc.vector.tensor_copy(hidT[:, r, :], ps_ht[0:F, r, 0:P]).then_inc(hidT_done, 1)
                            if q - 2 >= 0:
                                n, r = n0 + q - 2, (q - 2) % 2
                                dve.wait_ge(result_full, n + 3)
                                if q == 2:
                                    dve.wait_ge(stored[s], 16 + ee * 16)
                                nc.vector.tensor_copy(res[:, s, q - 2, :], ps_y[:, r, :]).then_inc(res_done, 1)

            @block.tensor
            def _(pe):
                pe.wait_ge(consts_in, 3 * 16)
                pe.sem_inc(hidden_full, 2)
                pe.sem_inc(hid_turned, 2)
                pe.sem_inc(result_full, 2)
                with pe.Fori(0, E_N // 2) as ee:
                    for s in range(2):
                        e = 2 * ee + s
                        n0 = e * ST
                        pe.wait_ge(loaded[s], (ee + 1) * 16)
                        for q in range(ST + 3):
                            if q < ST:
                                n, r = n0 + q, q % 2
                                pe.wait_ge(rowsT_done, n + 1)
                                for c in range(C):
                                    last = nc.tensor.transpose(ps_t[:, r, c * P:(c + 1) * P],
                                                               rows[:, s, q, c * P:(c + 1) * P], ident[:])
                                last.then_inc(turned, 1)
                            if 0 <= q - 1 < ST:
                                n, r = n0 + q - 1, (q - 1) % 2
                                pe.wait_ge(rowsT_done, n + 3)
                                pe.wait_ge(z_done, n + 1)
                                for c in range(C):
                                    last = nc.tensor.matmul(
                                        ps_h[:, r, 0:2 * F], rowsT[:, r, c * P:(c + 1) * P],
                                        w13[:, ds(e, 1), c, :].rearrange("p a f -> p (a f)"),
                                        start=(c == 0), stop=(c == C - 1))
                                last.then_inc(hidden_full, 1)
                            if 0 <= q - 2 < ST:
                                n, r = n0 + q - 2, (q - 2) % 2
                                pe.wait_ge(hid_done, n + 1)
                                wait_alone(pe, hidT_done, n + 1, pe_passed)
                                nc.tensor.transpose(ps_ht[0:F, r, 0:P], hid[:, r, :], ident[:]).then_inc(hid_turned, 1)
                            if 0 <= q - 3 < ST:
                                n, r = n0 + q - 3, (q - 3) % 2
                                pe.wait_ge(hidT_done, n + 3)
                                wait_alone(pe, res_done, n + 1, pe_passed)
                                nc.tensor.matmul(ps_y[:, r, :], hidT[:, r, :],
                                                 w2[:, ds(e, 1), :].rearrange("f a d -> f (a d)"),
                                                 start=True, stop=True).then_inc(result_full, 1)

        with ExitStack() as ctx:
            m = Memory(nc, ctx, tag + "c")
            x4 = m.sb("x4", [P, 2, J, D])
            got = m.sb("got", [P, 2, 2 * J, D])
            row4 = m.sb("row4", [P, 2, 2 * J], U32)
            w4 = m.sb("w4", [P, 2, 2 * J])
            part = m.sb("part", [P, 2, J, D])
            total = m.sb("total", [P, 2, J, D])
            loaded = [m.sem(f"loaded{i}") for i in range(2)]
            gathered = [m.sem(f"gathered{i}") for i in range(2)]
            stored = [m.sem(f"stored{i}") for i in range(2)]
            rows_set = m.sem("rows_set")
            w4_set = m.sem("w4_set")
            part_done = m.sem("part_done")
            total_done = m.sem("total_done")
            sp_passed, pool_passed = m.sem("sp_passed"), m.sem("pool_passed")
            block = ctx.enter_context(nc.Block())

            @block.sync
            def _(sp):
                for s in range(2):
                    sp.sem_inc(stored[s], 16)
                    sp.dma_start(x4[:, s], tiles_of(x)[s]).then_inc(loaded[s], 16)
                with sp.Fori(0, STEPS // 2) as ii:
                    for s in range(2):
                        i = 2 * ii + s
                        wait_alone(sp, total_done, 2 * J + (i + 1) * J, sp_passed)
                        sp.dma_start(tiles_of(x_out)[ds(i, 1)].rearrange("a p j d -> (a p) j d"), total[:, s]
                                     ).then_inc(stored[s], 16)
                        nxt = tiles_of(x)[ds((i + 2) % STEPS, 1)]
                        sp.dma_start(x4[:, s], nxt.rearrange("a p j d -> (a p) j d")).then_inc(loaded[s], 16)
                for s in range(2):
                    sp.wait_ge(stored[s], 16 + STEPS // 2 * 16)
                    sp.wait_ge(loaded[s], (STEPS // 2 + 1) * 16)

            @block.gpsimd
            def _(pool):
                with pool.Fori(0, STEPS // 2) as ii:
                    for s in range(2):
                        i = 2 * ii + s
                        wait_alone(pool, total_done, (i + 1) * J, pool_passed)
                        nc.gpsimd.tensor_copy(row4[:, s, :], row_of[:, ds(2 * i * J, 2 * J)]).then_inc(rows_set, 1)
                        wait_alone(pool, rows_set, i + 1, pool_passed)
                        for n in range(2 * J):
                            nc.gpsimd.indirect_dma_start(
                                got[:, s, n, :], None, rows_out,
                                bass.IndirectOffsetOnAxis(row4[:, s, n:n + 1], 0)).then_inc(gathered[s], 16)

            @block.vector
            def _(dve):
                dve.sem_inc(total_done, 2 * J)
                with dve.Fori(0, STEPS // 2) as ii:
                    for s in range(2):
                        i = 2 * ii + s
                        nc.vector.tensor_copy(w4[:, s, :], weight[:, ds(2 * i * J, 2 * J)]).then_inc(w4_set, 1)
                        dve.wait_ge(w4_set, i + 1)
                        dve.wait_ge(loaded[s], (ii + 1) * 16)
                        dve.wait_ge(gathered[s], (ii + 1) * (2 * J * 16))
                        for j in range(J):
                            nc.vector.scalar_tensor_tensor(part[:, s, j, :], got[:, s, 2 * j, :],
                                                           w4[:, s, 2 * j:2 * j + 1], x4[:, s, j, :],
                                                           ALU.mult, ALU.add).then_inc(part_done, 1)
                        dve.wait_ge(stored[s], 16 + ii * 16)
                        dve.wait_ge(part_done, (i + 1) * J)
                        for j in range(J):
                            nc.vector.scalar_tensor_tensor(total[:, s, j, :], got[:, s, 2 * j + 1, :],
                                                           w4[:, s, 2 * j + 1:2 * j + 2], part[:, s, j, :],
                                                           ALU.mult, ALU.add).then_inc(total_done, 1)

def attention_b(nc, x, x_out, w):
    NT = S // P
    SCALE = float(HD) ** -0.5
    tile_rows = x.rearrange("(l t p) d -> t p l d", l=2, p=P)
    out_rows = x_out.rearrange("(l t p) d -> t p l d", l=2, p=P)
    PROJ = [(1, 0), (0, 1), (1, 1), (0, 2), (1, 2)]
    NP = len(PROJ)
    K = 13

    with ExitStack() as ctx:
        m = Memory(nc, ctx, "ab")
        ident = m.sb("ident", [P, P])
        wqkv = m.sb("wqkv", [P, C, 3 * D])
        wo = m.sb("wo", [P, C, D])
        half = m.sb("half", [P, 2])
        x2 = m.sb("x2", [P, 2, 2, D])
        xn = m.sb("xn", [P, 2, D])
        xnT = m.sb("xnT", [P, 2, 2, D])
        stats = m.sb("stats", [P, 2, 6])
        mv = m.sb("mv", [P, 2, 2])
        veps = m.sb("veps", [P, 2])
        rstd = m.sb("rstd", [P, 2])
        q1 = m.sb("q1", [P, D])
        v01 = m.sb("v01", [P, 2, D])
        prod = m.sb("prod", [P, 2, D])
        score = m.sb("score", [P, 2, H])
        top = m.sb("top", [P, H])
        prob = m.sb("prob", [P, 2, H])
        den = m.sb("den", [P, H])
        ctx1 = m.sb("ctx1", [P, D])
        ctxT = m.sb("ctxT", [P, 2, D])
        total = m.sb("total", [P, 2, 2, D])
        ps_t = m.ps("turned", [P, D])
        ps_p = m.ps("projected", [P, NP, D])
        ps_o = m.ps("out", [P, 2, D])

        consts_in = m.sem("consts_in")
        half_set = m.sem("half_set")
        loaded = [m.sem(f"loaded{i}") for i in range(2)]
        stored = [m.sem(f"stored{i}") for i in range(2)]
        stats_done = m.sem("stats_done")
        mean_done = m.sem("mean_done")
        var_done = m.sem("var_done")
        rstd_done = m.sem("rstd_done")
        xn_done = m.sem("xn_done")
        turned_x = m.sem("turned_x")
        turned_c = m.sem("turned_c")
        xnT_done = m.sem("xnT_done")
        ctxT_done = m.sem("ctxT_done")
        projected = m.sem("projected")
        q1_done = m.sem("q1_done")
        v_done = m.sem("v_done")
        chain = m.sem("chain")
        exp_done = m.sem("exp_done")
        ctx_done = m.sem("ctx_done")
        out_full = m.sem("out_full")
        total_done = m.sem("total_done")
        sp_passed, dve_passed = m.sem("sp_passed"), m.sem("dve_passed")
        block = ctx.enter_context(nc.Block())

        @block.sync
        def _(sp):
            for s in range(2):
                sp.sem_inc(stored[s], 16)
                sp.dma_start(x2[:, s], tile_rows[s]).then_inc(loaded[s], 16)
            sp.dma_start(ident[:], w["ident"]).then_inc(consts_in, 16)
            sp.dma_start(wqkv[:], w["bqkvT"].rearrange("(c p) n -> p c n", p=P)).then_inc(consts_in, 16)
            sp.dma_start(wo[:], w["boT"].rearrange("(c p) n -> p c n", p=P)).then_inc(consts_in, 16)
            with sp.Fori(0, NT // 2) as ii:
                for s in range(2):
                    i = 2 * ii + s
                    wait_alone(sp, total_done, 2 + 2 * i + 2, sp_passed)
                    sp.dma_start(out_rows[ds(i, 1)].rearrange("a p l d -> (a p) l d"), total[:, s]
                                 ).then_inc(stored[s], 16)
                    nxt = tile_rows[ds((i + 2) % NT, 1)]
                    sp.dma_start(x2[:, s], nxt.rearrange("a p l d -> (a p) l d")).then_inc(loaded[s], 16)
            for s in range(2):
                sp.wait_ge(stored[s], 16 + NT // 2 * 16)
                sp.wait_ge(loaded[s], (NT // 2 + 1) * 16)

        @block.gpsimd
        def _(pool):
            nc.gpsimd.memset(half[:], -0.5).then_inc(half_set, 1)
            pool.wait_ge(half_set, 1)
            with pool.Fori(0, NT) as i:
                pool.wait_ge(var_done, i + 1)
                nc.gpsimd.tensor_tensor(rstd[:], veps[:], half[:], ALU.pow).then_inc(rstd_done, 1)

        def pipeline(eng, front, back):
            front(0, 0)
            with eng.Fori(0, NT // 2 - 1) as ii:
                front(ii, 1)
                back(ii, 0)
                front(ii + 1, 0)
                back(ii, 1)
            front(NT // 2 - 1, 1)
            back(NT // 2 - 1, 0)
            back(NT // 2 - 1, 1, True)

        @block.scalar
        def _(act):
            for sem, n in ((xnT_done, 2), (ctxT_done, 2), (q1_done, 1), (v_done, 2)):
                act.sem_inc(sem, n)

            def front(ii, s):
                i = 2 * ii + s
                act.wait_ge(projected, (i + 1) * NP)
                for l in range(2):
                    act.wait_ge(turned_x, 1 + 2 * i + l + 1)
                    nc.scalar.copy(xnT[:, s, l, :], ps_t[:]).then_inc(xnT_done, 1)

            def back(ii, s, last_tile=False):
                i = 2 * ii + s
                act.wait_ge(projected, (2 + i) * NP + 1)
                act.wait_ge(chain, i * K + 2)
                nc.scalar.mul(q1[:], ps_p[:, 0, :], SCALE).then_inc(q1_done, 1)
                act.wait_ge(chain, i * K + 12)
                act.wait_ge(turned_c, 1 + 2 * i)
                for l in range(2):
                    act.wait_ge(projected, (2 + i) * NP + 4 + l)
                    nc.scalar.copy(v01[:, l, :], ps_p[:, 3 + l, :]).then_inc(v_done, 1)
                act.wait_ge(chain, (1 + i) * K + 6)
                nc.scalar.activation(prob[:], score[:], ACT.Exp).then_inc(exp_done, 1)
                for l in range(2):
                    act.wait_ge(turned_c, 1 + 2 * i + l + 1)
                    act.wait_ge(out_full, 2 * i + l + 1)
                    nc.scalar.copy(ctxT[:, l, :], ps_t[:]).then_inc(ctxT_done, 1)

            pipeline(act, front, back)

        @block.vector
        def _(dve):
            dve.sem_inc(chain, K)
            dve.sem_inc(total_done, 2)

            def front(ii, s):
                i = 2 * ii + s
                dve.wait_ge(loaded[s], (ii + 1) * 16)
                for l in range(2):
                    nc.vector.bn_stats(stats[:, l, :], x2[:, s, l, :]).then_inc(stats_done, 1)
                wait_alone(dve, stats_done, (i + 1) * 2, dve_passed)
                for l in range(2):
                    nc.vector.bn_aggr(mv[:, l, :], stats[:, l, :]).then_inc(mean_done, 1)
                dve.wait_ge(mean_done, (i + 1) * 2)
                nc.vector.tensor_scalar(veps[:], mv[:, :, 1], EPS, None, ALU.add).then_inc(var_done, 1)
                dve.wait_ge(rstd_done, i + 1)
                dve.wait_ge(turned_x, 1 + 2 * i)
                for l in range(2):
                    nc.vector.tensor_scalar(xn[:, l, :], x2[:, s, l, :], mv[:, l, 0:1], rstd[:, l:l + 1],
                                            ALU.subtract, ALU.mult).then_inc(xn_done, 1)

            def back(ii, s, last_tile=False):
                i = 2 * ii + s
                n = 0

                def link(ins):
                    nonlocal n
                    ins.then_inc(chain, 1)
                    n += 1
                    dve.wait_ge(chain, (1 + i) * K + n)

                heads = lambda a: a.rearrange("p (h d) -> p h d", d=HD)
                wide = lambda a: a.unsqueeze(2).to_broadcast([P, H, HD])
                dve.wait_ge(q1_done, 1 + i + 1)
                for l in range(2):
                    dve.wait_ge(projected, (2 + i) * NP + 2 + l)
                    link(nc.vector.tensor_tensor(prod[:, l, :], ps_p[:, 1 + l, :], q1[:], ALU.mult))
                link(nc.vector.tensor_reduce(score[:].rearrange("p l h -> p (l h)"),
                                             prod[:].rearrange("p l (h d) -> p (l h) d", d=HD), AX.X, ALU.add))
                link(nc.vector.tensor_tensor(top[:], score[:, 0, :], score[:, 1, :], ALU.max))
                for l in range(2):
                    link(nc.vector.tensor_tensor(score[:, l, :], score[:, l, :], top[:], ALU.subtract))
                dve.wait_ge(exp_done, i + 1)
                link(nc.vector.tensor_tensor(den[:], prob[:, 0, :], prob[:, 1, :], ALU.add))
                link(nc.vector.reciprocal(top[:], den[:]))
                for l in range(2):
                    link(nc.vector.tensor_tensor(score[:, l, :], prob[:, l, :], top[:], ALU.mult))
                for l in range(2):
                    dve.wait_ge(v_done, 2 + 2 * i + l + 1)
                    link(nc.vector.tensor_tensor(heads(prod[:, l, :]), heads(v01[:, l, :]), wide(score[:, l, :]),
                                                 ALU.mult))
                dve.wait_ge(turned_c, 1 + 2 * i)
                link(nc.vector.tensor_tensor(ctx1[:], prod[:, 0, :], prod[:, 1, :], ALU.add))
                assert n == K
                dve.wait_ge(stored[s], 16 + ii * 16)
                for l in range(2):
                    dve.wait_ge(out_full, 2 + 2 * i + l + 1)
                    nc.vector.tensor_tensor(total[:, s, l, :], ps_o[:, l, :], x2[:, s, l, :], ALU.add
                                            ).then_inc(total_done, 1)

            pipeline(dve, front, back)

        @block.tensor
        def _(pe):
            pe.wait_ge(consts_in, 3 * 16)
            for sem, n in ((turned_x, 1), (turned_c, 1), (projected, 2 * NP), (out_full, 2)):
                pe.sem_inc(sem, n)

            def front(ii, s):
                i = 2 * ii + s
                pe.wait_ge(ctxT_done, 2 * i if not isinstance(i, int) or i else 2)
                for l in range(2):
                    pe.wait_ge(xnT_done, 2 + 2 * i + l)
                    pe.wait_ge(xn_done, 2 * i + l + 1)
                    for c in range(C):
                        last = nc.tensor.transpose(ps_t[:, c * P:(c + 1) * P], xn[:, l, c * P:(c + 1) * P], ident[:])
                    last.then_inc(turned_x, 1)
                pe.wait_ge(xnT_done, 2 + 2 * i + 2)
                for n, (l, kind) in enumerate(PROJ):
                    sem, value = ((q1_done, 1 + i), (chain, i * K + 1), (chain, i * K + 2),
                                  (v_done, 2 * i + 1), (v_done, 2 * i + 2))[n]
                    pe.wait_ge(sem, value)
                    for c in range(C):
                        last = nc.tensor.matmul(ps_p[:, n, :], xnT[:, s, l, c * P:(c + 1) * P],
                                                wqkv[:, c, kind * D:(kind + 1) * D],
                                                start=(c == 0), stop=(c == C - 1))
                    last.then_inc(projected, 1)

            def back(ii, s, last_tile=False):
                i = 2 * ii + s
                pe.wait_ge(xnT_done, 2 + 2 * i + (2 if last_tile else 4))
                for l in range(2):
                    if l == 0:
                        pe.wait_ge(v_done, 2 + 2 * i + 1)
                    else:
                        pe.wait_ge(chain, (1 + i) * K + K)
                    pe.wait_ge(ctxT_done, 2 + 2 * i + l)
                    for c in range(C):
                        src = v01[:, 0, c * P:(c + 1) * P] if l == 0 else ctx1[:, c * P:(c + 1) * P]
                        last = nc.tensor.transpose(ps_t[:, c * P:(c + 1) * P], src, ident[:])
                    last.then_inc(turned_c, 1)
                for l in range(2):
                    pe.wait_ge(ctxT_done, 2 + 2 * i + l + 1)
                    pe.wait_ge(total_done, 2 * i + l + 1)
                    for c in range(C):
                        last = nc.tensor.matmul(ps_o[:, l, :], ctxT[:, l, c * P:(c + 1) * P], wo[:, c, :],
                                                start=(c == 0), stop=(c == C - 1))
                    last.then_inc(out_full, 1)

            pipeline(pe, front, back)


def constants():
    row = np.arange(P) % HD
    u = np.arange(S)
    distance = np.zeros((P, S), np.float32)
    distance[row < 3] = -(u // 16 * 16)
    distance[(row >= 3) & (row < 6)] = -(u % 16)
    distance[(row >= 6) & (row < 9)] = 1
    mult = np.zeros((P, P), np.float32)
    mult[row < 6] = 1
    mult[(row >= 6) & (row < 9)] = np.arange(P)
    part_of = np.zeros((P, 3), np.float32)
    for n in range(3):
        part_of[(row < 9) & (row % 3 == n), n] = 1
    slots = E_N * SLOTS
    return {
        "before": np.triu(np.ones((P, P), np.float32), 1),
        "expert_no": np.tile(np.arange(E_N, dtype=np.float32), (P, 1)),
        "spare_row": (slots + np.arange(P, dtype=np.float32))[:, None],
        "ident": np.eye(P, dtype=np.float32),
        "distance": distance,
        "mult": mult,
        "part_of": part_of,
    }


def lay_out(v):
    a = "L0_attn_a_"
    turned = lambda w: np.ascontiguousarray(np.swapaxes(w, -1, -2))
    rows = lambda r: np.ascontiguousarray(np.broadcast_to(r, (P, r.shape[0])))
    return {
        "x": np.ascontiguousarray(v[a + "hidden_states"].reshape(T, D)),
        "wqkvT": np.stack([turned(v[a + n]) for n in ("Wq", "Wk", "Wv")]),
        "woT": turned(v[a + "Wo"]),
        "qk_bias": np.ascontiguousarray(
            np.stack([v[a + n].reshape(GROUPS, P).T for n in ("bq", "bk")], axis=1)),
        "bv": rows(v[a + "bv"]),
        "bo": rows(v[a + "bo"]),
        "gateT": turned(v["L0_ffn_gate_w"]),
        "w13T": np.concatenate([turned(v["L0_ffn_w1"]), turned(v["L0_ffn_w3"])], axis=2),
        "w2T": turned(v["L0_ffn_w2"]),
        "bqkvT": turned(v["L0_attn_b_weight_qkv"]),
        "boT": turned(v["L0_attn_b_weight_out"]),
        "slopes": np.ascontiguousarray(np.repeat(v[a + "alibi_slopes"].reshape(GROUPS, HG).T, HD, axis=0)),
    }


def build(nc, ins, out):
    dram = lambda name, rows: nc.dram_tensor(name, (rows, D), F32, kind="Internal").ap()
    x1, x2, x3, xn = (dram(n, T) for n in ("x1", "x2", "x3", "xn"))
    rows_in, rows_out = (dram(n, E_N * SLOTS + P) for n in ("rows_in", "rows_out"))
    scratch = (xn, rows_in, rows_out)
    attention_a(nc, ins["x"], x1, ins)
    moe(nc, "f1", x1, x2, ins, scratch, True)
    attention_b(nc, x2, x3, ins)
    moe(nc, "f2", x3, out, ins, scratch, False)


def kernel(**inputs):
    import concourse.bacc as bacc
    from concourse.bass_utils import run_bass_kernel_spmd

    v = {k: np.asarray(a) for k, a in inputs.items()}
    arrays = dict(constants())
    arrays.update(lay_out(v))
    nc = bacc.Bacc("TRN2", target_bir_lowering=False, num_devices=1)
    ins = {}
    for name, a in arrays.items():
        ins[name] = nc.dram_tensor(f"in_{name}", a.shape, mybir.dt.from_np(a.dtype), kind="ExternalInput").ap()
    out = nc.dram_tensor("out_dram", (T, D), F32, kind="ExternalOutput").ap()
    build(nc, ins, out)
    r = run_bass_kernel_spmd(nc, [{f"in_{k}": a for k, a in arrays.items()}], core_ids=[0])
    return r.results[0]["out_dram"].reshape(B, S, D)
```

```python
from contextlib import ExitStack

import numpy as np

import concourse.bass as bass
from concourse import mybir

P = 128
B, S, D = 2, 2048, 512
H, HD = 16, 32
T = B * S
TILES = T // P
C = D // P
HG = P // HD
GROUPS = H // HG
QW = 512
QB, KB = S // QW, S // P
E_N, F = 12, 64
CAP = -(-T * 5 // (E_N * 4))
SLOTS = 512
EPS = 1e-5
CAPPED = 30.0
SQRT_HD = float(np.sqrt(np.float32(HD)))

F32 = mybir.dt.float32
BF16 = mybir.dt.bfloat16
F32R = mybir.dt.float32r
U32 = mybir.dt.uint32
ALU = mybir.AluOpType
ACT = mybir.ActivationFunctionType
AX = mybir.AxisListType
ds = bass.DynSlice


class Memory:

    def __init__(self, nc, ctx, tag):
        self.nc, self.ctx, self.tag = nc, ctx, tag
        self.sems = []
        ctx.callback(self.free_semaphores)

    def sb(self, name, shape, dt=F32):
        return self.ctx.enter_context(self.nc.sbuf_tensor(f"{self.tag}_{name}", shape, dt))

    def ps(self, name, shape, dt=F32):
        return self.ctx.enter_context(self.nc.psum_tensor(f"{self.tag}_ps_{name}", shape, dt))

    def sem(self, name):
        self.sems.append(self.nc.alloc_semaphore(f"{self.tag}_{name}"))
        return self.sems[-1]

    def free_semaphores(self):
        if self.sems:
            self.nc.clear_and_free_semaphores(self.sems)
            self.nc.all_engine_barrier()


def wait_alone(eng, sem, value, passed):
    eng.wait_ge(sem, value)
    eng.sem_inc(passed, 1)

def attention_a(nc, x, x_out, w):
    QUAD = 4
    units = [(h, qb, kq) for h in range(HG) for qb in range(QB) for kq in range(qb + 1)]
    NU = len(units)
    PER_HEAD = NU // HG
    last_of = {(h, qb): u for u, (h, qb, kq) in enumerate(units) if kq == qb}
    diag = {u: n for n, u in enumerate(sorted(last_of.values()))}
    NDIAG = len(diag)
    NPROJ = 3 * QB
    proj_after = {1 + 3 * k: k for k in range(NPROJ)}
    NEV = HG * QB
    RP = 4
    RANGES = S // 256
    AL = 2 * RANGES + 2
    KR = 3 * HD
    PAIR = 2 * HD
    LN_IT = 4

    def off(u, p):
        return 2 * P * p if u in diag else 0

    with ExitStack() as ctx:
        m = Memory(nc, ctx, "aa")
        ident = m.sb("ident", [P, P])
        slopes = m.sb("slopes", [P, 1])
        half = m.sb("half", [P, LN_IT])
        bias_all = m.sb("bias_all", [P, 2, GROUPS])
        bias = m.sb("bias", [P, 2])
        bv = m.sb("bv_g", [P, QW // P, P])
        bv_all = m.sb("bv_all", [P, D])
        bo_all = m.sb("bo_all", [P, D])
        wo = m.sb("wo", [P, C, D])
        wg = m.sb("wg", [P, 3, C, P])
        stats = m.sb("stats", [P, LN_IT, 6])
        mv = m.sb("mv", [P, LN_IT, 2])
        veps = m.sb("veps", [P, LN_IT])
        rstd = m.sb("rstd", [P, LN_IT])
        xnT = m.sb("xnT", [P, C, S])
        stage = m.sb("stage", [P, 2, 2, QW], F32R)
        v_next = m.sb("v_next", [P, S])
        v_ones = m.sb("v_ones", [P, KB, HG, PAIR])
        keys = m.sb("keys", [P, 2, S], F32R)
        queries = m.sb("queries", [P, 2, S], F32R)
        probs = m.sb("probs", [P, RP, HG, QW])
        taken = m.sb("taken", [PAIR, 2, QW])
        ctx_g = m.sb("ctx_g", [P, S])
        sums = m.sb("sums", [P, S])
        recip = m.sb("recip", [P, QW])
        ctxT = m.sb("ctxT", [P, GROUPS, S])
        assert LN_IT * D == HG * QW
        xn, x_in = probs[:, 0:2], probs[:, 2:4]
        x_new, x_old = probs[:, 0, 0:2, :], probs[:, 0, 2:4, :]

        alibi_d = nc.dram_tensor("alibi_rows", (H, AL, S), F32, kind="Internal").ap()
        qk_d = nc.dram_tensor("qk_parts", (B * GROUPS, 2, 2, P, S), F32, kind="Internal").ap()

        ps_s = m.ps("scores", [P, 2, 2, QW])
        ps_v = m.ps("values", [P, 2, QW])
        ps_x = m.ps("projected", [P, 2, QW])

        dve_passed, pool_passed, sp_passed = m.sem("dve_passed"), m.sem("pool_passed"), m.sem("sp_passed")
        consts_in = m.sem("consts_in")
        alibi_done = m.sem("alibi_done")
        alibi_stored = m.sem("alibi_stored")
        ranges_done = m.sem("ranges_done")
        ranges_in = m.sem("ranges_in")
        hi_done = m.sem("hi_done")
        qk_stored = [m.sem(f"qk_stored{i}") for i in range(2)]
        head_loaded = [m.sem(f"head_loaded{i}") for i in range(2)]
        evac_done = m.sem("evac_done")
        moved = [m.sem(f"moved{i}") for i in range(2)]
        ones_set = m.sem("ones_set")
        x_loaded = [m.sem(f"x_loaded{i}") for i in range(2)]
        ln_chain = m.sem("ln_chain")
        rstd_done = m.sem("rstd_done")
        var_done = m.sem("var_done")
        xn_done = m.sem("xn_done")
        turned = m.sem("turned")
        xnT_done = m.sem("xnT_done")
        w_loaded = m.sem("w_loaded")
        bias_done = m.sem("bias_done")
        shared_full = m.sem("shared_full")
        shared_free = m.sem("shared_free")
        group_set = m.sem("group_set")
        scores_done = m.sem("scores_done")
        tanh_done = m.sem("tanh_done")
        exp_done = m.sem("exp_done")
        masked = m.sem("masked")
        pv_done = m.sem("pv_done")
        recip_done = m.sem("recip_done")
        ctx_done = m.sem("ctx_done")
        out_full = m.sem("out_full")
        out_chain = m.sem("out_chain")
        out_done = m.sem("out_done")
        res_loaded = [m.sem(f"res_loaded{i}") for i in range(2)]
        stored = [m.sem(f"stored{i}") for i in range(2)]

        x_tiles = x.rearrange("(b i j p) d -> b i p j d", b=B, j=LN_IT, p=P)
        x_rows = x.rearrange("(b t p) d -> b t p d", b=B, p=P)
        o_rows = x_out.rearrange("(b t p) d -> b t p d", b=B, p=P)
        LN_STEPS = S // P // LN_IT
        NT = S // P

        block = ctx.enter_context(nc.Block())

        @block.sync
        def _(sp):
            for sem in stored:
                sp.sem_inc(sem, 16)
            for sem in qk_stored + moved:
                sp.sem_inc(sem, 32)
            for dst, src in ((xnT[:, 0, :], w["key_ranges"]), (v_next[0:AL, :], w["query_ranges"]), (slopes[:], w["slopes"]), (ident[:], w["ident"]),
                             (bias_all[:], w["qk_bias"]), (bv_all[:], w["bv"]), (bo_all[:], w["bo"]),
                             (wo[:], w["woT"].rearrange("(c p) n -> p c n", p=P))):
                sp.dma_start(dst, src).then_inc(consts_in, 16)

            def load_weights(hg, g):
                wait_alone(sp, shared_full, 1 + g * NPROJ, sp_passed)
                for n in range(3):
                    src = w["wqkvT"][n].rearrange("(c p) n -> p c n", p=P)
                    sp.dma_start(wg[:, n, :, :], src[:, :, ds(hg * P, P)]).then_inc(w_loaded, 16)

            load_weights(0, 0)
            sp.wait_ge(alibi_done, 4)
            for part in range(2):
                sp.dma_start(alibi_d[:, part * RANGES:(part + 1) * RANGES, :],
                             keys[:, part, :].bitcast(F32)).then_inc(alibi_stored, 16)
                sp.dma_start(alibi_d[:, 2 * RANGES + part, :],
                             queries[0:P:RANGES, part, :].bitcast(F32)).then_inc(alibi_stored, 16)
            sp.wait_ge(alibi_stored, 64)
            sp.wait_ge(ranges_done, 1)
            for i in range(2):
                sp.dma_start(queries[KR:KR + AL, i, :].bitcast(F32), queries[0:AL, 0, :].bitcast(F32)
                             ).then_inc(ranges_in, 16)
            sp.wait_ge(ranges_in, 32)

            def store_parts(g, k):
                kind, blk = divmod(k, QB)
                wait_alone(sp, shared_free, 2 + g * NPROJ + k + 1, sp_passed)
                for part in range(2):
                    dst = qk_d[ds(g, 1), kind, part, :, blk * QW:(blk + 1) * QW].rearrange("a p n -> (a p) n")
                    sp.dma_start(dst, stage[:, k % 2, part, :].bitcast(F32)).then_inc(qk_stored[k % 2], 16)

            def load_head(g, hg, h):
                wait_alone(sp, scores_done, (g * HG + h + 1) * 2 * PER_HEAD, sp_passed)
                if h == 0:
                    for i in range(2):
                        wait_alone(sp, qk_stored[i], 32 + (g + 1) * QB * 32, sp_passed)
                for dst, kind, parts in ((queries, 0, (0, 0, 1)), (keys, 1, (0, 1, 0))):
                    for n, part in enumerate(parts):
                        src = qk_d[ds(g, 1), kind, part, h * HD:(h + 1) * HD, :].rearrange("a p n -> (a p) n")
                        sp.dma_start(dst[n * HD:(n + 1) * HD, h % 2, :].bitcast(F32), src
                                     ).then_inc(head_loaded[h % 2], 16)
                src = alibi_d[ds(hg * HG + h, 1)].rearrange("a r n -> (a r) n")
                sp.dma_start(keys[KR:KR + AL, h % 2, :].bitcast(F32), src).then_inc(head_loaded[h % 2], 16)

            def move_context(g, h, qb):
                e = h * QB + qb
                wait_alone(sp, evac_done, 2 + g * NEV + e + 1, sp_passed)
                if h == 0:
                    wait_alone(sp, ctx_done, g * QB + qb + 1, sp_passed)
                cols = slice(qb * QW, (qb + 1) * QW)
                for n, dst in enumerate((ctx_g, sums)):
                    sp.dma_start(dst[h * HD:(h + 1) * HD, cols], taken[n * HD:(n + 1) * HD, e % 2, :]
                                 ).then_inc(moved[e % 2], 16)

            def group(hg, g, project):
                for u, (h, qb, kq) in enumerate(units):
                    if kq == qb == 0 and h < HG - 1:
                        load_head(g, hg, h + 1)
                    if project and kq == qb == 0 and h == HG - 1:
                        load_head(g + 1, hg + 1, 0)
                    if u - 2 in diag:
                        move_context(g, units[u - 2][0], units[u - 2][1])
                    if project and proj_after.get(u, NPROJ) < 2 * QB:
                        store_parts(g + 1, proj_after[u])
                move_context(g, HG - 1, QB - 1)
                if project:
                    load_weights((hg + 2) % GROUPS, g + 2)

            with sp.Fori(0, B) as b:
                for i in range(LN_STEPS):
                    if i >= 2:
                        wait_alone(sp, xn_done, b * LN_STEPS + i - 1, sp_passed)
                    else:
                        wait_alone(sp, stored[i], 16 + b * (NT // 2) * 16, sp_passed)
                        wait_alone(sp, out_done, 1 + b * NT, sp_passed)
                    sp.dma_start(x_in[:, i % 2, :, :], x_tiles[ds(b, 1), i].rearrange("a p j d -> (a p) j d")
                                 ).then_inc(x_loaded[i % 2], 16)
                for k in range(2 * QB):
                    store_parts(b * GROUPS, k)
                load_head(b * GROUPS, 0, 0)
                load_weights(1, b * GROUPS + 1)
                with sp.Fori(0, GROUPS - 1) as hg:
                    group(hg, b * GROUPS + hg, True)
                group(GROUPS - 1, b * GROUPS + GROUPS - 1, False)
                for t in range(NT):
                    if t >= 2:
                        wait_alone(sp, out_done, 1 + b * NT + t - 1, sp_passed)
                    else:
                        wait_alone(sp, ctx_done, QB + (b + 1) * GROUPS * QB, sp_passed)
                    sp.dma_start(x_old[:, t % 2, :], x_rows[ds(b, 1), t].rearrange("a p d -> (a p) d")
                                 ).then_inc(res_loaded[t % 2], 16)
                    wait_alone(sp, out_done, 1 + b * NT + t + 1, sp_passed)
                    sp.dma_start(o_rows[ds(b, 1), t].rearrange("a p d -> (a p) d"), x_new[:, t % 2, :]
                                 ).then_inc(stored[t % 2], 16)
            for i in range(2):
                sp.wait_ge(stored[i], 16 + B * NT // 2 * 16)
            sp.wait_ge(w_loaded, (B * GROUPS + 1) * 48)

        @block.gpsimd
        def _(pool):
            nc.gpsimd.memset(v_ones[:], 1.0).then_inc(ones_set, 1)
            nc.gpsimd.memset(half[:], -0.5).then_inc(ones_set, 1)
            nc.gpsimd.memset(xnT[:, 1, :], 1.0).then_inc(ones_set, 1)
            pool.wait_ge(ones_set, 3)
            with pool.Fori(0, B) as b:
                for i in range(LN_STEPS):
                    pool.wait_ge(var_done, b * LN_STEPS + i + 1)
                    nc.gpsimd.tensor_tensor(rstd[:], veps[:], half[:], ALU.pow).then_inc(rstd_done, 1)

                def masks(g):
                    for u in diag:
                        wait_alone(pool, exp_done, g * NU + u + 1, pool_passed)
                        for p in range(2):
                            at = probs[:, u % RP, 2 * p:2 * p + 2, off(u, p):off(u, p) + 2 * P]
                            nc.gpsimd.affine_select(out=at, in_=at, compare_op=ALU.is_ge, fill=0.0, base=0,
                                                    pattern=[[-P, 2], [1, 2 * P]], channel_multiplier=-1
                                                    ).then_inc(masked, 1)

                with pool.Fori(0, GROUPS) as hg:
                    masks(b * GROUPS + hg)

        @block.scalar
        def _(act):
            act.sem_inc(tanh_done, 1)
            with act.Fori(0, B) as b:
                for i in range(LN_STEPS * LN_IT):
                    act.wait_ge(turned, b * NT + i + 1)
                    nc.scalar.copy(xnT[:, :, i * P:(i + 1) * P],
                                   ps_s[:, i % 4 // 2, i % 2, :].rearrange("p (c t) -> p c t", c=C)
                                   ).then_inc(xnT_done, 1)

                def group(g):
                    for u in range(NU):
                        r = u % RP
                        act.wait_ge(pv_done, g * NU + u + 1)
                        for p in range(2):
                            act.wait_ge(scores_done, 4 * PER_HEAD + (g * NU + u) * 2 + p + 1)
                            nc.scalar.activation(probs[:, r, 2 * p:2 * p + 2, off(u, p):],
                                                 ps_s[:, p, :, off(u, p):], ACT.Tanh,
                                                 scale=1.0 / (SQRT_HD * CAPPED)).then_inc(tanh_done, 1)
                        act.wait_ge(tanh_done, 1 + (g * NU + u) * 2 + 2)
                        if u in diag:
                            for p in range(2):
                                at = probs[:, r, 2 * p:2 * p + 2, off(u, p):]
                                last = nc.scalar.activation(at, at, ACT.Exp, scale=CAPPED)
                        else:
                            last = nc.scalar.activation(probs[:, r], probs[:, r], ACT.Exp, scale=CAPPED)
                        last.then_inc(exp_done, 1)

                with act.Fori(0, GROUPS) as hg:
                    group(b * GROUPS + hg)

        @block.vector
        def _(dve):
            for sem, n in ((shared_free, 2), (out_done, 1), (ctx_done, QB), (evac_done, 2)):
                dve.sem_inc(sem, n)
            dve.wait_ge(consts_in, 8 * 16)
            dve.wait_ge(ones_set, 3)
            for n, dst in enumerate((keys, queries)):
                nc.vector.tensor_scalar(dst[:, 0, :], xnT[:, n, :], slopes[:], None, ALU.mult).then_inc(alibi_done, 1)
                dve.wait_ge(alibi_done, 2 * n + 1)
                nc.vector.scalar_tensor_tensor(dst[:, 1, :], xnT[:, n, :], slopes[:], dst[:, 0, :].bitcast(F32),
                                               ALU.mult, ALU.subtract).then_inc(alibi_done, 1)
            dve.wait_ge(alibi_stored, 64)
            nc.vector.tensor_copy(queries[0:AL, 0, :], v_next[0:AL, :]).then_inc(ranges_done, 1)

            with dve.Fori(0, B) as b:
                for i in range(LN_STEPS):
                    dve.wait_ge(x_loaded[i % 2], (b * (LN_STEPS // 2) + i // 2 + 1) * 16)
                    for j in range(LN_IT):
                        nc.vector.bn_stats(stats[:, j, :], x_in[:, i % 2, j, :]).then_inc(ln_chain, 1)
                    wait_alone(dve, ln_chain, (b * LN_STEPS + i) * (2 * LN_IT) + LN_IT, dve_passed)
                    for j in range(LN_IT):
                        nc.vector.bn_aggr(mv[:, j, :], stats[:, j, :]).then_inc(ln_chain, 1)
                    dve.wait_ge(ln_chain, (b * LN_STEPS + i + 1) * (2 * LN_IT))
                    nc.vector.tensor_scalar(veps[:], mv[:, :, 1], EPS, None, ALU.add).then_inc(var_done, 1)
                    dve.wait_ge(rstd_done, b * LN_STEPS + i + 1)
                    if i >= 2:
                        dve.wait_ge(turned, b * NT + (i - 1) * LN_IT)
                    for j in range(LN_IT):
                        last = nc.vector.tensor_scalar(xn[:, i % 2, j, :], x_in[:, i % 2, j, :], mv[:, j, 0:1],
                                                       rstd[:, j:j + 1], ALU.subtract, ALU.mult)
                    last.then_inc(xn_done, 1)

                def take(k, g):
                    kind, blk = divmod(k, QB)
                    dve.wait_ge(shared_full, 1 + g * NPROJ + k + 1)
                    if kind < 2:
                        dve.wait_ge(qk_stored[k % 2], 32 + (g * QB + k // 2) * 32)
                        hi = stage[:, k % 2, 0, :]
                        nc.vector.tensor_scalar(hi, ps_x[:, k % 2, :], bias[:, kind:kind + 1], None, ALU.add
                                                ).then_inc(hi_done, 1)
                        dve.wait_ge(hi_done, g * 2 * QB + k + 1)
                        nc.vector.scalar_tensor_tensor(stage[:, k % 2, 1, :], ps_x[:, k % 2, :],
                                                       bias[:, kind:kind + 1], hi.bitcast(F32),
                                                       ALU.add, ALU.subtract).then_inc(shared_free, 1)
                    else:
                        tiles = QW // P
                        nc.vector.tensor_tensor(
                            v_next[:, blk * QW:(blk + 1) * QW].rearrange("p (t n) -> p t n", t=tiles),
                            ps_x[:, k % 2, :].rearrange("p (t n) -> p t n", t=tiles), bv[:], ALU.add
                            ).then_inc(shared_free, 1)

                def take_context(g, h, qb):
                    e = h * QB + qb
                    dve.wait_ge(pv_done, RP + g * NU + last_of[h, qb] + 1)
                    dve.wait_ge(moved[e % 2], 32 + (g * NEV // 2 + e // 2) * 32)
                    nc.vector.tensor_copy(taken[:, e % 2, :], ps_v[0:PAIR, e % 2, :]).then_inc(evac_done, 1)

                def divide(g, hg, qb):
                    e = (HG - 1) * QB + qb
                    dve.wait_ge(moved[e % 2], 32 + (g * NEV // 2 + e // 2 + 1) * 32)
                    cols = slice(qb * QW, (qb + 1) * QW)
                    dve.wait_ge(ctx_done, QB + g * QB + qb)
                    nc.vector.reciprocal(recip[:], sums[:, cols]).then_inc(recip_done, 1)
                    dve.wait_ge(recip_done, g * QB + qb + 1)
                    nc.vector.tensor_tensor(ctxT[:, ds(hg, 1), cols].rearrange("p a n -> p (a n)"),
                                            ctx_g[:, cols], recip[:], ALU.mult).then_inc(ctx_done, 1)

                def set_bias(hg, g):
                    nc.vector.tensor_copy(bias[:], bias_all[:, :, ds(hg, 1)].rearrange("p a b -> p (a b)")
                                          ).then_inc(bias_done, 1)
                    nc.vector.tensor_copy(bv[:, 0, :], bv_all[:, ds(hg * P, P)]).then_inc(bias_done, 1)
                    for t in range(1, QW // P):
                        nc.vector.tensor_copy(bv[:, t, :], bv_all[:, ds(hg * P, P)]).then_inc(bias_done, 1)
                    dve.wait_ge(bias_done, (g + 1) * 5)

                def group(hg, project):
                    g = b * GROUPS + hg
                    dve.wait_ge(shared_free, 2 + (g + 1) * NPROJ)
                    dve.wait_ge(pv_done, RP + g * NU)
                    nc.vector.tensor_copy(v_ones[:, :, :, 0:HD],
                                          v_next[:].rearrange("p (t h d) -> p t h d", h=HG, d=HD)
                                          ).then_inc(group_set, 1)
                    dve.wait_ge(group_set, g + 1)
                    if project:
                        set_bias(hg + 1, g + 1)
                    for u in range(NU):
                        if u - 2 in diag:
                            take_context(g, units[u - 2][0], units[u - 2][1])
                        if u - 4 in diag and units[u - 4][0] == HG - 1:
                            divide(g, hg, units[u - 4][1])
                        if project and u in proj_after:
                            take(proj_after[u], g + 1)
                    take_context(g, HG - 1, QB - 1)
                    divide(g, hg, QB - 1)

                set_bias(0, b * GROUPS)
                for k in range(NPROJ):
                    take(k, b * GROUPS)
                with dve.Fori(0, GROUPS - 1) as hg:
                    group(hg, True)
                group(GROUPS - 1, False)

                for t in range(NT):
                    dve.wait_ge(out_full, b * NT + t + 1)
                    if t >= 2:
                        dve.wait_ge(stored[t % 2], 16 + (b * (NT // 2) + t // 2) * 16)
                    nc.vector.tensor_tensor(x_new[:, t % 2, :], ps_s[:, 0, t % 2, :], bo_all[:], ALU.add
                                            ).then_inc(out_chain, 1)
                    dve.wait_ge(out_chain, b * NT + t + 1)
                    dve.wait_ge(res_loaded[t % 2], (b * (NT // 2) + t // 2 + 1) * 16)
                    nc.vector.tensor_tensor(x_new[:, t % 2, :], x_new[:, t % 2, :], x_old[:, t % 2, :], ALU.add
                                            ).then_inc(out_done, 1)

        @block.tensor
        def _(pe):
            for sem, n in ((pv_done, RP), (shared_full, 1), (scores_done, 4 * PER_HEAD)):
                pe.sem_inc(sem, n)
            pe.wait_ge(consts_in, 8 * 16)
            pe.wait_ge(ones_set, 3)
            pe.wait_ge(alibi_done, 4)
            pe.wait_ge(ranges_in, 32)

            with pe.Fori(0, B) as b:
                for i in range(NT):
                    if i >= 4:
                        pe.wait_ge(xnT_done, b * NT + i - 3)
                    else:
                        pe.wait_ge(out_done, 1 + b * NT)
                    pe.wait_ge(xn_done, b * LN_STEPS + i // LN_IT + 1)
                    for c in range(C):
                        last = nc.tensor.transpose(ps_s[:, i % 4 // 2, i % 2, c * P:(c + 1) * P],
                                                   xn[:, i // LN_IT % 2, i % LN_IT, c * P:(c + 1) * P], ident[:])
                    last.then_inc(turned, 1)
                pe.wait_ge(xnT_done, (b + 1) * NT)

                def project(k, g):
                    kind, blk = divmod(k, QB)
                    if k == 0:
                        pe.wait_ge(w_loaded, (g + 1) * 48)
                    pe.wait_ge(shared_free, g * NPROJ + k + 1)
                    dst = ps_x[:, k % 2, :]
                    if kind < 2:
                        for c in range(C):
                            last = nc.tensor.matmul(dst, wg[:, kind, c, :], xnT[:, c, blk * QW:(blk + 1) * QW],
                                                    start=(c == 0), stop=(c == C - 1))
                    else:
                        for t in range(QW // P):
                            at = blk * QW + t * P
                            for c in range(C):
                                last = nc.tensor.matmul(dst[:, t * P:(t + 1) * P], xnT[:, c, at:at + P],
                                                        wg[:, 2, c, :], start=(c == 0), stop=(c == C - 1))
                    last.then_inc(shared_full, 1)

                def scores(g, u, p):
                    h, qb, kq = units[u]
                    if qb == kq == p == 0:
                        pe.wait_ge(head_loaded[h % 2], (g * HG // 2 + h // 2 + 1) * 112)
                    pe.wait_ge(tanh_done, 1 + (g * NU + u) * 2 + p - 1 if u else 1 + g * NU * 2)
                    for i in range(2):
                        kb = kq * QUAD + 2 * p + i
                        last = nc.tensor.matmul(ps_s[:, p, i, off(u, p):],
                                                keys[0:KR + AL, h % 2, kb * P:(kb + 1) * P],
                                                queries[0:KR + AL, h % 2, qb * QW + off(u, p):(qb + 1) * QW],
                                                start=True, stop=True)
                    last.then_inc(scores_done, 1)

                def values(g, u, p):
                    h, qb, kq = units[u]
                    e = h * QB + qb
                    if p == 0:
                        if kq == 0:
                            pe.wait_ge(evac_done, g * NEV + e + 1)
                        if u in diag:
                            pe.wait_ge(masked, 2 * (g * NDIAG + diag[u] + 1))
                        else:
                            pe.wait_ge(exp_done, g * NU + u + 1)
                    for i in range(2):
                        n = 2 * p + i
                        first = n * P if u in diag else 0
                        last = nc.tensor.matmul(ps_v[0:PAIR, e % 2, first:], v_ones[:, kq * QUAD + n, h, :],
                                                probs[:, u % RP, n, first:], start=(kq == n == 0),
                                                stop=(kq == qb and n == QUAD - 1))
                    if p == 1:
                        last.then_inc(pv_done, 1)

                def group(hg, project_next):
                    g = b * GROUPS + hg
                    pe.wait_ge(group_set, g + 1)
                    scores(g, 0, 0)
                    scores(g, 0, 1)
                    for u in range(NU):
                        for p in range(2):
                            if u:
                                values(g, u - 1, p)
                            if u + 1 < NU:
                                scores(g, u + 1, p)
                        if project_next and u in proj_after:
                            project(proj_after[u], g + 1)
                    values(g, NU - 1, 0)
                    values(g, NU - 1, 1)

                for k in range(NPROJ):
                    project(k, b * GROUPS)
                with pe.Fori(0, GROUPS - 1) as hg:
                    group(hg, True)
                group(GROUPS - 1, False)

                for t in range(NT):
                    pe.wait_ge(ctx_done, QB + (b + 1) * GROUPS * QB)
                    if t >= 2:
                        pe.wait_ge(out_chain, b * NT + t - 1)
                    for c in range(C):
                        last = nc.tensor.matmul(ps_s[:, 0, t % 2, :], ctxT[:, c, t * P:(t + 1) * P], wo[:, c, :],
                                                start=(c == 0), stop=(c == C - 1))
                    last.then_inc(out_full, 1)

def moe(nc, tag, x, x_out, w, scratch, clear_scratch):
    xn_d, rows_in, rows_out = scratch
    NROWS = E_N * SLOTS
    J = 4
    STEPS = TILES // J
    ST = SLOTS // P
    NE = 2 * TILES
    tiles_of = lambda d: d.rearrange("(i j p) d -> i p j d", j=J, p=P)

    with ExitStack() as keep:
        k = Memory(nc, keep, tag)
        row_of = k.sb("row_of", [P, NE], U32)
        weight = k.sb("weight", [P, NE])

        with ExitStack() as ctx:
            m = Memory(nc, ctx, tag + "r")
            ident = m.sb("ident", [P, P])
            gate = m.sb("gate", [P, C, E_N])
            before = m.sb("before", [P, P], BF16)
            before_f = m.sb("before_f", [P, P])
            ones_b = m.sb("ones_b", [P, P], BF16)
            ones_f = m.sb("ones_f", [P, E_N * NE])
            expert_no = m.sb("expert_no", [P, E_N])
            spare_row = m.sb("spare_row", [P, 1])
            half = m.sb("half", [P, J])
            zero = m.sb("zero", [P, SLOTS * D // P])
            x_in = m.sb("x_in", [P, 2, J, D])
            xn = m.sb("xn", [P, 2, J, D])
            xnT = m.sb("xnT", [P, 2, J, D])
            stats = m.sb("stats", [P, J, 6])
            mv = m.sb("mv", [P, J, 2])
            veps = m.sb("veps", [P, J])
            rstd = m.sb("rstd", [P, J])
            logits = m.sb("logits", [P, J, E_N])
            best = m.sb("best", [P, J, 8])
            best_no = m.sb("best_no", [P, J, 8], U32)
            chosen_f = m.sb("chosen_f", [P, J, 2])
            chosen = m.sb("chosen", [P, NE])
            gap = m.sb("gap", [P, TILES])
            hot = m.sb("hot", [P, E_N, 2, TILES], BF16)
            e_gap = m.sb("e_gap", [P, TILES])
            den = m.sb("den", [P, TILES])
            share = m.sb("share", [P, 2, TILES])
            totals = m.sb("totals", [P, E_N * NE])
            running = m.sb("running", [P, E_N * NE])
            earlier = m.sb("earlier", [P, E_N * NE])
            place = m.sb("place", [P, E_N * NE])
            placed = m.sb("placed", [P, E_N * NE])
            pos = m.sb("pos", [P, NE])
            fits = m.sb("fits", [P, NE])
            row_f = m.sb("row_f", [P, NE])
            row_g = m.sb("row_g", [P, NE])
            ps_t = m.ps("turned", [P, J, D])
            ps_l = m.ps("logits", [P, 2, D])
            ps_c = m.ps("counts", [P, 2, D])

            consts_in = m.sem("consts_in")
            sets = m.sem("sets")
            cleared = m.sem("cleared")
            x_loaded = [m.sem(f"x_loaded{i}") for i in range(2)]
            xn_stored = [m.sem(f"xn_stored{i}") for i in range(2)]
            stats_done = m.sem("stats_done")
            mean_done = m.sem("mean_done")
            var_done = m.sem("var_done")
            rstd_done = m.sem("rstd_done")
            xn_done = m.sem("xn_done")
            turned = m.sem("turned")
            xnT_done = m.sem("xnT_done")
            logits_full = m.sem("logits_full")
            logits_done = m.sem("logits_done")
            best_done = m.sem("best_done")
            chain = m.sem("chain")
            gaps_done = m.sem("gaps_done")
            e_done = m.sem("e_done")
            prefix_full = m.sem("prefix_full")
            totals_full = m.sem("totals_full")
            chosen_done = m.sem("chosen_done")
            hot_done = m.sem("hot_done")
            place_done = m.sem("place_done")
            dve_passed, sp_passed = m.sem("dve_passed"), m.sem("sp_passed")

            block = ctx.enter_context(nc.Block())

            @block.sync
            def _(sp):
                for dst, src in ((ident, w["ident"]), (gate, w["gateT"].rearrange("(c p) e -> p c e", p=P)),
                                 (before_f, w["before"]), (expert_no, w["expert_no"]), (spare_row, w["spare_row"])):
                    sp.dma_start(dst[:], src).then_inc(consts_in, 16)
                for s in range(2):
                    sp.sem_inc(xn_stored[s], 16)
                    sp.dma_start(x_in[:, s], tiles_of(x)[s]).then_inc(x_loaded[s], 16)
                with sp.Fori(0, STEPS // 2) as ii:
                    for s in range(2):
                        wait_alone(sp, xn_done, (2 * ii + s + 1) * J, sp_passed)
                        sp.dma_start(tiles_of(xn_d)[ds(2 * ii + s, 1)].rearrange("a p j d -> (a p) j d"), xn[:, s]
                                     ).then_inc(xn_stored[s], 16)
                        nxt = tiles_of(x)[ds((2 * ii + 2 + s) % STEPS, 1)]
                        sp.dma_start(x_in[:, s], nxt.rearrange("a p j d -> (a p) j d")).then_inc(x_loaded[s], 16)
                for s in range(2):
                    sp.wait_ge(xn_stored[s], 16 + STEPS // 2 * 16)
                    sp.wait_ge(x_loaded[s], (STEPS // 2 + 1) * 16)
                if clear_scratch:
                    sp.wait_ge(sets, 4)
                    for e in range(E_N):
                        sp.dma_start(rows_in[e * SLOTS:(e + 1) * SLOTS, :].rearrange("(p r) d -> p (r d)", p=P),
                                     zero[:]).then_inc(cleared, 16)
                    for d in (rows_in, rows_out):
                        sp.dma_start(d[NROWS:NROWS + P, :], zero[:, 0:D]).then_inc(cleared, 16)
                    sp.wait_ge(cleared, (E_N + 2) * 16)

            @block.gpsimd
            def _(pool):
                nc.gpsimd.memset(ones_b[:], 1.0).then_inc(sets, 1)
                nc.gpsimd.memset(ones_f[:], 1.0).then_inc(sets, 1)
                nc.gpsimd.memset(half[:], -0.5).then_inc(sets, 1)
                nc.gpsimd.memset(zero[:], 0.0).then_inc(sets, 1)
                pool.wait_ge(consts_in, 5 * 16)
                nc.gpsimd.tensor_copy(before[:], before_f[:]).then_inc(sets, 1)
                pool.wait_ge(sets, 5)
                with pool.Fori(0, STEPS) as i:
                    pool.wait_ge(var_done, i + 1)
                    nc.gpsimd.tensor_tensor(rstd[:], veps[:], half[:], ALU.pow).then_inc(rstd_done, 1)

            @block.scalar
            def _(act):
                act.sem_inc(xnT_done, 1)
                with act.Fori(0, STEPS // 2) as ii:
                    for s in range(2):
                        i = 2 * ii + s
                        for j in range(J):
                            act.wait_ge(turned, i * J + j + 1)
                            if j == 0:
                                act.wait_ge(logits_full, i + 1)
                            nc.scalar.copy(xnT[:, s, j, :], ps_t[:, j, :]).then_inc(xnT_done, 1)
                act.wait_ge(gaps_done, STEPS)
                nc.scalar.activation(e_gap[:], gap[:], ACT.Exp).then_inc(e_done, 1)

            @block.tensor
            def _(pe):
                pe.wait_ge(consts_in, 5 * 16)
                pe.wait_ge(sets, 5)
                pe.sem_inc(logits_full, 2)
                with pe.Fori(0, STEPS // 2) as ii:
                    for s in range(2):
                        i = 2 * ii + s
                        pe.wait_ge(xn_done, (i + 1) * J)
                        pe.wait_ge(xnT_done, 1 + i * J)
                        for j in range(J):
                            for c in range(C):
                                last = nc.tensor.transpose(ps_t[:, j, c * P:(c + 1) * P],
                                                           xn[:, s, j, c * P:(c + 1) * P], ident[:])
                            last.then_inc(turned, 1)
                        pe.wait_ge(logits_done, i + 1)
                        for j in range(J):
                            pe.wait_ge(xnT_done, 1 + i * J + j + 1)
                            for c in range(C):
                                last = nc.tensor.matmul(ps_l[:, s, j * E_N:(j + 1) * E_N],
                                                        xnT[:, s, j, c * P:(c + 1) * P], gate[:, c, :],
                                                        start=(c == 0), stop=(c == C - 1))
                        last.then_inc(logits_full, 1)
                pe.wait_ge(hot_done, STEPS * (2 * J + 1))
                flat = hot[:, :, :, :].rearrange("p e s t -> p (e s t)")
                n = E_N * NE // 2
                for i in range(2):
                    last = nc.tensor.matmul(ps_c[:, i, 0:n], before[:], flat[:, i * n:(i + 1) * n], start=True, stop=True)
                last.then_inc(prefix_full, 1)
                pe.wait_ge(logits_done, 2 + STEPS)
                for i in range(2):
                    last = nc.tensor.matmul(ps_l[:, i, 0:n], ones_b[:], flat[:, i * n:(i + 1) * n], start=True, stop=True)
                last.then_inc(totals_full, 1)

            @block.vector
            def _(dve):
                dve.wait_ge(consts_in, 5 * 16)
                dve.wait_ge(sets, 4)
                dve.sem_inc(logits_done, 2)
                with dve.Fori(0, STEPS // 2) as ii:
                    for s in range(2):
                        i = 2 * ii + s
                        dve.wait_ge(x_loaded[s], (ii + 1) * 16)
                        for j in range(J):
                            nc.vector.bn_stats(stats[:, j, :], x_in[:, s, j, :]).then_inc(stats_done, 1)
                        wait_alone(dve, stats_done, (i + 1) * J, dve_passed)
                        for j in range(J):
                            nc.vector.bn_aggr(mv[:, j, :], stats[:, j, :]).then_inc(mean_done, 1)
                        dve.wait_ge(mean_done, (i + 1) * J)
                        nc.vector.tensor_scalar(veps[:], mv[:, :, 1], EPS, None, ALU.add).then_inc(var_done, 1)
                        dve.wait_ge(xn_stored[s], 16 + ii * 16)
                        dve.wait_ge(logits_done, i + 1)
                        dve.wait_ge(rstd_done, i + 1)
                        for j in range(J):
                            nc.vector.tensor_scalar(xn[:, s, j, :], x_in[:, s, j, :], mv[:, j, 0:1],
                                                    rstd[:, j:j + 1], ALU.subtract, ALU.mult).then_inc(xn_done, 1)
                        dve.wait_ge(logits_full, i + 3)
                        nc.vector.tensor_copy(logits[:].rearrange("p j e -> p (j e)"), ps_l[:, s, 0:J * E_N]
                                              ).then_inc(logits_done, 1)
                        wait_alone(dve, logits_done, i + 3, dve_passed)
                        for j in range(J):
                            nc.vector.max(best[:, j, :], logits[:, j, :]).then_inc(best_done, 1)
                        wait_alone(dve, best_done, (2 * i + 1) * J, dve_passed)
                        for j in range(J):
                            nc.vector.max_index(best_no[:, j, :], best[:, j, :], logits[:, j, :]).then_inc(best_done, 1)
                        nc.vector.tensor_tensor(gap[:, ds(i * J, J)], best[:, :, 1], best[:, :, 0], ALU.subtract
                                                ).then_inc(gaps_done, 1)
                        dve.wait_ge(best_done, (2 * i + 2) * J)
                        nc.vector.tensor_copy(chosen_f[:], best_no[:, :, 0:2]).then_inc(chosen_done, 1)
                        dve.wait_ge(chosen_done, i + 1)
                        nc.vector.tensor_copy(chosen[:, ds(2 * i * J, 2 * J)],
                                              chosen_f[:].rearrange("p j s -> p (j s)")).then_inc(hot_done, 1)
                        for j in range(J):
                            for c in range(2):
                                nc.vector.tensor_scalar(
                                    hot[:, :, c, ds(i * J + j, 1)].rearrange("p e a -> p (e a)"), expert_no[:],
                                    chosen_f[:, j, c:c + 1], None, ALU.is_equal).then_inc(hot_done, 1)
                dve.wait_ge(hot_done, STEPS * (2 * J + 1))
                n_chain = 0

                def link(ins):
                    nonlocal n_chain
                    ins.then_inc(chain, 1)
                    n_chain += 1
                    dve.wait_ge(chain, n_chain)

                dve.wait_ge(e_done, 1)
                link(nc.vector.tensor_scalar(den[:], e_gap[:], 1.0, None, ALU.add))
                link(nc.vector.reciprocal(share[:, 0, :], den[:]))
                link(nc.vector.tensor_tensor(share[:, 1, :], e_gap[:], share[:, 0, :], ALU.mult))
                dve.wait_ge(totals_full, 1)
                n = E_N * NE // 2
                for q in range(2):
                    link(nc.vector.tensor_copy(totals[:, q * n:(q + 1) * n], ps_l[:, q, 0:n]))
                link(nc.vector.tensor_tensor_scan(running[:], ones_f[:], totals[:], 0.0, ALU.mult, ALU.add))
                link(nc.vector.tensor_tensor(earlier[:], running[:], totals[:], ALU.subtract))
                dve.wait_ge(prefix_full, 1)
                for e in range(E_N):
                    q = e * NE // n
                    own = slice(e * NE, (e + 1) * NE)
                    nc.vector.scalar_tensor_tensor(place[:, own], earlier[:, own], earlier[:, e * NE:e * NE + 1],
                                                   ps_c[:, q, e * NE - q * n:(e + 1) * NE - q * n],
                                                   ALU.subtract, ALU.add).then_inc(place_done, 1)
                dve.wait_ge(place_done, E_N)
                link(nc.vector.tensor_tensor(placed[:], place[:], hot[:].rearrange("p e c t -> p (e c t)"), ALU.mult))
                link(nc.vector.tensor_reduce(pos[:], placed[:].rearrange("p (e n) -> p n e", e=E_N), AX.X, ALU.add))
                link(nc.vector.tensor_scalar(fits[:], pos[:], float(CAP), None, ALU.is_lt))
                turn = lambda a: a.rearrange("p (c t) -> p t c", c=2)
                pair = lambda a: a.rearrange("p (t c) -> p t c", c=2)
                link(nc.vector.scalar_tensor_tensor(pair(row_f[:]), pair(chosen[:]), float(SLOTS), turn(pos[:]),
                                                    ALU.mult, ALU.add))
                link(nc.vector.tensor_scalar(row_g[:], row_f[:], spare_row[:, 0:1], None, ALU.subtract))
                link(nc.vector.tensor_tensor(pair(row_f[:]), pair(row_g[:]), turn(fits[:]), ALU.mult))
                link(nc.vector.tensor_scalar(row_g[:], row_f[:], spare_row[:, 0:1], None, ALU.add))
                link(nc.vector.tensor_copy(row_of[:], row_g[:]))
                link(nc.vector.tensor_tensor(pair(weight[:]), share[:].rearrange("p c t -> p t c"), turn(fits[:]),
                                             ALU.mult))

        with ExitStack() as ctx:
            m = Memory(nc, ctx, tag + "s")
            xn4 = m.sb("xn4", [P, 2, J, D])
            row4 = m.sb("row4", [P, 2, 2 * J], U32)
            loaded = [m.sem(f"loaded{i}") for i in range(2)]
            scattered = m.sem("scattered")
            rows_set = m.sem("rows_set")
            sp_passed, pool_passed = m.sem("sp_passed"), m.sem("pool_passed")
            block = ctx.enter_context(nc.Block())

            @block.sync
            def _(sp):
                for s in range(2):
                    sp.dma_start(xn4[:, s], tiles_of(xn_d)[s]).then_inc(loaded[s], 16)
                with sp.Fori(1, STEPS // 2) as ii:
                    for s in range(2):
                        wait_alone(sp, scattered, (2 * ii + s - 1) * (2 * J * 16), sp_passed)
                        src = tiles_of(xn_d)[ds(2 * ii + s, 1)]
                        sp.dma_start(xn4[:, s], src.rearrange("a p j d -> (a p) j d")).then_inc(loaded[s], 16)

            @block.gpsimd
            def _(pool):
                def step(ii, first):
                    for s in range(2):
                        i = 2 * ii + s
                        nc.gpsimd.tensor_copy(row4[:, s, :], row_of[:, ds(2 * i * J, 2 * J)]).then_inc(rows_set, 1)
                        wait_alone(pool, loaded[s], (ii + 1) * 16, pool_passed)
                        wait_alone(pool, rows_set, i + 1, pool_passed)
                        for j in range(J):
                            for c in range(2):
                                if not (first and s == j == c == 0):
                                    wait_alone(pool, scattered, (i * 2 * J + 2 * j + c) * 16, pool_passed)
                                nc.gpsimd.indirect_dma_start(
                                    rows_in, bass.IndirectOffsetOnAxis(row4[:, s, 2 * j + c:2 * j + c + 1], 0),
                                    xn4[:, s, j, :], None).then_inc(scattered, 16)

                step(0, True)
                with pool.Fori(1, STEPS // 2) as ii:
                    step(ii, False)
                pool.wait_ge(scattered, STEPS * 2 * J * 16)

        with ExitStack() as ctx:
            m = Memory(nc, ctx, tag + "e")
            ident = m.sb("ident", [P, P])
            w13 = m.sb("w13", [P, E_N, C, 2 * F])
            w2 = m.sb("w2", [F, E_N, D])
            rows = m.sb("rows", [P, 2, ST, D])
            rowsT = m.sb("rowsT", [P, 2, D])
            up = m.sb("up", [P, 2, F])
            z = m.sb("z", [P, 2, F])
            th = m.sb("th", [P, 2, F])
            hid = m.sb("hid", [P, 2, F])
            hidT = m.sb("hidT", [F, 2, P])
            res = m.sb("res", [P, 2, ST, D])
            ps_t = m.ps("turned", [P, 2, D])
            ps_h = m.ps("hidden", [P, 2, D])
            ps_ht = m.ps("hidden_turned", [P, 2, D])
            ps_y = m.ps("result", [P, 2, D])
            consts_in = m.sem("consts_in")
            loaded = [m.sem(f"loaded{i}") for i in range(2)]
            stored = [m.sem(f"stored{i}") for i in range(2)]
            turned = m.sem("turned")
            rowsT_done = m.sem("rowsT_done")
            hidden_full = m.sem("hidden_full")
            up_done = m.sem("up_done")
            z_done = m.sem("z_done")
            th_done = m.sem("th_done")
            hid_done = m.sem("hid_done")
            hid_turned = m.sem("hid_turned")
            hidT_done = m.sem("hidT_done")
            result_full = m.sem("result_full")
            res_done = m.sem("res_done")
            sp_passed, pe_passed = m.sem("sp_passed"), m.sem("pe_passed")
            block = ctx.enter_context(nc.Block())
            rows_of = lambda d: d[0:NROWS, :].rearrange("(e j p) d -> e p j d", j=ST, p=P)

            @block.sync
            def _(sp):
                for s in range(2):
                    sp.sem_inc(stored[s], 16)
                    sp.dma_start(rows[:, s], rows_of(rows_in)[s]).then_inc(loaded[s], 16)
                sp.dma_start(ident[:], w["ident"]).then_inc(consts_in, 16)
                sp.dma_start(w13[:], w["w13T"].rearrange("e (c p) f -> p e c f", p=P)).then_inc(consts_in, 16)
                sp.dma_start(w2[:], w["w2T"].rearrange("e f d -> f e d")).then_inc(consts_in, 16)
                with sp.Fori(0, E_N // 2) as ee:
                    for s in range(2):
                        e = 2 * ee + s
                        wait_alone(sp, turned, (e + 1) * ST, sp_passed)
                        nxt = rows_of(rows_in)[ds((e + 2) % E_N, 1)]
                        sp.dma_start(rows[:, s], nxt.rearrange("a p j d -> (a p) j d")).then_inc(loaded[s], 16)
                        wait_alone(sp, res_done, 2 + (e + 1) * ST, sp_passed)
                        dst = rows_of(rows_out)[ds(e, 1)]
                        sp.dma_start(dst.rearrange("a p j d -> (a p) j d"), res[:, s]).then_inc(stored[s], 16)
                for s in range(2):
                    sp.wait_ge(stored[s], 16 + E_N // 2 * 16)
                    sp.wait_ge(loaded[s], (E_N // 2 + 1) * 16)

            @block.scalar
            def _(act):
                act.sem_inc(rowsT_done, 2)
                with act.Fori(0, E_N // 2) as ee:
                    for s in range(2):
                        n0 = (2 * ee + s) * ST
                        for q in range(ST + 1):
                            if q < ST:
                                n = n0 + q
                                act.wait_ge(turned, n + 1)
                                act.wait_ge(hidden_full, n + 1)
                                nc.scalar.copy(rowsT[:, q % 2, :], ps_t[:, q % 2, :]).then_inc(rowsT_done, 1)
                            if q >= 1:
                                n, r = n0 + q - 1, (q - 1) % 2
                                act.wait_ge(hidden_full, n + 3)
                                nc.scalar.copy(up[:, r, :], ps_h[:, r, F:2 * F]).then_inc(up_done, 1)
                                act.wait_ge(z_done, n + 3)
                                nc.scalar.activation(th[:, r, :], z[:, r, :], ACT.Tanh).then_inc(th_done, 1)

            @block.vector
            def _(dve):
                dve.sem_inc(z_done, 2)
                dve.sem_inc(hidT_done, 2)
                dve.sem_inc(res_done, 2)
                with dve.Fori(0, E_N // 2) as ee:
                    for s in range(2):
                        n0 = (2 * ee + s) * ST
                        for q in range(ST + 2):
                            if q < ST:
                                n, r = n0 + q, q % 2
                                dve.wait_ge(up_done, n + 1)
                                nc.vector.scalar_tensor_tensor(z[:, r, :], ps_h[:, r, 0:F], 0.5, up[:, r, :],
                                                               ALU.mult, ALU.mult).then_inc(z_done, 1)
                                dve.wait_ge(th_done, n + 1)
                                dve.wait_ge(z_done, n + 3)
                                dve.wait_ge(hid_turned, n + 1)
                                nc.vector.scalar_tensor_tensor(hid[:, r, :], th[:, r, :], 1.0, z[:, r, :],
                                                               ALU.add, ALU.mult).then_inc(hid_done, 1)
                            if 0 <= q - 1 < ST:
                                n, r = n0 + q - 1, (q - 1) % 2
                                dve.wait_ge(hid_turned, n + 3)
                                dve.wait_ge(result_full, n + 1)
                                nc.vector.tensor_copy(hidT[:, r, :], ps_ht[0:F, r, 0:P]).then_inc(hidT_done, 1)
                            if q - 2 >= 0:
                                n, r = n0 + q - 2, (q - 2) % 2
                                dve.wait_ge(result_full, n + 3)
                                if q == 2:
                                    dve.wait_ge(stored[s], 16 + ee * 16)
                                nc.vector.tensor_copy(res[:, s, q - 2, :], ps_y[:, r, :]).then_inc(res_done, 1)

            @block.tensor
            def _(pe):
                pe.wait_ge(consts_in, 3 * 16)
                pe.sem_inc(hidden_full, 2)
                pe.sem_inc(hid_turned, 2)
                pe.sem_inc(result_full, 2)
                with pe.Fori(0, E_N // 2) as ee:
                    for s in range(2):
                        e = 2 * ee + s
                        n0 = e * ST
                        pe.wait_ge(loaded[s], (ee + 1) * 16)
                        for q in range(ST + 3):
                            if q < ST:
                                n, r = n0 + q, q % 2
                                pe.wait_ge(rowsT_done, n + 1)
                                for c in range(C):
                                    last = nc.tensor.transpose(ps_t[:, r, c * P:(c + 1) * P],
                                                               rows[:, s, q, c * P:(c + 1) * P], ident[:])
                                last.then_inc(turned, 1)
                            if 0 <= q - 1 < ST:
                                n, r = n0 + q - 1, (q - 1) % 2
                                pe.wait_ge(rowsT_done, n + 3)
                                pe.wait_ge(z_done, n + 1)
                                for c in range(C):
                                    last = nc.tensor.matmul(
                                        ps_h[:, r, 0:2 * F], rowsT[:, r, c * P:(c + 1) * P],
                                        w13[:, ds(e, 1), c, :].rearrange("p a f -> p (a f)"),
                                        start=(c == 0), stop=(c == C - 1))
                                last.then_inc(hidden_full, 1)
                            if 0 <= q - 2 < ST:
                                n, r = n0 + q - 2, (q - 2) % 2
                                pe.wait_ge(hid_done, n + 1)
                                wait_alone(pe, hidT_done, n + 1, pe_passed)
                                nc.tensor.transpose(ps_ht[0:F, r, 0:P], hid[:, r, :], ident[:]).then_inc(hid_turned, 1)
                            if 0 <= q - 3 < ST:
                                n, r = n0 + q - 3, (q - 3) % 2
                                pe.wait_ge(hidT_done, n + 3)
                                wait_alone(pe, res_done, n + 1, pe_passed)
                                nc.tensor.matmul(ps_y[:, r, :], hidT[:, r, :],
                                                 w2[:, ds(e, 1), :].rearrange("f a d -> f (a d)"),
                                                 start=True, stop=True).then_inc(result_full, 1)

        with ExitStack() as ctx:
            m = Memory(nc, ctx, tag + "c")
            x4 = m.sb("x4", [P, 2, J, D])
            got = m.sb("got", [P, 2, 2 * J, D])
            row4 = m.sb("row4", [P, 2, 2 * J], U32)
            w4 = m.sb("w4", [P, 2, 2 * J])
            part = m.sb("part", [P, 2, J, D])
            total = m.sb("total", [P, 2, J, D])
            loaded = [m.sem(f"loaded{i}") for i in range(2)]
            gathered = [m.sem(f"gathered{i}") for i in range(2)]
            stored = [m.sem(f"stored{i}") for i in range(2)]
            rows_set = m.sem("rows_set")
            w4_set = m.sem("w4_set")
            part_done = m.sem("part_done")
            total_done = m.sem("total_done")
            sp_passed, pool_passed = m.sem("sp_passed"), m.sem("pool_passed")
            block = ctx.enter_context(nc.Block())

            @block.sync
            def _(sp):
                for s in range(2):
                    sp.sem_inc(stored[s], 16)
                    sp.dma_start(x4[:, s], tiles_of(x)[s]).then_inc(loaded[s], 16)
                with sp.Fori(0, STEPS // 2) as ii:
                    for s in range(2):
                        i = 2 * ii + s
                        wait_alone(sp, total_done, 2 * J + (i + 1) * J, sp_passed)
                        sp.dma_start(tiles_of(x_out)[ds(i, 1)].rearrange("a p j d -> (a p) j d"), total[:, s]
                                     ).then_inc(stored[s], 16)
                        nxt = tiles_of(x)[ds((i + 2) % STEPS, 1)]
                        sp.dma_start(x4[:, s], nxt.rearrange("a p j d -> (a p) j d")).then_inc(loaded[s], 16)
                for s in range(2):
                    sp.wait_ge(stored[s], 16 + STEPS // 2 * 16)
                    sp.wait_ge(loaded[s], (STEPS // 2 + 1) * 16)

            @block.gpsimd
            def _(pool):
                with pool.Fori(0, STEPS // 2) as ii:
                    for s in range(2):
                        i = 2 * ii + s
                        wait_alone(pool, total_done, (i + 1) * J, pool_passed)
                        nc.gpsimd.tensor_copy(row4[:, s, :], row_of[:, ds(2 * i * J, 2 * J)]).then_inc(rows_set, 1)
                        wait_alone(pool, rows_set, i + 1, pool_passed)
                        for n in range(2 * J):
                            nc.gpsimd.indirect_dma_start(
                                got[:, s, n, :], None, rows_out,
                                bass.IndirectOffsetOnAxis(row4[:, s, n:n + 1], 0)).then_inc(gathered[s], 16)

            @block.vector
            def _(dve):
                dve.sem_inc(total_done, 2 * J)
                with dve.Fori(0, STEPS // 2) as ii:
                    for s in range(2):
                        i = 2 * ii + s
                        nc.vector.tensor_copy(w4[:, s, :], weight[:, ds(2 * i * J, 2 * J)]).then_inc(w4_set, 1)
                        dve.wait_ge(w4_set, i + 1)
                        dve.wait_ge(loaded[s], (ii + 1) * 16)
                        dve.wait_ge(gathered[s], (ii + 1) * (2 * J * 16))
                        for j in range(J):
                            nc.vector.scalar_tensor_tensor(part[:, s, j, :], got[:, s, 2 * j, :],
                                                           w4[:, s, 2 * j:2 * j + 1], x4[:, s, j, :],
                                                           ALU.mult, ALU.add).then_inc(part_done, 1)
                        dve.wait_ge(stored[s], 16 + ii * 16)
                        dve.wait_ge(part_done, (i + 1) * J)
                        for j in range(J):
                            nc.vector.scalar_tensor_tensor(total[:, s, j, :], got[:, s, 2 * j + 1, :],
                                                           w4[:, s, 2 * j + 1:2 * j + 2], part[:, s, j, :],
                                                           ALU.mult, ALU.add).then_inc(total_done, 1)

def attention_b(nc, x, x_out, w):
    NT = S // P
    SCALE = float(HD) ** -0.5
    tile_rows = x.rearrange("(l t p) d -> t p l d", l=2, p=P)
    out_rows = x_out.rearrange("(l t p) d -> t p l d", l=2, p=P)
    PROJ = [(1, 0), (0, 1), (1, 1), (0, 2), (1, 2)]
    NP = len(PROJ)
    K = 13

    with ExitStack() as ctx:
        m = Memory(nc, ctx, "ab")
        ident = m.sb("ident", [P, P])
        wqkv = m.sb("wqkv", [P, C, 3 * D])
        wo = m.sb("wo", [P, C, D])
        half = m.sb("half", [P, 2])
        x2 = m.sb("x2", [P, 2, 2, D])
        xn = m.sb("xn", [P, 2, D])
        xnT = m.sb("xnT", [P, 2, 2, D])
        stats = m.sb("stats", [P, 2, 6])
        mv = m.sb("mv", [P, 2, 2])
        veps = m.sb("veps", [P, 2])
        rstd = m.sb("rstd", [P, 2])
        q1 = m.sb("q1", [P, D])
        v01 = m.sb("v01", [P, 2, D])
        prod = m.sb("prod", [P, 2, D])
        score = m.sb("score", [P, 2, H])
        top = m.sb("top", [P, H])
        prob = m.sb("prob", [P, 2, H])
        den = m.sb("den", [P, H])
        ctx1 = m.sb("ctx1", [P, D])
        ctxT = m.sb("ctxT", [P, 2, D])
        total = m.sb("total", [P, 2, 2, D])
        ps_t = m.ps("turned", [P, D])
        ps_p = m.ps("projected", [P, NP, D])
        ps_o = m.ps("out", [P, 2, D])

        consts_in = m.sem("consts_in")
        half_set = m.sem("half_set")
        loaded = [m.sem(f"loaded{i}") for i in range(2)]
        stored = [m.sem(f"stored{i}") for i in range(2)]
        stats_done = m.sem("stats_done")
        mean_done = m.sem("mean_done")
        var_done = m.sem("var_done")
        rstd_done = m.sem("rstd_done")
        xn_done = m.sem("xn_done")
        turned_x = m.sem("turned_x")
        turned_c = m.sem("turned_c")
        xnT_done = m.sem("xnT_done")
        ctxT_done = m.sem("ctxT_done")
        projected = m.sem("projected")
        q1_done = m.sem("q1_done")
        v_done = m.sem("v_done")
        chain = m.sem("chain")
        exp_done = m.sem("exp_done")
        ctx_done = m.sem("ctx_done")
        out_full = m.sem("out_full")
        total_done = m.sem("total_done")
        sp_passed, dve_passed = m.sem("sp_passed"), m.sem("dve_passed")
        block = ctx.enter_context(nc.Block())

        @block.sync
        def _(sp):
            for s in range(2):
                sp.sem_inc(stored[s], 16)
                sp.dma_start(x2[:, s], tile_rows[s]).then_inc(loaded[s], 16)
            sp.dma_start(ident[:], w["ident"]).then_inc(consts_in, 16)
            sp.dma_start(wqkv[:], w["bqkvT"].rearrange("(c p) n -> p c n", p=P)).then_inc(consts_in, 16)
            sp.dma_start(wo[:], w["boT"].rearrange("(c p) n -> p c n", p=P)).then_inc(consts_in, 16)
            with sp.Fori(0, NT // 2) as ii:
                for s in range(2):
                    i = 2 * ii + s
                    wait_alone(sp, total_done, 2 + 2 * i + 2, sp_passed)
                    sp.dma_start(out_rows[ds(i, 1)].rearrange("a p l d -> (a p) l d"), total[:, s]
                                 ).then_inc(stored[s], 16)
                    nxt = tile_rows[ds((i + 2) % NT, 1)]
                    sp.dma_start(x2[:, s], nxt.rearrange("a p l d -> (a p) l d")).then_inc(loaded[s], 16)
            for s in range(2):
                sp.wait_ge(stored[s], 16 + NT // 2 * 16)
                sp.wait_ge(loaded[s], (NT // 2 + 1) * 16)

        @block.gpsimd
        def _(pool):
            nc.gpsimd.memset(half[:], -0.5).then_inc(half_set, 1)
            pool.wait_ge(half_set, 1)
            with pool.Fori(0, NT) as i:
                pool.wait_ge(var_done, i + 1)
                nc.gpsimd.tensor_tensor(rstd[:], veps[:], half[:], ALU.pow).then_inc(rstd_done, 1)

        def pipeline(eng, front, back):
            front(0, 0)
            with eng.Fori(0, NT // 2 - 1) as ii:
                front(ii, 1)
                back(ii, 0)
                front(ii + 1, 0)
                back(ii, 1)
            front(NT // 2 - 1, 1)
            back(NT // 2 - 1, 0)
            back(NT // 2 - 1, 1, True)

        @block.scalar
        def _(act):
            for sem, n in ((xnT_done, 2), (ctxT_done, 2), (q1_done, 1), (v_done, 2)):
                act.sem_inc(sem, n)

            def front(ii, s):
                i = 2 * ii + s
                act.wait_ge(projected, (i + 1) * NP)
                for l in range(2):
                    act.wait_ge(turned_x, 1 + 2 * i + l + 1)
                    nc.scalar.copy(xnT[:, s, l, :], ps_t[:]).then_inc(xnT_done, 1)

            def back(ii, s, last_tile=False):
                i = 2 * ii + s
                act.wait_ge(projected, (2 + i) * NP + 1)
                act.wait_ge(chain, i * K + 2)
                nc.scalar.mul(q1[:], ps_p[:, 0, :], SCALE).then_inc(q1_done, 1)
                act.wait_ge(chain, i * K + 12)
                act.wait_ge(turned_c, 1 + 2 * i)
                for l in range(2):
                    act.wait_ge(projected, (2 + i) * NP + 4 + l)
                    nc.scalar.copy(v01[:, l, :], ps_p[:, 3 + l, :]).then_inc(v_done, 1)
                act.wait_ge(chain, (1 + i) * K + 6)
                nc.scalar.activation(prob[:], score[:], ACT.Exp).then_inc(exp_done, 1)
                for l in range(2):
                    act.wait_ge(turned_c, 1 + 2 * i + l + 1)
                    act.wait_ge(out_full, 2 * i + l + 1)
                    nc.scalar.copy(ctxT[:, l, :], ps_t[:]).then_inc(ctxT_done, 1)

            pipeline(act, front, back)

        @block.vector
        def _(dve):
            dve.sem_inc(chain, K)
            dve.sem_inc(total_done, 2)

            def front(ii, s):
                i = 2 * ii + s
                dve.wait_ge(loaded[s], (ii + 1) * 16)
                for l in range(2):
                    nc.vector.bn_stats(stats[:, l, :], x2[:, s, l, :]).then_inc(stats_done, 1)
                wait_alone(dve, stats_done, (i + 1) * 2, dve_passed)
                for l in range(2):
                    nc.vector.bn_aggr(mv[:, l, :], stats[:, l, :]).then_inc(mean_done, 1)
                dve.wait_ge(mean_done, (i + 1) * 2)
                nc.vector.tensor_scalar(veps[:], mv[:, :, 1], EPS, None, ALU.add).then_inc(var_done, 1)
                dve.wait_ge(rstd_done, i + 1)
                dve.wait_ge(turned_x, 1 + 2 * i)
                for l in range(2):
                    nc.vector.tensor_scalar(xn[:, l, :], x2[:, s, l, :], mv[:, l, 0:1], rstd[:, l:l + 1],
                                            ALU.subtract, ALU.mult).then_inc(xn_done, 1)

            def back(ii, s, last_tile=False):
                i = 2 * ii + s
                n = 0

                def link(ins):
                    nonlocal n
                    ins.then_inc(chain, 1)
                    n += 1
                    dve.wait_ge(chain, (1 + i) * K + n)

                heads = lambda a: a.rearrange("p (h d) -> p h d", d=HD)
                wide = lambda a: a.unsqueeze(2).to_broadcast([P, H, HD])
                dve.wait_ge(q1_done, 1 + i + 1)
                for l in range(2):
                    dve.wait_ge(projected, (2 + i) * NP + 2 + l)
                    link(nc.vector.tensor_tensor(prod[:, l, :], ps_p[:, 1 + l, :], q1[:], ALU.mult))
                link(nc.vector.tensor_reduce(score[:].rearrange("p l h -> p (l h)"),
                                             prod[:].rearrange("p l (h d) -> p (l h) d", d=HD), AX.X, ALU.add))
                link(nc.vector.tensor_tensor(top[:], score[:, 0, :], score[:, 1, :], ALU.max))
                for l in range(2):
                    link(nc.vector.tensor_tensor(score[:, l, :], score[:, l, :], top[:], ALU.subtract))
                dve.wait_ge(exp_done, i + 1)
                link(nc.vector.tensor_tensor(den[:], prob[:, 0, :], prob[:, 1, :], ALU.add))
                link(nc.vector.reciprocal(top[:], den[:]))
                for l in range(2):
                    link(nc.vector.tensor_tensor(score[:, l, :], prob[:, l, :], top[:], ALU.mult))
                for l in range(2):
                    dve.wait_ge(v_done, 2 + 2 * i + l + 1)
                    link(nc.vector.tensor_tensor(heads(prod[:, l, :]), heads(v01[:, l, :]), wide(score[:, l, :]),
                                                 ALU.mult))
                dve.wait_ge(turned_c, 1 + 2 * i)
                link(nc.vector.tensor_tensor(ctx1[:], prod[:, 0, :], prod[:, 1, :], ALU.add))
                assert n == K
                dve.wait_ge(stored[s], 16 + ii * 16)
                for l in range(2):
                    dve.wait_ge(out_full, 2 + 2 * i + l + 1)
                    nc.vector.tensor_tensor(total[:, s, l, :], ps_o[:, l, :], x2[:, s, l, :], ALU.add
                                            ).then_inc(total_done, 1)

            pipeline(dve, front, back)

        @block.tensor
        def _(pe):
            pe.wait_ge(consts_in, 3 * 16)
            for sem, n in ((turned_x, 1), (turned_c, 1), (projected, 2 * NP), (out_full, 2)):
                pe.sem_inc(sem, n)

            def front(ii, s):
                i = 2 * ii + s
                pe.wait_ge(ctxT_done, 2 * i if not isinstance(i, int) or i else 2)
                for l in range(2):
                    pe.wait_ge(xnT_done, 2 + 2 * i + l)
                    pe.wait_ge(xn_done, 2 * i + l + 1)
                    for c in range(C):
                        last = nc.tensor.transpose(ps_t[:, c * P:(c + 1) * P], xn[:, l, c * P:(c + 1) * P], ident[:])
                    last.then_inc(turned_x, 1)
                pe.wait_ge(xnT_done, 2 + 2 * i + 2)
                for n, (l, kind) in enumerate(PROJ):
                    sem, value = ((q1_done, 1 + i), (chain, i * K + 1), (chain, i * K + 2),
                                  (v_done, 2 * i + 1), (v_done, 2 * i + 2))[n]
                    pe.wait_ge(sem, value)
                    for c in range(C):
                        last = nc.tensor.matmul(ps_p[:, n, :], xnT[:, s, l, c * P:(c + 1) * P],
                                                wqkv[:, c, kind * D:(kind + 1) * D],
                                                start=(c == 0), stop=(c == C - 1))
                    last.then_inc(projected, 1)

            def back(ii, s, last_tile=False):
                i = 2 * ii + s
                pe.wait_ge(xnT_done, 2 + 2 * i + (2 if last_tile else 4))
                for l in range(2):
                    if l == 0:
                        pe.wait_ge(v_done, 2 + 2 * i + 1)
                    else:
                        pe.wait_ge(chain, (1 + i) * K + K)
                    pe.wait_ge(ctxT_done, 2 + 2 * i + l)
                    for c in range(C):
                        src = v01[:, 0, c * P:(c + 1) * P] if l == 0 else ctx1[:, c * P:(c + 1) * P]
                        last = nc.tensor.transpose(ps_t[:, c * P:(c + 1) * P], src, ident[:])
                    last.then_inc(turned_c, 1)
                for l in range(2):
                    pe.wait_ge(ctxT_done, 2 + 2 * i + l + 1)
                    pe.wait_ge(total_done, 2 * i + l + 1)
                    for c in range(C):
                        last = nc.tensor.matmul(ps_o[:, l, :], ctxT[:, l, c * P:(c + 1) * P], wo[:, c, :],
                                                start=(c == 0), stop=(c == C - 1))
                    last.then_inc(out_full, 1)

            pipeline(pe, front, back)


def constants():
    at, ranges = np.arange(S), S // 256
    starts = 256 * (np.arange(P) % ranges)
    inside = (at // 256 == np.arange(ranges)[:, None]).astype(np.float32)
    from_start = np.broadcast_to(-(at % 256), (2, S)).astype(np.float32)
    slots = E_N * SLOTS
    return {
        "before": np.triu(np.ones((P, P), np.float32), 1),
        "expert_no": np.tile(np.arange(E_N, dtype=np.float32), (P, 1)),
        "spare_row": (slots + np.arange(P, dtype=np.float32))[:, None],
        "ident": np.eye(P, dtype=np.float32),
        "key_ranges": (at[None, :] - starts[:, None]).astype(np.float32),
        "query_ranges": np.concatenate([inside, inside, from_start]),
    }


def lay_out(v):
    a = "L0_attn_a_"
    turned = lambda w: np.ascontiguousarray(np.swapaxes(w, -1, -2))
    rows = lambda r: np.ascontiguousarray(np.broadcast_to(r, (P, r.shape[0])))
    return {
        "x": np.ascontiguousarray(v[a + "hidden_states"].reshape(T, D)),
        "wqkvT": np.stack([turned(v[a + n]) for n in ("Wq", "Wk", "Wv")]),
        "woT": turned(v[a + "Wo"]),
        "qk_bias": np.ascontiguousarray(
            np.stack([v[a + n].reshape(GROUPS, P).T for n in ("bq", "bk")], axis=1)),
        "bv": rows(v[a + "bv"]),
        "bo": rows(v[a + "bo"]),
        "gateT": turned(v["L0_ffn_gate_w"]),
        "w13T": np.concatenate([turned(v["L0_ffn_w1"]), turned(v["L0_ffn_w3"])], axis=2),
        "w2T": turned(v["L0_ffn_w2"]),
        "bqkvT": turned(v["L0_attn_b_weight_qkv"]),
        "boT": turned(v["L0_attn_b_weight_out"]),
        "slopes": np.repeat(v[a + "alibi_slopes"].reshape(-1), S // 256)[:, None],
    }


def build(nc, ins, out):
    dram = lambda name, rows: nc.dram_tensor(name, (rows, D), F32, kind="Internal").ap()
    x1, x2, x3, xn = (dram(n, T) for n in ("x1", "x2", "x3", "xn"))
    rows_in, rows_out = (dram(n, E_N * SLOTS + P) for n in ("rows_in", "rows_out"))
    scratch = (xn, rows_in, rows_out)
    attention_a(nc, ins["x"], x1, ins)
    moe(nc, "f1", x1, x2, ins, scratch, True)
    attention_b(nc, x2, x3, ins)
    moe(nc, "f2", x3, out, ins, scratch, False)


def kernel(**inputs):
    import concourse.bacc as bacc
    from concourse.bass_utils import run_bass_kernel_spmd

    v = {k: np.asarray(a) for k, a in inputs.items()}
    arrays = dict(constants())
    arrays.update(lay_out(v))
    nc = bacc.Bacc("TRN2", target_bir_lowering=False, num_devices=1)
    ins = {}
    for name, a in arrays.items():
        ins[name] = nc.dram_tensor(f"in_{name}", a.shape, mybir.dt.from_np(a.dtype), kind="ExternalInput").ap()
    out = nc.dram_tensor("out_dram", (T, D), F32, kind="ExternalOutput").ap()
    build(nc, ins, out)
    r = run_bass_kernel_spmd(nc, [{f"in_{k}": a for k, a in arrays.items()}], core_ids=[0])
    return r.results[0]["out_dram"].reshape(B, S, D)
```

```python
from contextlib import ExitStack

import numpy as np

import concourse.bass as bass
from concourse import mybir

P = 128
B, S, D = 2, 2048, 512
H, HD = 16, 32
T = B * S
TILES = T // P
C = D // P
HG = P // HD
GROUPS = H // HG
QW = 512
QB, KB = S // QW, S // P
E_N, F = 12, 64
CAP = -(-T * 5 // (E_N * 4))
SLOTS = 512
EPS = 1e-5
CAPPED = 30.0
SQRT_HD = float(np.sqrt(np.float32(HD)))

F32 = mybir.dt.float32
BF16 = mybir.dt.bfloat16
F32R = mybir.dt.float32r
U32 = mybir.dt.uint32
ALU = mybir.AluOpType
ACT = mybir.ActivationFunctionType
AX = mybir.AxisListType
ds = bass.DynSlice


class Memory:

    def __init__(self, nc, ctx, tag):
        self.nc, self.ctx, self.tag = nc, ctx, tag
        self.sems = []
        ctx.callback(self.free_semaphores)

    def sb(self, name, shape, dt=F32):
        return self.ctx.enter_context(self.nc.sbuf_tensor(f"{self.tag}_{name}", shape, dt))

    def ps(self, name, shape, dt=F32):
        return self.ctx.enter_context(self.nc.psum_tensor(f"{self.tag}_ps_{name}", shape, dt))

    def sem(self, name):
        self.sems.append(self.nc.alloc_semaphore(f"{self.tag}_{name}"))
        return self.sems[-1]

    def free_semaphores(self):
        if self.sems:
            self.nc.clear_and_free_semaphores(self.sems)
            self.nc.all_engine_barrier()


def wait_alone(eng, sem, value, passed):
    eng.wait_ge(sem, value)
    eng.sem_inc(passed, 1)

def attention_a(nc, x, x_out, w):
    QUAD = 4
    units = [(h, qb, kq) for h in range(HG) for qb in range(QB) for kq in range(qb + 1)]
    NU = len(units)
    PER_HEAD = NU // HG
    last_of = {(h, qb): u for u, (h, qb, kq) in enumerate(units) if kq == qb}
    diag = {u: n for n, u in enumerate(sorted(last_of.values()))}
    NDIAG = len(diag)
    pair_no = {up: n for n, up in enumerate((u, p) for u in range(NU) for p in range(1 if u in diag else 2))}
    NPAIRS = len(pair_no)
    NPROJ = 3 * QB
    piece_at = {3 + 4 * i // 3: divmod(i, 4) for i in range(4 * NPROJ)}
    step_at = {slot // 2 + 3: k for slot, (k, q) in piece_at.items() if q == 3}
    take_at = {k: u for u, k in step_at.items()}
    NEV = HG * QB
    RP, RL = 4, 2
    RANGES = S // 256
    AL = 2 * RANGES + 2
    KR = 3 * HD
    VC = 3 * HD
    LN_IT = 4

    AHEAD = 3
    USED = PER_HEAD + RL

    def late(u, lag, first):
        v = u - lag
        if v >= 0:
            return 0, v if v < NU else None
        return (0, None) if first else (1, v + NU)

    def off(u, p):
        return 2 * P * p if u in diag else 0

    with ExitStack() as ctx:
        m = Memory(nc, ctx, "aa")
        ident = m.sb("ident", [P, P])
        slopes = m.sb("slopes", [P, 1])
        half = m.sb("half", [P, LN_IT])
        bias_all = m.sb("bias_all", [P, 2, GROUPS])
        bias = m.sb("bias", [P, 2])
        bv = m.sb("bv_g", [P, QW // P, P])
        bv_all = m.sb("bv_all", [P, D])
        bo_all = m.sb("bo_all", [P, D])
        wg = m.sb("wg", [P, 3, C, P])
        stats = m.sb("stats", [P, LN_IT, 6])
        mv = m.sb("mv", [P, LN_IT, 2])
        veps = m.sb("veps", [P, LN_IT])
        rstd = m.sb("rstd", [P, LN_IT])
        xnT = m.sb("xnT", [P, C, S])
        stage = m.sb("stage", [P, 2, 2, QW], F32R)
        v_next = m.sb("v_next", [P, S])
        v_ones = m.sb("v_ones", [P, 2, KB, VC], F32R)
        keys = m.sb("keys", [P, 2, S], F32R)
        queries = m.sb("queries", [P, 2, S], F32R)
        probs_all = m.sb("probs", [P, RP * S + QW])
        probs = probs_all[:, 0:RP * S].rearrange("p (r n q) -> p r n q", r=RP, n=QUAD)
        until = m.sb("until", [P, P])
        parts = m.sb("parts", [P, RL, 2, HG, QW], F32R)
        taken = m.sb("taken", [VC, 2, QW])
        gathered = m.sb("gathered", [P, 3, S])
        ctx_out = m.sb("ctx_out", [P, 2, QW])
        assert LN_IT * D == HG * QW == S == C * D
        x_in = probs[:, 2:4]
        xn = gathered[:, 0:2, :].rearrange("p s (j d) -> p s j d", j=LN_IT)
        x_new, x_old = probs[:, 0, 0:2, :], probs[:, 0, 2:4, :]
        wo = v_next[:].rearrange("p (c d) -> p c d", c=C)
        ctxT = xnT

        alibi_d = nc.dram_tensor("alibi_rows", (H, AL, S), F32, kind="Internal").ap()
        ctx_d = nc.dram_tensor("contexts", (B, GROUPS - 1, P, S), F32, kind="Internal").ap()
        qk_d = nc.dram_tensor("qk_parts", (B * GROUPS, 2, 2, P, S), F32, kind="Internal").ap()

        ps_s = m.ps("scores", [P, 2, 2, QW])
        ps_v = m.ps("values", [P, 2, QW])
        ps_x = m.ps("projected", [P, 2, QW])

        dve_passed, pool_passed, sp_passed = m.sem("dve_passed"), m.sem("pool_passed"), m.sem("sp_passed")
        consts_in = m.sem("consts_in")
        alibi_done = m.sem("alibi_done")
        alibi_stored = m.sem("alibi_stored")
        ranges_done = m.sem("ranges_done")
        ranges_in = m.sem("ranges_in")
        hi_done = m.sem("hi_done")
        qk_stored = [m.sem(f"qk_stored{i}") for i in range(2)]
        head_loaded = [m.sem(f"head_loaded{i}") for i in range(2)]
        masked = m.sem("masked")
        parts_hi = m.sem("parts_hi")
        split_done = m.sem("split_done")
        added = m.sem("added")
        ctx_stored = [m.sem(f"ctx_stored{i}") for i in range(2)]
        ctx_loaded = m.sem("ctx_loaded")
        wo_loaded = m.sem("wo_loaded")
        evac_done = m.sem("evac_done")
        moved = [m.sem(f"moved{i}") for i in range(2)]
        ones_set = m.sem("ones_set")
        x_loaded = [m.sem(f"x_loaded{i}") for i in range(2)]
        ln_chain = m.sem("ln_chain")
        rstd_done = m.sem("rstd_done")
        var_done = m.sem("var_done")
        xn_done = m.sem("xn_done")
        turned = m.sem("turned")
        xnT_done = m.sem("xnT_done")
        w_loaded = [m.sem("w_qk_loaded"), m.sem("w_v_loaded")]
        bias_done = m.sem("bias_done")
        shared_full = m.sem("shared_full")
        shared_free = m.sem("shared_free")
        v_set = m.sem("v_set")
        scores_done = m.sem("scores_done")
        tanh_done = m.sem("tanh_done")
        exp_done = m.sem("exp_done")
        pv_done = m.sem("pv_done")
        recip_done = m.sem("recip_done")
        ctx_done = m.sem("ctx_done")
        out_full = m.sem("out_full")
        out_chain = m.sem("out_chain")
        out_done = m.sem("out_done")
        res_loaded = [m.sem(f"res_loaded{i}") for i in range(2)]
        stored = [m.sem(f"stored{i}") for i in range(2)]

        x_tiles = x.rearrange("(b i j p) d -> b i p j d", b=B, j=LN_IT, p=P)
        x_rows = x.rearrange("(b t p) d -> b t p d", b=B, p=P)
        o_rows = x_out.rearrange("(b t p) d -> b t p d", b=B, p=P)
        LN_STEPS = S // P // LN_IT
        NT = S // P

        block = ctx.enter_context(nc.Block())

        @block.sync
        def _(sp):
            for sem in stored:
                sp.sem_inc(sem, 16)
            for sem in ctx_stored:
                sp.sem_inc(sem, 16)
            for sem in qk_stored:
                sp.sem_inc(sem, 32)
            for sem in moved:
                sp.sem_inc(sem, 48)
            for dst, src in ((xnT[:, 0, :], w["key_ranges"]), (v_next[0:AL, :], w["query_ranges"]), (slopes[:], w["slopes"]), (ident[:], w["ident"]),
                             (bias_all[:], w["qk_bias"]), (bv_all[:], w["bv"]), (bo_all[:], w["bo"]), (until[:], w["until"])):
                sp.dma_start(dst, src).then_inc(consts_in, 16)

            def load_weights(hg, g, kinds):
                wait_alone(sp, shared_full, 1 + (g - 1) * NPROJ + (kinds[-1] + 1) * QB if kinds[-1] < 2
                           else 1 + g * NPROJ, sp_passed)
                for n in kinds:
                    src = w["wqkvT"][n].rearrange("(c p) n -> p c n", p=P)
                    sp.dma_start(wg[:, n, :, :], src[:, :, ds(hg * P, P)]).then_inc(w_loaded[n // 2], 16)

            for n in range(3):
                src = w["wqkvT"][n].rearrange("(c p) n -> p c n", p=P)
                sp.dma_start(wg[:, n, :, :], src[:, :, 0:P]).then_inc(w_loaded[n // 2], 16)
            sp.wait_ge(alibi_done, 4)
            for part in range(2):
                sp.dma_start(alibi_d[:, part * RANGES:(part + 1) * RANGES, :],
                             keys[:, part, :].bitcast(F32)).then_inc(alibi_stored, 16)
                sp.dma_start(alibi_d[:, 2 * RANGES + part, :],
                             queries[0:P:RANGES, part, :].bitcast(F32)).then_inc(alibi_stored, 16)
            sp.wait_ge(alibi_stored, 64)
            sp.wait_ge(ranges_done, 1)
            for i in range(2):
                sp.dma_start(queries[KR:KR + AL, i, :].bitcast(F32), queries[0:AL, 0, :].bitcast(F32)
                             ).then_inc(ranges_in, 16)
            sp.wait_ge(ranges_in, 32)

            def store_parts(g, k):
                kind, blk = divmod(k, QB)
                wait_alone(sp, shared_free, 2 + g * NPROJ + k + 1, sp_passed)
                for part in range(2):
                    dst = qk_d[ds(g, 1), kind, part, :, blk * QW:(blk + 1) * QW].rearrange("a p n -> (a p) n")
                    sp.dma_start(dst, stage[:, k % 2, part, :].bitcast(F32)).then_inc(qk_stored[k % 2], 16)

            def load_head(g, hg, h):
                wait_alone(sp, scores_done, (g * HG + h + 1) * 2 * PER_HEAD, sp_passed)
                if h == 0:
                    for i in range(2):
                        wait_alone(sp, qk_stored[i], 32 + (g + 1) * QB * 32, sp_passed)
                for dst, kind, parts in ((queries, 0, (0, 0, 1)), (keys, 1, (0, 1, 0))):
                    for n, part in enumerate(parts):
                        src = qk_d[ds(g, 1), kind, part, h * HD:(h + 1) * HD, :].rearrange("a p n -> (a p) n")
                        sp.dma_start(dst[n * HD:(n + 1) * HD, h % 2, :].bitcast(F32), src
                                     ).then_inc(head_loaded[h % 2], 16)
                src = alibi_d[ds(hg * HG + h, 1)].rearrange("a r n -> (a r) n")
                sp.dma_start(keys[KR:KR + AL, h % 2, :].bitcast(F32), src).then_inc(head_loaded[h % 2], 16)

            def move_context(g, h, qb):
                e = h * QB + qb
                wait_alone(sp, evac_done, 2 + g * NEV + e + 1, sp_passed)
                if h == 0:
                    wait_alone(sp, ctx_done, g * QB + qb + 1, sp_passed)
                cols = slice(qb * QW, (qb + 1) * QW)
                for n in range(3):
                    sp.dma_start(gathered[h * HD:(h + 1) * HD, n, cols], taken[n * HD:(n + 1) * HD, e % 2, :]
                                 ).then_inc(moved[e % 2], 16)

            def store_context(b, g, hg, qb):
                wait_alone(sp, ctx_done, QB + g * QB + qb + 1, sp_passed)
                dst = ctx_d[ds(b, 1), ds(hg, 1), :, qb * QW:(qb + 1) * QW].rearrange("a b p n -> (a b p) n")
                sp.dma_start(dst, ctx_out[:, qb % 2, :]).then_inc(ctx_stored[qb % 2], 16)

            def load_for_output(b, g):
                wait_alone(sp, shared_full, 1 + (g + 1) * NPROJ, sp_passed)
                for i in range(2):
                    wait_alone(sp, ctx_stored[i], 16 + (b + 1) * (GROUPS - 1) * (QB // 2) * 16, sp_passed)
                for n in range(GROUPS - 1):
                    sp.dma_start(ctxT[:, n, :], ctx_d[ds(b, 1), n].rearrange("a p n -> (a p) n")
                                 ).then_inc(ctx_loaded, 16)

            def group(b, hg, g, project):
                if not project:
                    load_for_output(b, g)
                for u, (h, qb, kq) in enumerate(units):
                    if not project and u == 2 * PER_HEAD + 5:
                        wait_alone(sp, v_set, 2 + (g + 1) * HG * 2, sp_passed)
                        sp.dma_start(wo, w["woT"].rearrange("(c p) n -> p c n", p=P)).then_inc(wo_loaded, 16)
                    if project and u == take_at[2 * QB - 1] + 1:
                        load_weights((hg + 2) % GROUPS, g + 2, (0, 1))
                    if kq == qb == 0 and h < HG - 1:
                        load_head(g, hg, h + 1)
                    if project and kq == qb == 0 and h == HG - 1:
                        load_head(g + 1, hg + 1, 0)
                    if u - 3 in diag:
                        move_context(g, units[u - 3][0], units[u - 3][1])
                    if project and u - 6 in diag and units[u - 6][0] == HG - 1:
                        store_context(b, g, hg, units[u - 6][1])
                    if project and step_at.get(u, NPROJ) < 2 * QB:
                        store_parts(g + 1, step_at[u])
                if project:
                    load_weights((hg + 2) % GROUPS, g + 2, (2,))
                move_context(g, HG - 1, QB - 1)
                if project:
                    for qb in range(QB):
                        if last_of[HG - 1, qb] + 6 >= NU:
                            store_context(b, g, hg, qb)

            with sp.Fori(0, B) as b:
                for i in range(LN_STEPS):
                    if i >= 2:
                        wait_alone(sp, xn_done, b * LN_STEPS + i - 1, sp_passed)
                    else:
                        wait_alone(sp, stored[i], 16 + b * (NT // 2) * 16, sp_passed)
                        wait_alone(sp, out_done, 1 + b * NT, sp_passed)
                    sp.dma_start(x_in[:, i % 2, :, :], x_tiles[ds(b, 1), i].rearrange("a p j d -> (a p) j d")
                                 ).then_inc(x_loaded[i % 2], 16)
                for k in range(2 * QB):
                    store_parts(b * GROUPS, k)
                load_head(b * GROUPS, 0, 0)
                load_weights(1, b * GROUPS + 1, (0, 1))
                load_weights(1, b * GROUPS + 1, (2,))
                with sp.Fori(0, GROUPS - 1) as hg:
                    group(b, hg, b * GROUPS + hg, True)
                group(b, GROUPS - 1, b * GROUPS + GROUPS - 1, False)
                for t in range(NT):
                    if t >= 2:
                        wait_alone(sp, out_done, 1 + b * NT + t - 1, sp_passed)
                    else:
                        wait_alone(sp, ctx_done, QB + (b + 1) * GROUPS * QB, sp_passed)
                    sp.dma_start(x_old[:, t % 2, :], x_rows[ds(b, 1), t].rearrange("a p d -> (a p) d")
                                 ).then_inc(res_loaded[t % 2], 16)
                    wait_alone(sp, out_done, 1 + b * NT + t + 1, sp_passed)
                    sp.dma_start(o_rows[ds(b, 1), t].rearrange("a p d -> (a p) d"), x_new[:, t % 2, :]
                                 ).then_inc(stored[t % 2], 16)
            for i in range(2):
                sp.wait_ge(stored[i], 16 + B * NT // 2 * 16)
            sp.wait_ge(w_loaded[0], (B * GROUPS + 1) * 32)
            sp.wait_ge(w_loaded[1], (B * GROUPS + 1) * 16)

        @block.gpsimd
        def _(pool):
            pool.sem_inc(ctx_done, QB)
            nc.gpsimd.memset(half[:], -0.5).then_inc(ones_set, 1)
            nc.gpsimd.memset(xnT[:, 1, :], 1.0).then_inc(ones_set, 1)
            pool.wait_ge(ones_set, 2)
            with pool.Fori(0, B) as b:
                for i in range(LN_STEPS):
                    pool.wait_ge(var_done, b * LN_STEPS + i + 1)
                    nc.gpsimd.tensor_tensor(rstd[:], veps[:], half[:], ALU.pow).then_inc(rstd_done, 1)

                def divide(g, hg, qb):
                    e = (HG - 1) * QB + qb
                    pool.wait_ge(moved[e % 2], 48 + (g * NEV // 2 + e // 2 + 1) * 48)
                    cols = slice(qb * QW, (qb + 1) * QW)
                    nc.gpsimd.tensor_tensor(gathered[:, 0, cols], gathered[:, 0, cols], gathered[:, 1, cols], ALU.add
                                            ).then_inc(added, 1)
                    pool.wait_ge(added, g * QB + qb + 1)
                    pool.wait_ge(recip_done, g * QB + qb + 1)
                    if hg is None:
                        dst = ctxT[:, GROUPS - 1, cols]
                    else:
                        done = b * (GROUPS - 1) * (QB // 2) + hg * (QB // 2) + qb // 2
                        pool.wait_ge(ctx_stored[qb % 2], 16 + done * 16)
                        dst = ctx_out[:, qb % 2, :]
                    nc.gpsimd.tensor_tensor(dst, gathered[:, 0, cols], gathered[:, 2, cols], ALU.mult
                                            ).then_inc(ctx_done, 1)

                def group(hg, first, last):
                    g = b * GROUPS + hg
                    for u in range(NU + 5 if last else NU):
                        back, v = late(u, 5, first)
                        if v in diag and units[v][0] == HG - 1:
                            divide(g - back, None if last and not back else hg - back, units[v][1])

                group(0, True, False)
                with pool.Fori(1, GROUPS - 1) as hg:
                    group(hg, False, False)
                group(GROUPS - 1, False, True)

        @block.scalar
        def _(act):
            act.sem_inc(tanh_done, 2)
            act.sem_inc(evac_done, 2)
            with act.Fori(0, B) as b:
                for i in range(LN_STEPS * LN_IT):
                    act.wait_ge(turned, b * NT + i + 1)
                    nc.scalar.copy(xnT[:, :, i * P:(i + 1) * P],
                                   ps_s[:, i % 4 // 2, i % 2, :].rearrange("p (c t) -> p c t", c=C)
                                   ).then_inc(xnT_done, 1)

                def take_context(g, h, qb):
                    e = h * QB + qb
                    act.wait_ge(pv_done, 2 * (USED + g * NU + last_of[h, qb] + 1))
                    act.wait_ge(moved[e % 2], 48 + (g * NEV // 2 + e // 2) * 48)
                    nc.scalar.copy(taken[:, e % 2, :], ps_v[0:VC, e % 2, :]).then_inc(evac_done, 1)

                def unit(g, u):
                    r = u % RP
                    act.wait_ge(split_done, 2 * (g * NU + u + 1))
                    if (u - RP) % NU in diag:
                        act.wait_ge(pv_done, 2 * (USED + g * NU + u - RP + 1))
                    for p in range(2):
                        act.wait_ge(scores_done, 4 * PER_HEAD + (g * NU + u) * 2 + p + 1)
                        nc.scalar.activation(probs[:, r, 2 * p:2 * p + 2, off(u, p):],
                                             ps_s[:, p, :, off(u, p):], ACT.Tanh,
                                             scale=1.0 / (SQRT_HD * CAPPED)).then_inc(tanh_done, 1)
                    act.wait_ge(tanh_done, 2 + (g * NU + u) * 2 + 2)
                    if u in diag:
                        for p in range(2):
                            at = probs[:, r, 2 * p:2 * p + 2, off(u, p):]
                            last = nc.scalar.activation(at, at, ACT.Exp, scale=CAPPED)
                    else:
                        last = nc.scalar.activation(probs[:, r], probs[:, r], ACT.Exp, scale=CAPPED)
                    last.then_inc(exp_done, 1)

                def group(hg, first, last):
                    g = b * GROUPS + hg
                    for u in range(NU + 4 if last else NU):
                        if u < NU:
                            unit(g, u)
                        back, v = late(u, 4, first)
                        if v in diag:
                            take_context(g - back, units[v][0], units[v][1])

                group(0, True, False)
                with act.Fori(1, GROUPS - 1) as hg:
                    group(hg, False, False)
                group(GROUPS - 1, False, True)

        @block.vector
        def _(dve):
            for sem, n in ((shared_free, 2), (out_done, 1), (split_done, 2 * RP), (v_set, 2)):
                dve.sem_inc(sem, n)
            dve.wait_ge(consts_in, 8 * 16)
            dve.wait_ge(ones_set, 2)
            for n, dst in enumerate((keys, queries)):
                nc.vector.tensor_scalar(dst[:, 0, :], xnT[:, n, :], slopes[:], None, ALU.mult).then_inc(alibi_done, 1)
                dve.wait_ge(alibi_done, 2 * n + 1)
                nc.vector.scalar_tensor_tensor(dst[:, 1, :], xnT[:, n, :], slopes[:], dst[:, 0, :].bitcast(F32),
                                               ALU.mult, ALU.subtract).then_inc(alibi_done, 1)
            nc.vector.tensor_copy(v_ones[:, :, :, 2 * HD:],
                                  xnT[:, 1, 0:2 * KB * HD].rearrange("p (i t d) -> p i t d", i=2, t=KB)
                                  ).then_inc(alibi_done, 1)
            dve.wait_ge(alibi_stored, 64)
            nc.vector.tensor_copy(queries[0:AL, 0, :], v_next[0:AL, :]).then_inc(ranges_done, 1)

            with dve.Fori(0, B) as b:
                for i in range(LN_STEPS):
                    dve.wait_ge(x_loaded[i % 2], (b * (LN_STEPS // 2) + i // 2 + 1) * 16)
                    for j in range(LN_IT):
                        nc.vector.bn_stats(stats[:, j, :], x_in[:, i % 2, j, :]).then_inc(ln_chain, 1)
                    wait_alone(dve, ln_chain, (b * LN_STEPS + i) * (2 * LN_IT) + LN_IT, dve_passed)
                    for j in range(LN_IT):
                        nc.vector.bn_aggr(mv[:, j, :], stats[:, j, :]).then_inc(ln_chain, 1)
                    dve.wait_ge(ln_chain, (b * LN_STEPS + i + 1) * (2 * LN_IT))
                    nc.vector.tensor_scalar(veps[:], mv[:, :, 1], EPS, None, ALU.add).then_inc(var_done, 1)
                    dve.wait_ge(rstd_done, b * LN_STEPS + i + 1)
                    if i >= 2:
                        dve.wait_ge(turned, b * NT + (i - 1) * LN_IT)
                    for j in range(LN_IT):
                        last = nc.vector.tensor_scalar(xn[:, i % 2, j, :], x_in[:, i % 2, j, :], mv[:, j, 0:1],
                                                       rstd[:, j:j + 1], ALU.subtract, ALU.mult)
                    last.then_inc(xn_done, 1)

                def take(k, g):
                    kind, blk = divmod(k, QB)
                    dve.wait_ge(shared_full, 1 + g * NPROJ + k + 1)
                    if kind < 2:
                        dve.wait_ge(qk_stored[k % 2], 32 + (g * QB + k // 2) * 32)
                        hi = stage[:, k % 2, 0, :]
                        nc.vector.tensor_scalar(hi, ps_x[:, k % 2, :], bias[:, kind:kind + 1], None, ALU.add
                                                ).then_inc(hi_done, 1)
                        dve.wait_ge(hi_done, g * 2 * QB + k + 1)
                        nc.vector.scalar_tensor_tensor(stage[:, k % 2, 1, :], ps_x[:, k % 2, :],
                                                       bias[:, kind:kind + 1], hi.bitcast(F32),
                                                       ALU.add, ALU.subtract).then_inc(shared_free, 1)
                    else:
                        dve.wait_ge(v_set, 2 + g * HG * 2)
                        tiles = QW // P
                        nc.vector.tensor_tensor(
                            v_next[:, blk * QW:(blk + 1) * QW].rearrange("p (t n) -> p t n", t=tiles),
                            ps_x[:, k % 2, :].rearrange("p (t n) -> p t n", t=tiles), bv[:], ALU.add
                            ).then_inc(shared_free, 1)

                def split(g, u):
                    r, s = u % RP, u % RL
                    dve.wait_ge(exp_done, g * NU + u + 1)
                    if u in diag:
                        squares = probs_all[:, r * S:r * S + QUAD * (QW + P)].rearrange(
                            "p (n q) -> p n q", n=QUAD)[:, :, 0:P]
                        nc.vector.tensor_tensor(squares, squares, until[:].unsqueeze(1).to_broadcast([P, QUAD, P]),
                                                ALU.mult).then_inc(masked, 1)
                        dve.wait_ge(masked, g * NDIAG + diag[u] + 1)
                    pairs = [(p, slice(2 * p, 2 * p + 2)) for p in range(1 if u in diag else 2)]
                    for p, pair in pairs:
                        dve.wait_ge(pv_done, 2 * (PER_HEAD + g * NU + u) + p + 1)
                        nc.vector.tensor_copy(parts[:, s, 0, pair], probs[:, r, pair]).then_inc(parts_hi, 1)
                    for p, pair in pairs:
                        dve.wait_ge(parts_hi, g * NPAIRS + pair_no[u, p] + 1)
                        nc.vector.tensor_tensor(parts[:, s, 1, pair], probs[:, r, pair],
                                                parts[:, s, 0, pair].bitcast(F32), ALU.subtract
                                                ).then_inc(split_done, 2 if u in diag else 1)

                def invert_sums(g, qb):
                    e = (HG - 1) * QB + qb
                    dve.wait_ge(moved[e % 2], 48 + (g * NEV // 2 + e // 2 + 1) * 48)
                    cols = slice(qb * QW, (qb + 1) * QW)
                    nc.vector.reciprocal(gathered[:, 2, cols], gathered[:, 2, cols]).then_inc(recip_done, 1)

                def set_bias(hg, g):
                    nc.vector.tensor_copy(bias[:], bias_all[:, :, ds(hg, 1)].rearrange("p a b -> p (a b)")
                                          ).then_inc(bias_done, 1)
                    nc.vector.tensor_copy(bv[:, 0, :], bv_all[:, ds(hg * P, P)]).then_inc(bias_done, 1)
                    for t in range(1, QW // P):
                        nc.vector.tensor_copy(bv[:, t, :], bv_all[:, ds(hg * P, P)]).then_inc(bias_done, 1)
                    dve.wait_ge(bias_done, (g + 1) * 5)

                def split_values(g, h):
                    dve.wait_ge(shared_free, 2 + (g + 1) * NPROJ)
                    dve.wait_ge(pv_done, 2 * (USED + g * NU + (h - 1) * PER_HEAD))
                    v = v_next[:].rearrange("p (t h d) -> p h t d", h=HG, d=HD)[:, h]
                    hi = v_ones[:, h % 2, :, 0:HD]
                    nc.vector.tensor_copy(hi, v).then_inc(v_set, 1)
                    dve.wait_ge(v_set, 2 + (g * HG + h) * 2 + 1)
                    nc.vector.tensor_tensor(v_ones[:, h % 2, :, HD:2 * HD], v, hi.bitcast(F32), ALU.subtract
                                            ).then_inc(v_set, 1)

                def group(hg, first, last):
                    g = b * GROUPS + hg
                    if not last:
                        set_bias(hg + 1, g + 1)
                    for u in range(NU + 5 if last else NU):
                        if u < NU:
                            split(g, u)
                        back, v = late(u, 5, first)
                        if v in diag and units[v][0] == HG - 1:
                            invert_sums(g - back, units[v][1])
                        if not last and u in step_at:
                            take(step_at[u], g + 1)
                        if u in (3, 3 + PER_HEAD, 3 + 2 * PER_HEAD):
                            split_values(g, u // PER_HEAD + 1)
                        if not last and u == take_at[NPROJ - 1] + 1:
                            split_values(g + 1, 0)

                set_bias(0, b * GROUPS)
                for k in range(NPROJ):
                    take(k, b * GROUPS)
                split_values(b * GROUPS, 0)
                group(0, True, False)
                with dve.Fori(1, GROUPS - 1) as hg:
                    group(hg, False, False)
                group(GROUPS - 1, False, True)

                for t in range(NT):
                    dve.wait_ge(out_full, b * NT + t + 1)
                    if t >= 2:
                        dve.wait_ge(stored[t % 2], 16 + (b * (NT // 2) + t // 2) * 16)
                    nc.vector.tensor_tensor(x_new[:, t % 2, :], ps_s[:, 0, t % 2, :], bo_all[:], ALU.add
                                            ).then_inc(out_chain, 1)
                    dve.wait_ge(out_chain, b * NT + t + 1)
                    dve.wait_ge(res_loaded[t % 2], (b * (NT // 2) + t // 2 + 1) * 16)
                    nc.vector.tensor_tensor(x_new[:, t % 2, :], x_new[:, t % 2, :], x_old[:, t % 2, :], ALU.add
                                            ).then_inc(out_done, 1)

        @block.tensor
        def _(pe):
            for sem, n in ((pv_done, 2 * USED), (shared_full, 1), (scores_done, 4 * PER_HEAD)):
                pe.sem_inc(sem, n)
            pe.wait_ge(consts_in, 8 * 16)
            pe.wait_ge(ones_set, 2)
            pe.wait_ge(alibi_done, 5)
            pe.wait_ge(ranges_in, 32)

            with pe.Fori(0, B) as b:
                for i in range(NT):
                    if i >= 4:
                        pe.wait_ge(xnT_done, b * NT + i - 3)
                    else:
                        pe.wait_ge(out_done, 1 + b * NT)
                    pe.wait_ge(xn_done, b * LN_STEPS + i // LN_IT + 1)
                    for c in range(C):
                        last = nc.tensor.transpose(ps_s[:, i % 4 // 2, i % 2, c * P:(c + 1) * P],
                                                   xn[:, i // LN_IT % 2, i % LN_IT, c * P:(c + 1) * P], ident[:])
                    last.then_inc(turned, 1)
                pe.wait_ge(xnT_done, (b + 1) * NT)

                def project(k, q, g):
                    kind, blk = divmod(k, QB)
                    if k == q == 0:
                        pe.wait_ge(w_loaded[0], (g + 1) * 32)
                    if k == 2 * QB and q == 0:
                        pe.wait_ge(w_loaded[1], (g + 1) * 16)
                    if q == 0:
                        pe.wait_ge(shared_free, g * NPROJ + k + 1)
                    dst = ps_x[:, k % 2, :]
                    if kind < 2:
                        last = nc.tensor.matmul(dst, wg[:, kind, q, :], xnT[:, q, blk * QW:(blk + 1) * QW],
                                                start=(q == 0), stop=(q == C - 1))
                    else:
                        at = blk * QW + q * P
                        for c in range(C):
                            last = nc.tensor.matmul(dst[:, q * P:(q + 1) * P], xnT[:, c, at:at + P],
                                                    wg[:, 2, c, :], start=(c == 0), stop=(c == C - 1))
                    if q == 3:
                        last.then_inc(shared_full, 1)

                def scores(g, u, p):
                    h, qb, kq = units[u]
                    if qb == kq == p == 0:
                        pe.wait_ge(head_loaded[h % 2], (g * HG // 2 + h // 2 + 1) * 112)
                    pe.wait_ge(tanh_done, (g * NU + u) * 2 + p + 1)
                    for i in range(2):
                        kb = kq * QUAD + 2 * p + i
                        last = nc.tensor.matmul(ps_s[:, p, i, off(u, p):],
                                                keys[0:KR + AL, h % 2, kb * P:(kb + 1) * P],
                                                queries[0:KR + AL, h % 2, qb * QW + off(u, p):(qb + 1) * QW],
                                                start=True, stop=True)
                    last.then_inc(scores_done, 1)

                def values(g, u, p):
                    h, qb, kq = units[u]
                    e = h * QB + qb
                    if p == 0:
                        if kq == 0:
                            pe.wait_ge(evac_done, g * NEV + e + 1)
                            if qb == 0:
                                pe.wait_ge(v_set, 2 + (g * HG + h + 1) * 2)
                    pe.wait_ge(split_done, 2 * (RP + g * NU + u) + p + 1)
                    for i in range(2):
                        n = 2 * p + i
                        first = n * P if u in diag else 0
                        if u in diag and p == 1:
                            last = nc.tensor.matmul(ps_v[0:VC, e % 2, first:],
                                                    v_ones[:, h % 2, kq * QUAD + n, :].bitcast(F32),
                                                    probs[:, u % RP, n, first:], start=False,
                                                    stop=(n == QUAD - 1))
                            continue
                        for part in range(2):
                            last = nc.tensor.matmul(ps_v[0:VC, e % 2, first:], v_ones[:, h % 2, kq * QUAD + n, :],
                                                    parts[:, u % RL, part, n, first:],
                                                    start=(kq == n == part == 0), stop=False)
                    last.then_inc(pv_done, 1)

                def group(hg, last):
                    g = b * GROUPS + hg
                    for u in range(2, NU + 2):
                        for p in range(2):
                            if u + 1 < NU:
                                scores(g, u + 1, p)
                            elif not last:
                                scores(g + 1, u + 1 - NU, p)
                            values(g, u - 2, p)
                        for slot in (2 * (u - 2), 2 * (u - 2) + 1):
                            if not last and slot in piece_at:
                                k, q = piece_at[slot]
                                project(k, q, g + 1)

                for k in range(NPROJ):
                    for q in range(4):
                        project(k, q, b * GROUPS)
                for u in range(AHEAD):
                    scores(b * GROUPS, u, 0)
                    scores(b * GROUPS, u, 1)
                with pe.Fori(0, GROUPS - 1) as hg:
                    group(hg, False)
                group(GROUPS - 1, True)

                for t in range(NT):
                    pe.wait_ge(ctx_done, QB + (b + 1) * GROUPS * QB)
                    pe.wait_ge(ctx_loaded, (b + 1) * (GROUPS - 1) * 16)
                    pe.wait_ge(wo_loaded, (b + 1) * 16)
                    if t >= 2:
                        pe.wait_ge(out_chain, b * NT + t - 1)
                    for c in range(C):
                        last = nc.tensor.matmul(ps_s[:, 0, t % 2, :], ctxT[:, c, t * P:(t + 1) * P], wo[:, c, :],
                                                start=(c == 0), stop=(c == C - 1))
                    last.then_inc(out_full, 1)

def moe(nc, tag, x, x_out, w, scratch, clear_scratch):
    xn_d, rows_in, rows_out = scratch
    NROWS = E_N * SLOTS
    J = 4
    STEPS = TILES // J
    ST = SLOTS // P
    NE = 2 * TILES
    tiles_of = lambda d: d.rearrange("(i j p) d -> i p j d", j=J, p=P)

    with ExitStack() as keep:
        k = Memory(nc, keep, tag)
        row_of = k.sb("row_of", [P, NE], U32)
        weight = k.sb("weight", [P, NE])

        with ExitStack() as ctx:
            m = Memory(nc, ctx, tag + "r")
            ident = m.sb("ident", [P, P])
            gate = m.sb("gate", [P, C, E_N])
            before = m.sb("before", [P, P], BF16)
            before_f = m.sb("before_f", [P, P])
            ones_b = m.sb("ones_b", [P, P], BF16)
            ones_f = m.sb("ones_f", [P, E_N * NE])
            expert_no = m.sb("expert_no", [P, E_N])
            spare_row = m.sb("spare_row", [P, 1])
            half = m.sb("half", [P, J])
            zero = m.sb("zero", [P, SLOTS * D // P])
            x_in = m.sb("x_in", [P, 2, J, D])
            xn = m.sb("xn", [P, 2, J, D])
            xnT = m.sb("xnT", [P, 2, J, D])
            stats = m.sb("stats", [P, J, 6])
            mv = m.sb("mv", [P, J, 2])
            veps = m.sb("veps", [P, J])
            rstd = m.sb("rstd", [P, J])
            logits = m.sb("logits", [P, J, E_N])
            best = m.sb("best", [P, J, 8])
            best_no = m.sb("best_no", [P, J, 8], U32)
            chosen_f = m.sb("chosen_f", [P, J, 2])
            chosen = m.sb("chosen", [P, NE])
            gap = m.sb("gap", [P, TILES])
            hot = m.sb("hot", [P, E_N, 2, TILES], BF16)
            e_gap = m.sb("e_gap", [P, TILES])
            den = m.sb("den", [P, TILES])
            share = m.sb("share", [P, 2, TILES])
            totals = m.sb("totals", [P, E_N * NE])
            running = m.sb("running", [P, E_N * NE])
            earlier = m.sb("earlier", [P, E_N * NE])
            place = m.sb("place", [P, E_N * NE])
            placed = m.sb("placed", [P, E_N * NE])
            pos = m.sb("pos", [P, NE])
            fits = m.sb("fits", [P, NE])
            row_f = m.sb("row_f", [P, NE])
            row_g = m.sb("row_g", [P, NE])
            ps_t = m.ps("turned", [P, J, D])
            ps_l = m.ps("logits", [P, 2, D])
            ps_c = m.ps("counts", [P, 2, D])

            consts_in = m.sem("consts_in")
            sets = m.sem("sets")
            cleared = m.sem("cleared")
            x_loaded = [m.sem(f"x_loaded{i}") for i in range(2)]
            xn_stored = [m.sem(f"xn_stored{i}") for i in range(2)]
            stats_done = m.sem("stats_done")
            mean_done = m.sem("mean_done")
            var_done = m.sem("var_done")
            rstd_done = m.sem("rstd_done")
            xn_done = m.sem("xn_done")
            turned = m.sem("turned")
            xnT_done = m.sem("xnT_done")
            logits_full = m.sem("logits_full")
            logits_done = m.sem("logits_done")
            best_done = m.sem("best_done")
            chain = m.sem("chain")
            gaps_done = m.sem("gaps_done")
            e_done = m.sem("e_done")
            prefix_full = m.sem("prefix_full")
            totals_full = m.sem("totals_full")
            chosen_done = m.sem("chosen_done")
            hot_done = m.sem("hot_done")
            place_done = m.sem("place_done")
            dve_passed, sp_passed = m.sem("dve_passed"), m.sem("sp_passed")

            block = ctx.enter_context(nc.Block())

            def one_ahead(eng, front, back):
                front(0, 0)
                with eng.Fori(0, STEPS // 2 - 1) as ii:
                    front(ii, 1)
                    back(ii, 0)
                    front(ii + 1, 0)
                    back(ii, 1)
                front(STEPS // 2 - 1, 1)
                back(STEPS // 2 - 1, 0)
                back(STEPS // 2 - 1, 1)

            @block.sync
            def _(sp):
                for dst, src in ((ident, w["ident"]), (gate, w["gateT"].rearrange("(c p) e -> p c e", p=P)),
                                 (before_f, w["before"]), (expert_no, w["expert_no"]), (spare_row, w["spare_row"])):
                    sp.dma_start(dst[:], src).then_inc(consts_in, 16)
                for s in range(2):
                    sp.sem_inc(xn_stored[s], 16)
                    sp.dma_start(x_in[:, s], tiles_of(x)[s]).then_inc(x_loaded[s], 16)
                if clear_scratch:
                    sp.wait_ge(sets, 4)
                    for e in range(E_N):
                        sp.dma_start(rows_in[e * SLOTS:(e + 1) * SLOTS, :].rearrange("(p r) d -> p (r d)", p=P),
                                     zero[:]).then_inc(cleared, 16)
                    for d in (rows_in, rows_out):
                        sp.dma_start(d[NROWS:NROWS + P, :], zero[:, 0:D]).then_inc(cleared, 16)
                with sp.Fori(0, STEPS // 2) as ii:
                    for s in range(2):
                        wait_alone(sp, xn_done, (2 * ii + s + 1) * J, sp_passed)
                        sp.dma_start(tiles_of(xn_d)[ds(2 * ii + s, 1)].rearrange("a p j d -> (a p) j d"), xn[:, s]
                                     ).then_inc(xn_stored[s], 16)
                        nxt = tiles_of(x)[ds((2 * ii + 2 + s) % STEPS, 1)]
                        sp.dma_start(x_in[:, s], nxt.rearrange("a p j d -> (a p) j d")).then_inc(x_loaded[s], 16)
                for s in range(2):
                    sp.wait_ge(xn_stored[s], 16 + STEPS // 2 * 16)
                    sp.wait_ge(x_loaded[s], (STEPS // 2 + 1) * 16)
                if clear_scratch:
                    sp.wait_ge(cleared, (E_N + 2) * 16)

            @block.gpsimd
            def _(pool):
                nc.gpsimd.memset(ones_b[:], 1.0).then_inc(sets, 1)
                nc.gpsimd.memset(ones_f[:], 1.0).then_inc(sets, 1)
                nc.gpsimd.memset(half[:], -0.5).then_inc(sets, 1)
                nc.gpsimd.memset(zero[:], 0.0).then_inc(sets, 1)
                pool.wait_ge(consts_in, 5 * 16)
                nc.gpsimd.tensor_copy(before[:], before_f[:]).then_inc(sets, 1)
                pool.wait_ge(sets, 5)
                with pool.Fori(0, STEPS) as i:
                    pool.wait_ge(var_done, i + 1)
                    nc.gpsimd.tensor_tensor(rstd[:], veps[:], half[:], ALU.pow).then_inc(rstd_done, 1)

            @block.scalar
            def _(act):
                act.sem_inc(xnT_done, 1)
                with act.Fori(0, STEPS // 2) as ii:
                    for s in range(2):
                        i = 2 * ii + s
                        for j in range(J):
                            act.wait_ge(turned, i * J + j + 1)
                            if j == 0:
                                act.wait_ge(logits_full, i + 1)
                            nc.scalar.copy(xnT[:, s, j, :], ps_t[:, j, :]).then_inc(xnT_done, 1)
                act.wait_ge(gaps_done, STEPS)
                nc.scalar.activation(e_gap[:], gap[:], ACT.Exp).then_inc(e_done, 1)

            @block.tensor
            def _(pe):
                pe.wait_ge(consts_in, 5 * 16)
                pe.wait_ge(sets, 5)
                pe.sem_inc(logits_full, 2)

                def turn(ii, s):
                    i = 2 * ii + s
                    pe.wait_ge(xn_done, (i + 1) * J)
                    pe.wait_ge(xnT_done, 1 + i * J)
                    for j in range(J):
                        for c in range(C):
                            last = nc.tensor.transpose(ps_t[:, j, c * P:(c + 1) * P],
                                                       xn[:, s, j, c * P:(c + 1) * P], ident[:])
                        last.then_inc(turned, 1)

                def gate_logits(ii, s):
                    i = 2 * ii + s
                    pe.wait_ge(logits_done, i + 1)
                    for j in range(J):
                        pe.wait_ge(xnT_done, 1 + i * J + j + 1)
                        for c in range(C):
                            last = nc.tensor.matmul(ps_l[:, s, j * E_N:(j + 1) * E_N],
                                                    xnT[:, s, j, c * P:(c + 1) * P], gate[:, c, :],
                                                    start=(c == 0), stop=(c == C - 1))
                    last.then_inc(logits_full, 1)

                one_ahead(pe, turn, gate_logits)
                pe.wait_ge(hot_done, STEPS * (2 * J + 1))
                flat = hot[:, :, :, :].rearrange("p e s t -> p (e s t)")
                n = E_N * NE // 2
                for i in range(2):
                    last = nc.tensor.matmul(ps_c[:, i, 0:n], before[:], flat[:, i * n:(i + 1) * n], start=True, stop=True)
                last.then_inc(prefix_full, 1)
                pe.wait_ge(logits_done, 2 + STEPS)
                for i in range(2):
                    last = nc.tensor.matmul(ps_l[:, i, 0:n], ones_b[:], flat[:, i * n:(i + 1) * n], start=True, stop=True)
                last.then_inc(totals_full, 1)

            @block.vector
            def _(dve):
                dve.wait_ge(consts_in, 5 * 16)
                dve.wait_ge(sets, 4)
                dve.sem_inc(logits_done, 2)

                def normalise(ii, s):
                    i = 2 * ii + s
                    dve.wait_ge(x_loaded[s], (ii + 1) * 16)
                    for j in range(J):
                        nc.vector.bn_stats(stats[:, j, :], x_in[:, s, j, :]).then_inc(stats_done, 1)
                    wait_alone(dve, stats_done, (i + 1) * J, dve_passed)
                    for j in range(J):
                        nc.vector.bn_aggr(mv[:, j, :], stats[:, j, :]).then_inc(mean_done, 1)
                    dve.wait_ge(mean_done, (i + 1) * J)
                    nc.vector.tensor_scalar(veps[:], mv[:, :, 1], EPS, None, ALU.add).then_inc(var_done, 1)
                    dve.wait_ge(xn_stored[s], 16 + ii * 16)
                    dve.wait_ge(logits_done, i + 1)
                    dve.wait_ge(rstd_done, i + 1)
                    for j in range(J):
                        nc.vector.tensor_scalar(xn[:, s, j, :], x_in[:, s, j, :], mv[:, j, 0:1],
                                                rstd[:, j:j + 1], ALU.subtract, ALU.mult).then_inc(xn_done, 1)

                def choose(ii, s):
                    i = 2 * ii + s
                    dve.wait_ge(logits_full, i + 3)
                    nc.vector.tensor_copy(logits[:].rearrange("p j e -> p (j e)"), ps_l[:, s, 0:J * E_N]
                                          ).then_inc(logits_done, 1)
                    wait_alone(dve, logits_done, i + 3, dve_passed)
                    for j in range(J):
                        nc.vector.max(best[:, j, :], logits[:, j, :]).then_inc(best_done, 1)
                    wait_alone(dve, best_done, (2 * i + 1) * J, dve_passed)
                    for j in range(J):
                        nc.vector.max_index(best_no[:, j, :], best[:, j, :], logits[:, j, :]).then_inc(best_done, 1)
                    nc.vector.tensor_tensor(gap[:, ds(i * J, J)], best[:, :, 1], best[:, :, 0], ALU.subtract
                                            ).then_inc(gaps_done, 1)
                    dve.wait_ge(best_done, (2 * i + 2) * J)
                    nc.vector.tensor_copy(chosen_f[:], best_no[:, :, 0:2]).then_inc(chosen_done, 1)
                    dve.wait_ge(chosen_done, i + 1)
                    nc.vector.tensor_copy(chosen[:, ds(2 * i * J, 2 * J)],
                                          chosen_f[:].rearrange("p j s -> p (j s)")).then_inc(hot_done, 1)
                    for j in range(J):
                        for c in range(2):
                            nc.vector.tensor_scalar(
                                hot[:, :, c, ds(i * J + j, 1)].rearrange("p e a -> p (e a)"), expert_no[:],
                                chosen_f[:, j, c:c + 1], None, ALU.is_equal).then_inc(hot_done, 1)

                one_ahead(dve, normalise, choose)
                dve.wait_ge(hot_done, STEPS * (2 * J + 1))
                n_chain = 0

                def link(ins):
                    nonlocal n_chain
                    ins.then_inc(chain, 1)
                    n_chain += 1
                    dve.wait_ge(chain, n_chain)

                dve.wait_ge(e_done, 1)
                link(nc.vector.tensor_scalar(den[:], e_gap[:], 1.0, None, ALU.add))
                link(nc.vector.reciprocal(share[:, 0, :], den[:]))
                link(nc.vector.tensor_tensor(share[:, 1, :], e_gap[:], share[:, 0, :], ALU.mult))
                dve.wait_ge(totals_full, 1)
                n = E_N * NE // 2
                for q in range(2):
                    link(nc.vector.tensor_copy(totals[:, q * n:(q + 1) * n], ps_l[:, q, 0:n]))
                link(nc.vector.tensor_tensor_scan(running[:], ones_f[:], totals[:], 0.0, ALU.mult, ALU.add))
                link(nc.vector.tensor_tensor(earlier[:], running[:], totals[:], ALU.subtract))
                dve.wait_ge(prefix_full, 1)
                for e in range(E_N):
                    q = e * NE // n
                    own = slice(e * NE, (e + 1) * NE)
                    nc.vector.scalar_tensor_tensor(place[:, own], earlier[:, own], earlier[:, e * NE:e * NE + 1],
                                                   ps_c[:, q, e * NE - q * n:(e + 1) * NE - q * n],
                                                   ALU.subtract, ALU.add).then_inc(place_done, 1)
                dve.wait_ge(place_done, E_N)
                link(nc.vector.tensor_tensor(placed[:], place[:], hot[:].rearrange("p e c t -> p (e c t)"), ALU.mult))
                link(nc.vector.tensor_reduce(pos[:], placed[:].rearrange("p (e n) -> p n e", e=E_N), AX.X, ALU.add))
                link(nc.vector.tensor_scalar(fits[:], pos[:], float(CAP), None, ALU.is_lt))
                turn = lambda a: a.rearrange("p (c t) -> p t c", c=2)
                pair = lambda a: a.rearrange("p (t c) -> p t c", c=2)
                link(nc.vector.scalar_tensor_tensor(pair(row_f[:]), pair(chosen[:]), float(SLOTS), turn(pos[:]),
                                                    ALU.mult, ALU.add))
                link(nc.vector.tensor_scalar(row_g[:], row_f[:], spare_row[:, 0:1], None, ALU.subtract))
                link(nc.vector.tensor_tensor(pair(row_f[:]), pair(row_g[:]), turn(fits[:]), ALU.mult))
                link(nc.vector.tensor_scalar(row_g[:], row_f[:], spare_row[:, 0:1], None, ALU.add))
                link(nc.vector.tensor_copy(row_of[:], row_g[:]))
                link(nc.vector.tensor_tensor(pair(weight[:]), share[:].rearrange("p c t -> p t c"), turn(fits[:]),
                                             ALU.mult))

        with ExitStack() as ctx:
            m = Memory(nc, ctx, tag + "s")
            xn4 = m.sb("xn4", [P, 2, J, D])
            row4 = m.sb("row4", [P, 2, 2 * J], U32)
            loaded = [m.sem(f"loaded{i}") for i in range(2)]
            scattered = m.sem("scattered")
            rows_set = m.sem("rows_set")
            sp_passed, pool_passed = m.sem("sp_passed"), m.sem("pool_passed")
            block = ctx.enter_context(nc.Block())

            @block.sync
            def _(sp):
                for s in range(2):
                    sp.dma_start(xn4[:, s], tiles_of(xn_d)[s]).then_inc(loaded[s], 16)
                with sp.Fori(1, STEPS // 2) as ii:
                    for s in range(2):
                        wait_alone(sp, scattered, (2 * ii + s - 1) * (2 * J * 16), sp_passed)
                        src = tiles_of(xn_d)[ds(2 * ii + s, 1)]
                        sp.dma_start(xn4[:, s], src.rearrange("a p j d -> (a p) j d")).then_inc(loaded[s], 16)

            @block.gpsimd
            def _(pool):
                def step(ii, first):
                    for s in range(2):
                        i = 2 * ii + s
                        nc.gpsimd.tensor_copy(row4[:, s, :], row_of[:, ds(2 * i * J, 2 * J)]).then_inc(rows_set, 1)
                        wait_alone(pool, loaded[s], (ii + 1) * 16, pool_passed)
                        wait_alone(pool, rows_set, i + 1, pool_passed)
                        for j in range(J):
                            for c in range(2):
                                if not (first and s == j == c == 0):
                                    wait_alone(pool, scattered, (i * 2 * J + 2 * j + c) * 16, pool_passed)
                                nc.gpsimd.indirect_dma_start(
                                    rows_in, bass.IndirectOffsetOnAxis(row4[:, s, 2 * j + c:2 * j + c + 1], 0),
                                    xn4[:, s, j, :], None).then_inc(scattered, 16)

                step(0, True)
                with pool.Fori(1, STEPS // 2) as ii:
                    step(ii, False)
                pool.wait_ge(scattered, STEPS * 2 * J * 16)

        with ExitStack() as ctx:
            m = Memory(nc, ctx, tag + "e")
            ident = m.sb("ident", [P, P])
            w13 = m.sb("w13", [P, E_N, C, 2 * F])
            w2 = m.sb("w2", [F, E_N, D])
            rows = m.sb("rows", [P, 2, ST, D])
            rowsT = m.sb("rowsT", [P, 2, D])
            up = m.sb("up", [P, 2, F])
            z = m.sb("z", [P, 2, F])
            th = m.sb("th", [P, 2, F])
            hid = m.sb("hid", [P, 2, F])
            hidT = m.sb("hidT", [F, 2, P])
            res = m.sb("res", [P, 2, ST, D])
            ps_t = m.ps("turned", [P, 2, D])
            ps_h = m.ps("hidden", [P, 2, D])
            ps_ht = m.ps("hidden_turned", [P, 2, D])
            ps_y = m.ps("result", [P, 2, D])
            consts_in = m.sem("consts_in")
            loaded = [m.sem(f"loaded{i}") for i in range(2)]
            stored = [m.sem(f"stored{i}") for i in range(2)]
            turned = m.sem("turned")
            rowsT_done = m.sem("rowsT_done")
            hidden_full = m.sem("hidden_full")
            up_done = m.sem("up_done")
            z_done = m.sem("z_done")
            th_done = m.sem("th_done")
            hid_done = m.sem("hid_done")
            hid_turned = m.sem("hid_turned")
            hidT_done = m.sem("hidT_done")
            result_full = m.sem("result_full")
            res_done = m.sem("res_done")
            sp_passed, pe_passed = m.sem("sp_passed"), m.sem("pe_passed")
            block = ctx.enter_context(nc.Block())
            rows_of = lambda d: d[0:NROWS, :].rearrange("(e j p) d -> e p j d", j=ST, p=P)

            @block.sync
            def _(sp):
                for s in range(2):
                    sp.sem_inc(stored[s], 16)
                    sp.dma_start(rows[:, s], rows_of(rows_in)[s]).then_inc(loaded[s], 16)
                sp.dma_start(ident[:], w["ident"]).then_inc(consts_in, 16)
                sp.dma_start(w13[:], w["w13T"].rearrange("e (c p) f -> p e c f", p=P)).then_inc(consts_in, 16)
                sp.dma_start(w2[:], w["w2T"].rearrange("e f d -> f e d")).then_inc(consts_in, 16)
                with sp.Fori(0, E_N // 2) as ee:
                    for s in range(2):
                        e = 2 * ee + s
                        wait_alone(sp, turned, (e + 1) * ST, sp_passed)
                        nxt = rows_of(rows_in)[ds((e + 2) % E_N, 1)]
                        sp.dma_start(rows[:, s], nxt.rearrange("a p j d -> (a p) j d")).then_inc(loaded[s], 16)
                        wait_alone(sp, res_done, 2 + (e + 1) * ST, sp_passed)
                        dst = rows_of(rows_out)[ds(e, 1)]
                        sp.dma_start(dst.rearrange("a p j d -> (a p) j d"), res[:, s]).then_inc(stored[s], 16)
                for s in range(2):
                    sp.wait_ge(stored[s], 16 + E_N // 2 * 16)
                    sp.wait_ge(loaded[s], (E_N // 2 + 1) * 16)

            @block.scalar
            def _(act):
                act.sem_inc(rowsT_done, 2)
                with act.Fori(0, E_N // 2) as ee:
                    for s in range(2):
                        n0 = (2 * ee + s) * ST
                        for q in range(ST + 1):
                            if q < ST:
                                n = n0 + q
                                act.wait_ge(turned, n + 1)
                                act.wait_ge(hidden_full, n + 1)
                                nc.scalar.copy(rowsT[:, q % 2, :], ps_t[:, q % 2, :]).then_inc(rowsT_done, 1)
                            if q >= 1:
                                n, r = n0 + q - 1, (q - 1) % 2
                                act.wait_ge(hidden_full, n + 3)
                                nc.scalar.copy(up[:, r, :], ps_h[:, r, F:2 * F]).then_inc(up_done, 1)
                                act.wait_ge(z_done, n + 3)
                                nc.scalar.activation(th[:, r, :], z[:, r, :], ACT.Tanh).then_inc(th_done, 1)

            @block.vector
            def _(dve):
                dve.sem_inc(z_done, 2)
                dve.sem_inc(hidT_done, 2)
                dve.sem_inc(res_done, 2)
                with dve.Fori(0, E_N // 2) as ee:
                    for s in range(2):
                        n0 = (2 * ee + s) * ST
                        for q in range(ST + 2):
                            if q < ST:
                                n, r = n0 + q, q % 2
                                dve.wait_ge(up_done, n + 1)
                                nc.vector.scalar_tensor_tensor(z[:, r, :], ps_h[:, r, 0:F], 0.5, up[:, r, :],
                                                               ALU.mult, ALU.mult).then_inc(z_done, 1)
                                dve.wait_ge(th_done, n + 1)
                                dve.wait_ge(z_done, n + 3)
                                dve.wait_ge(hid_turned, n + 1)
                                nc.vector.scalar_tensor_tensor(hid[:, r, :], th[:, r, :], 1.0, z[:, r, :],
                                                               ALU.add, ALU.mult).then_inc(hid_done, 1)
                            if 0 <= q - 1 < ST:
                                n, r = n0 + q - 1, (q - 1) % 2
                                dve.wait_ge(hid_turned, n + 3)
                                dve.wait_ge(result_full, n + 1)
                                nc.vector.tensor_copy(hidT[:, r, :], ps_ht[0:F, r, 0:P]).then_inc(hidT_done, 1)
                            if q - 2 >= 0:
                                n, r = n0 + q - 2, (q - 2) % 2
                                dve.wait_ge(result_full, n + 3)
                                if q == 2:
                                    dve.wait_ge(stored[s], 16 + ee * 16)
                                nc.vector.tensor_copy(res[:, s, q - 2, :], ps_y[:, r, :]).then_inc(res_done, 1)

            @block.tensor
            def _(pe):
                pe.wait_ge(consts_in, 3 * 16)
                pe.sem_inc(hidden_full, 2)
                pe.sem_inc(hid_turned, 2)
                pe.sem_inc(result_full, 2)
                with pe.Fori(0, E_N // 2) as ee:
                    for s in range(2):
                        e = 2 * ee + s
                        n0 = e * ST
                        pe.wait_ge(loaded[s], (ee + 1) * 16)
                        for q in range(ST + 3):
                            if q < ST:
                                n, r = n0 + q, q % 2
                                pe.wait_ge(rowsT_done, n + 1)
                                for c in range(C):
                                    last = nc.tensor.transpose(ps_t[:, r, c * P:(c + 1) * P],
                                                               rows[:, s, q, c * P:(c + 1) * P], ident[:])
                                last.then_inc(turned, 1)
                            if 0 <= q - 1 < ST:
                                n, r = n0 + q - 1, (q - 1) % 2
                                pe.wait_ge(rowsT_done, n + 3)
                                pe.wait_ge(z_done, n + 1)
                                for c in range(C):
                                    last = nc.tensor.matmul(
                                        ps_h[:, r, 0:2 * F], rowsT[:, r, c * P:(c + 1) * P],
                                        w13[:, ds(e, 1), c, :].rearrange("p a f -> p (a f)"),
                                        start=(c == 0), stop=(c == C - 1))
                                last.then_inc(hidden_full, 1)
                            if 0 <= q - 2 < ST:
                                n, r = n0 + q - 2, (q - 2) % 2
                                pe.wait_ge(hid_done, n + 1)
                                wait_alone(pe, hidT_done, n + 1, pe_passed)
                                nc.tensor.transpose(ps_ht[0:F, r, 0:P], hid[:, r, :], ident[:]).then_inc(hid_turned, 1)
                            if 0 <= q - 3 < ST:
                                n, r = n0 + q - 3, (q - 3) % 2
                                pe.wait_ge(hidT_done, n + 3)
                                wait_alone(pe, res_done, n + 1, pe_passed)
                                nc.tensor.matmul(ps_y[:, r, :], hidT[:, r, :],
                                                 w2[:, ds(e, 1), :].rearrange("f a d -> f (a d)"),
                                                 start=True, stop=True).then_inc(result_full, 1)

        with ExitStack() as ctx:
            m = Memory(nc, ctx, tag + "c")
            x4 = m.sb("x4", [P, 2, J, D])
            got = m.sb("got", [P, 2, 2 * J, D])
            row4 = m.sb("row4", [P, 2, 2 * J], U32)
            w4 = m.sb("w4", [P, 2, 2 * J])
            part = m.sb("part", [P, 2, J, D])
            total = m.sb("total", [P, 2, J, D])
            loaded = [m.sem(f"loaded{i}") for i in range(2)]
            gathered = [m.sem(f"gathered{i}") for i in range(2)]
            stored = [m.sem(f"stored{i}") for i in range(2)]
            rows_set = m.sem("rows_set")
            w4_set = m.sem("w4_set")
            part_done = m.sem("part_done")
            total_done = m.sem("total_done")
            sp_passed, pool_passed = m.sem("sp_passed"), m.sem("pool_passed")
            block = ctx.enter_context(nc.Block())

            @block.sync
            def _(sp):
                for s in range(2):
                    sp.sem_inc(stored[s], 16)
                    sp.dma_start(x4[:, s], tiles_of(x)[s]).then_inc(loaded[s], 16)
                with sp.Fori(0, STEPS // 2) as ii:
                    for s in range(2):
                        i = 2 * ii + s
                        wait_alone(sp, total_done, 2 * J + (i + 1) * J, sp_passed)
                        sp.dma_start(tiles_of(x_out)[ds(i, 1)].rearrange("a p j d -> (a p) j d"), total[:, s]
                                     ).then_inc(stored[s], 16)
                        nxt = tiles_of(x)[ds((i + 2) % STEPS, 1)]
                        sp.dma_start(x4[:, s], nxt.rearrange("a p j d -> (a p) j d")).then_inc(loaded[s], 16)
                for s in range(2):
                    sp.wait_ge(stored[s], 16 + STEPS // 2 * 16)
                    sp.wait_ge(loaded[s], (STEPS // 2 + 1) * 16)

            @block.gpsimd
            def _(pool):
                with pool.Fori(0, STEPS // 2) as ii:
                    for s in range(2):
                        i = 2 * ii + s
                        wait_alone(pool, total_done, (i + 1) * J, pool_passed)
                        nc.gpsimd.tensor_copy(row4[:, s, :], row_of[:, ds(2 * i * J, 2 * J)]).then_inc(rows_set, 1)
                        wait_alone(pool, rows_set, i + 1, pool_passed)
                        for n in range(2 * J):
                            nc.gpsimd.indirect_dma_start(
                                got[:, s, n, :], None, rows_out,
                                bass.IndirectOffsetOnAxis(row4[:, s, n:n + 1], 0)).then_inc(gathered[s], 16)

            @block.vector
            def _(dve):
                dve.sem_inc(total_done, 2 * J)
                with dve.Fori(0, STEPS // 2) as ii:
                    for s in range(2):
                        i = 2 * ii + s
                        nc.vector.tensor_copy(w4[:, s, :], weight[:, ds(2 * i * J, 2 * J)]).then_inc(w4_set, 1)
                        dve.wait_ge(w4_set, i + 1)
                        dve.wait_ge(loaded[s], (ii + 1) * 16)
                        dve.wait_ge(gathered[s], (ii + 1) * (2 * J * 16))
                        for j in range(J):
                            nc.vector.scalar_tensor_tensor(part[:, s, j, :], got[:, s, 2 * j, :],
                                                           w4[:, s, 2 * j:2 * j + 1], x4[:, s, j, :],
                                                           ALU.mult, ALU.add).then_inc(part_done, 1)
                        dve.wait_ge(stored[s], 16 + ii * 16)
                        dve.wait_ge(part_done, (i + 1) * J)
                        for j in range(J):
                            nc.vector.scalar_tensor_tensor(total[:, s, j, :], got[:, s, 2 * j + 1, :],
                                                           w4[:, s, 2 * j + 1:2 * j + 2], part[:, s, j, :],
                                                           ALU.mult, ALU.add).then_inc(total_done, 1)

def attention_b(nc, x, x_out, w):
    NT = S // P
    SCALE = float(HD) ** -0.5
    tile_rows = x.rearrange("(l t p) d -> t p l d", l=2, p=P)
    out_rows = x_out.rearrange("(l t p) d -> t p l d", l=2, p=P)
    PROJ = [(1, 0), (0, 1), (1, 1), (0, 2), (1, 2)]
    NP = len(PROJ)
    K = 13

    with ExitStack() as ctx:
        m = Memory(nc, ctx, "ab")
        ident = m.sb("ident", [P, P])
        wqkv = m.sb("wqkv", [P, C, 3 * D])
        wo = m.sb("wo", [P, C, D])
        half = m.sb("half", [P, 2])
        x2 = m.sb("x2", [P, 2, 2, D])
        xn = m.sb("xn", [P, 2, D])
        xnT = m.sb("xnT", [P, 2, 2, D])
        stats = m.sb("stats", [P, 2, 6])
        mv = m.sb("mv", [P, 2, 2])
        veps = m.sb("veps", [P, 2])
        rstd = m.sb("rstd", [P, 2])
        q1 = m.sb("q1", [P, D])
        v01 = m.sb("v01", [P, 2, D])
        prod = m.sb("prod", [P, 2, D])
        score = m.sb("score", [P, 2, H])
        top = m.sb("top", [P, H])
        prob = m.sb("prob", [P, 2, H])
        den = m.sb("den", [P, H])
        ctx1 = m.sb("ctx1", [P, D])
        ctxT = m.sb("ctxT", [P, 2, D])
        total = m.sb("total", [P, 2, 2, D])
        ps_t = m.ps("turned", [P, D])
        ps_p = m.ps("projected", [P, NP, D])
        ps_o = m.ps("out", [P, 2, D])

        consts_in = m.sem("consts_in")
        half_set = m.sem("half_set")
        loaded = [m.sem(f"loaded{i}") for i in range(2)]
        stored = [m.sem(f"stored{i}") for i in range(2)]
        stats_done = m.sem("stats_done")
        mean_done = m.sem("mean_done")
        var_done = m.sem("var_done")
        rstd_done = m.sem("rstd_done")
        xn_done = m.sem("xn_done")
        turned_x = m.sem("turned_x")
        turned_c = m.sem("turned_c")
        xnT_done = m.sem("xnT_done")
        ctxT_done = m.sem("ctxT_done")
        projected = m.sem("projected")
        q1_done = m.sem("q1_done")
        v_done = m.sem("v_done")
        chain = m.sem("chain")
        exp_done = m.sem("exp_done")
        ctx_done = m.sem("ctx_done")
        out_full = m.sem("out_full")
        total_done = m.sem("total_done")
        sp_passed, dve_passed = m.sem("sp_passed"), m.sem("dve_passed")
        block = ctx.enter_context(nc.Block())

        @block.sync
        def _(sp):
            for s in range(2):
                sp.sem_inc(stored[s], 16)
                sp.dma_start(x2[:, s], tile_rows[s]).then_inc(loaded[s], 16)
            sp.dma_start(ident[:], w["ident"]).then_inc(consts_in, 16)
            sp.dma_start(wqkv[:], w["bqkvT"].rearrange("(c p) n -> p c n", p=P)).then_inc(consts_in, 16)
            sp.dma_start(wo[:], w["boT"].rearrange("(c p) n -> p c n", p=P)).then_inc(consts_in, 16)
            with sp.Fori(0, NT // 2) as ii:
                for s in range(2):
                    i = 2 * ii + s
                    wait_alone(sp, total_done, 2 + 2 * i + 2, sp_passed)
                    sp.dma_start(out_rows[ds(i, 1)].rearrange("a p l d -> (a p) l d"), total[:, s]
                                 ).then_inc(stored[s], 16)
                    nxt = tile_rows[ds((i + 2) % NT, 1)]
                    sp.dma_start(x2[:, s], nxt.rearrange("a p l d -> (a p) l d")).then_inc(loaded[s], 16)
            for s in range(2):
                sp.wait_ge(stored[s], 16 + NT // 2 * 16)
                sp.wait_ge(loaded[s], (NT // 2 + 1) * 16)

        @block.gpsimd
        def _(pool):
            nc.gpsimd.memset(half[:], -0.5).then_inc(half_set, 1)
            pool.wait_ge(half_set, 1)
            with pool.Fori(0, NT) as i:
                pool.wait_ge(var_done, i + 1)
                nc.gpsimd.tensor_tensor(rstd[:], veps[:], half[:], ALU.pow).then_inc(rstd_done, 1)

        def pipeline(eng, front, back):
            front(0, 0)
            with eng.Fori(0, NT // 2 - 1) as ii:
                front(ii, 1)
                back(ii, 0)
                front(ii + 1, 0)
                back(ii, 1)
            front(NT // 2 - 1, 1)
            back(NT // 2 - 1, 0)
            back(NT // 2 - 1, 1, True)

        @block.scalar
        def _(act):
            for sem, n in ((xnT_done, 2), (ctxT_done, 2), (q1_done, 1), (v_done, 2)):
                act.sem_inc(sem, n)

            def front(ii, s):
                i = 2 * ii + s
                act.wait_ge(projected, (i + 1) * NP)
                for l in range(2):
                    act.wait_ge(turned_x, 1 + 2 * i + l + 1)
                    nc.scalar.copy(xnT[:, s, l, :], ps_t[:]).then_inc(xnT_done, 1)

            def back(ii, s, last_tile=False):
                i = 2 * ii + s
                act.wait_ge(projected, (2 + i) * NP + 1)
                act.wait_ge(chain, i * K + 2)
                nc.scalar.mul(q1[:], ps_p[:, 0, :], SCALE).then_inc(q1_done, 1)
                act.wait_ge(chain, i * K + 12)
                act.wait_ge(turned_c, 1 + 2 * i)
                for l in range(2):
                    act.wait_ge(projected, (2 + i) * NP + 4 + l)
                    nc.scalar.copy(v01[:, l, :], ps_p[:, 3 + l, :]).then_inc(v_done, 1)
                act.wait_ge(chain, (1 + i) * K + 6)
                nc.scalar.activation(prob[:], score[:], ACT.Exp).then_inc(exp_done, 1)
                for l in range(2):
                    act.wait_ge(turned_c, 1 + 2 * i + l + 1)
                    act.wait_ge(out_full, 2 * i + l + 1)
                    nc.scalar.copy(ctxT[:, l, :], ps_t[:]).then_inc(ctxT_done, 1)

            pipeline(act, front, back)

        @block.vector
        def _(dve):
            dve.sem_inc(chain, K)
            dve.sem_inc(total_done, 2)

            def front(ii, s):
                i = 2 * ii + s
                dve.wait_ge(loaded[s], (ii + 1) * 16)
                for l in range(2):
                    nc.vector.bn_stats(stats[:, l, :], x2[:, s, l, :]).then_inc(stats_done, 1)
                wait_alone(dve, stats_done, (i + 1) * 2, dve_passed)
                for l in range(2):
                    nc.vector.bn_aggr(mv[:, l, :], stats[:, l, :]).then_inc(mean_done, 1)
                dve.wait_ge(mean_done, (i + 1) * 2)
                nc.vector.tensor_scalar(veps[:], mv[:, :, 1], EPS, None, ALU.add).then_inc(var_done, 1)
                dve.wait_ge(rstd_done, i + 1)
                dve.wait_ge(turned_x, 1 + 2 * i)
                for l in range(2):
                    nc.vector.tensor_scalar(xn[:, l, :], x2[:, s, l, :], mv[:, l, 0:1], rstd[:, l:l + 1],
                                            ALU.subtract, ALU.mult).then_inc(xn_done, 1)

            def back(ii, s, last_tile=False):
                i = 2 * ii + s
                n = 0

                def link(ins):
                    nonlocal n
                    ins.then_inc(chain, 1)
                    n += 1
                    dve.wait_ge(chain, (1 + i) * K + n)

                heads = lambda a: a.rearrange("p (h d) -> p h d", d=HD)
                wide = lambda a: a.unsqueeze(2).to_broadcast([P, H, HD])
                dve.wait_ge(q1_done, 1 + i + 1)
                for l in range(2):
                    dve.wait_ge(projected, (2 + i) * NP + 2 + l)
                    link(nc.vector.tensor_tensor(prod[:, l, :], ps_p[:, 1 + l, :], q1[:], ALU.mult))
                link(nc.vector.tensor_reduce(score[:].rearrange("p l h -> p (l h)"),
                                             prod[:].rearrange("p l (h d) -> p (l h) d", d=HD), AX.X, ALU.add))
                link(nc.vector.tensor_tensor(top[:], score[:, 0, :], score[:, 1, :], ALU.max))
                for l in range(2):
                    link(nc.vector.tensor_tensor(score[:, l, :], score[:, l, :], top[:], ALU.subtract))
                dve.wait_ge(exp_done, i + 1)
                link(nc.vector.tensor_tensor(den[:], prob[:, 0, :], prob[:, 1, :], ALU.add))
                link(nc.vector.reciprocal(top[:], den[:]))
                for l in range(2):
                    link(nc.vector.tensor_tensor(score[:, l, :], prob[:, l, :], top[:], ALU.mult))
                for l in range(2):
                    dve.wait_ge(v_done, 2 + 2 * i + l + 1)
                    link(nc.vector.tensor_tensor(heads(prod[:, l, :]), heads(v01[:, l, :]), wide(score[:, l, :]),
                                                 ALU.mult))
                dve.wait_ge(turned_c, 1 + 2 * i)
                link(nc.vector.tensor_tensor(ctx1[:], prod[:, 0, :], prod[:, 1, :], ALU.add))
                assert n == K
                dve.wait_ge(stored[s], 16 + ii * 16)
                for l in range(2):
                    dve.wait_ge(out_full, 2 + 2 * i + l + 1)
                    nc.vector.tensor_tensor(total[:, s, l, :], ps_o[:, l, :], x2[:, s, l, :], ALU.add
                                            ).then_inc(total_done, 1)

            pipeline(dve, front, back)

        @block.tensor
        def _(pe):
            pe.wait_ge(consts_in, 3 * 16)
            for sem, n in ((turned_x, 1), (turned_c, 1), (projected, 2 * NP), (out_full, 2)):
                pe.sem_inc(sem, n)

            def front(ii, s):
                i = 2 * ii + s
                pe.wait_ge(ctxT_done, 2 * max(i, 1) if isinstance(i, int) else 2 * i)
                for l in range(2):
                    pe.wait_ge(xnT_done, 2 + 2 * i + l)
                    pe.wait_ge(xn_done, 2 * i + l + 1)
                    for c in range(C):
                        last = nc.tensor.transpose(ps_t[:, c * P:(c + 1) * P], xn[:, l, c * P:(c + 1) * P], ident[:])
                    last.then_inc(turned_x, 1)
                pe.wait_ge(xnT_done, 2 + 2 * i + 2)
                for n, (l, kind) in enumerate(PROJ):
                    sem, value = ((q1_done, 1 + i), (chain, i * K + 1), (chain, i * K + 2),
                                  (v_done, 2 * i + 1), (v_done, 2 * i + 2))[n]
                    pe.wait_ge(sem, value)
                    for c in range(C):
                        last = nc.tensor.matmul(ps_p[:, n, :], xnT[:, s, l, c * P:(c + 1) * P],
                                                wqkv[:, c, kind * D:(kind + 1) * D],
                                                start=(c == 0), stop=(c == C - 1))
                    last.then_inc(projected, 1)

            def back(ii, s, last_tile=False):
                i = 2 * ii + s
                pe.wait_ge(xnT_done, 2 + 2 * i + (2 if last_tile else 4))
                for l in range(2):
                    if l == 0:
                        pe.wait_ge(v_done, 2 + 2 * i + 1)
                    else:
                        pe.wait_ge(chain, (1 + i) * K + K)
                    pe.wait_ge(ctxT_done, 2 + 2 * i + l)
                    for c in range(C):
                        src = v01[:, 0, c * P:(c + 1) * P] if l == 0 else ctx1[:, c * P:(c + 1) * P]
                        last = nc.tensor.transpose(ps_t[:, c * P:(c + 1) * P], src, ident[:])
                    last.then_inc(turned_c, 1)
                for l in range(2):
                    pe.wait_ge(ctxT_done, 2 + 2 * i + l + 1)
                    pe.wait_ge(total_done, 2 * i + l + 1)
                    for c in range(C):
                        last = nc.tensor.matmul(ps_o[:, l, :], ctxT[:, l, c * P:(c + 1) * P], wo[:, c, :],
                                                start=(c == 0), stop=(c == C - 1))
                    last.then_inc(out_full, 1)

            pipeline(pe, front, back)


def constants():
    at, ranges = np.arange(S), S // 256
    starts = 256 * (np.arange(P) % ranges)
    inside = (at // 256 == np.arange(ranges)[:, None]).astype(np.float32)
    from_start = np.broadcast_to(-(at % 256), (2, S)).astype(np.float32)
    slots = E_N * SLOTS
    return {
        "before": np.triu(np.ones((P, P), np.float32), 1),
        "expert_no": np.tile(np.arange(E_N, dtype=np.float32), (P, 1)),
        "spare_row": (slots + np.arange(P, dtype=np.float32))[:, None],
        "ident": np.eye(P, dtype=np.float32),
        "until": np.triu(np.ones((P, P), np.float32)),
        "key_ranges": (at[None, :] - starts[:, None]).astype(np.float32),
        "query_ranges": np.concatenate([inside, inside, from_start]),
    }


def lay_out(v):
    a = "L0_attn_a_"
    turned = lambda w: np.ascontiguousarray(np.swapaxes(w, -1, -2))
    rows = lambda r: np.ascontiguousarray(np.broadcast_to(r, (P, r.shape[0])))
    return {
        "x": np.ascontiguousarray(v[a + "hidden_states"].reshape(T, D)),
        "wqkvT": np.stack([turned(v[a + n]) for n in ("Wq", "Wk", "Wv")]),
        "woT": turned(v[a + "Wo"]),
        "qk_bias": np.ascontiguousarray(
            np.stack([v[a + n].reshape(GROUPS, P).T for n in ("bq", "bk")], axis=1)),
        "bv": rows(v[a + "bv"]),
        "bo": rows(v[a + "bo"]),
        "gateT": turned(v["L0_ffn_gate_w"]),
        "w13T": np.concatenate([turned(v["L0_ffn_w1"]), turned(v["L0_ffn_w3"])], axis=2),
        "w2T": turned(v["L0_ffn_w2"]),
        "bqkvT": turned(v["L0_attn_b_weight_qkv"]),
        "boT": turned(v["L0_attn_b_weight_out"]),
        "slopes": np.repeat(v[a + "alibi_slopes"].reshape(-1), S // 256)[:, None],
    }


def build(nc, ins, out):
    dram = lambda name, rows: nc.dram_tensor(name, (rows, D), F32, kind="Internal").ap()
    x1, x2, x3, xn = (dram(n, T) for n in ("x1", "x2", "x3", "xn"))
    rows_in, rows_out = (dram(n, E_N * SLOTS + P) for n in ("rows_in", "rows_out"))
    scratch = (xn, rows_in, rows_out)
    attention_a(nc, ins["x"], x1, ins)
    moe(nc, "f1", x1, x2, ins, scratch, True)
    attention_b(nc, x2, x3, ins)
    moe(nc, "f2", x3, out, ins, scratch, False)


def kernel(**inputs):
    import concourse.bacc as bacc
    from concourse.bass_utils import run_bass_kernel_spmd

    v = {k: np.asarray(a) for k, a in inputs.items()}
    arrays = dict(constants())
    arrays.update(lay_out(v))
    nc = bacc.Bacc("TRN2", target_bir_lowering=False, num_devices=1)
    ins = {}
    for name, a in arrays.items():
        ins[name] = nc.dram_tensor(f"in_{name}", a.shape, mybir.dt.from_np(a.dtype), kind="ExternalInput").ap()
    out = nc.dram_tensor("out_dram", (T, D), F32, kind="ExternalOutput").ap()
    build(nc, ins, out)
    r = run_bass_kernel_spmd(nc, [{f"in_{k}": a for k, a in arrays.items()}], core_ids=[0])
    return r.results[0]["out_dram"].reshape(B, S, D)
```
